# Optimizing a Trainium2 kernel written in Bass

```python
import numpy as np
import jax
import jax.numpy as jnp

def _softmax(x, axis=-1):
    return jax.nn.softmax(x, axis=axis)

def _gelu(x):
    return jax.nn.gelu(x, approximate=True)

def _silu(x):
    return jax.nn.silu(x)

def _sigmoid(x):
    return jax.nn.sigmoid(x)

def _layernorm(x, axis=-1, eps=1e-05):
    m = jnp.mean(x, axis=axis, keepdims=True)
    v = jnp.var(x, axis=axis, keepdims=True)
    return (x - m) / jnp.sqrt(v + eps)

def _scatter_add(tgt, idx, src, axis=0):
    return tgt.at[idx].add(src)

def _segment_sum(src, seg, n):
    return jax.ops.segment_sum(src, seg, n)
kernel_name = 'mk_xattn_ffn_d4_seqx_r8_4d8c52'

def setup_inputs(seed: int=0):
    np.random.seed(seed)
    _w = jnp.asarray

    def _rec_inputs():
        import jax
        import jax.numpy as jnp
        _rk = jax.random.key(seed)
        x = 0.0002417 + 0.9998 * jax.random.normal(jax.random.fold_in(_rk, 1), (2, 256, 128), jnp.float32)
        _lenS = 256 - jax.random.randint(jax.random.fold_in(_rk, 7), (2,), 0, max(1, 256 // 4) + 1, jnp.int32)
        _lenS2 = 512 - jax.random.randint(jax.random.fold_in(_rk, 8), (2,), 0, max(1, 512 // 4) + 1, jnp.int32)
        _ctx_1024P = jax.random.normal(jax.random.fold_in(_rk, 11), (2, 16, 128), jnp.float32)
        _ctx_1024c = jax.random.dirichlet(jax.random.fold_in(_rk, 511), 0.3 * jnp.ones((16,), jnp.float32), (2, 512))
        _ctx_1024t = jnp.einsum('bsk,bkd->bsd', _ctx_1024c, _ctx_1024P)
        _ctx_1024t = _ctx_1024t * jax.lax.rsqrt(jnp.mean(jnp.square(_ctx_1024t)) + 1e-12) * 0.953939
        ctx_1024 = 7.22013e-05 + 1.00017 * (_ctx_1024t + 0.3 * jax.random.normal(jax.random.fold_in(_rk, 611), (2, 512, 128), jnp.float32))
        fside_BxS2_0 = jax.random.uniform(jax.random.fold_in(_rk, 12), (2, 512), jnp.float32, 0.0, 0.999707)
        return (x, ctx_1024, fside_BxS2_0)
    x, ctx_1024, fside_BxS2_0 = _rec_inputs()

    def _L0_xattn_setup():
        import jax, jax.numpy as jnp
        import numpy as np
        EMBED_SIZE = 128
        HEADS = 16
        HEAD_DIM = EMBED_SIZE // HEADS
        key = jax.random.key(seed)
        k1, k2, k3, k4 = jax.random.split(key, 4)
        N, L = (4, 256)
        return {'values': jax.random.normal(k1, (N, L, EMBED_SIZE), dtype=jnp.float32), 'keys': jax.random.normal(k2, (N, L, EMBED_SIZE), dtype=jnp.float32), 'query': jax.random.normal(k3, (N, L, EMBED_SIZE), dtype=jnp.float32), 'w_out': jax.random.normal(k4, (EMBED_SIZE, EMBED_SIZE), dtype=jnp.float32) * (1.0 / np.sqrt(EMBED_SIZE)), 'b_out': jnp.zeros((EMBED_SIZE,), dtype=jnp.float32)}
    _L0_xattn_all = _L0_xattn_setup()
    _L0_xattn_in = {k: v for k, v in _L0_xattn_all.items() if k in ('w_out', 'b_out')}
    del _L0_xattn_all

    def _L0_ffn_setup():
        import jax, jax.numpy as jnp
        import numpy as np
        TOP_K = 2
        LN_EPS = 1e-05
        B, S, H, E, F = (2, 256, 128, 8, 512)

        def _layernorm(x, w, b):
            mu = jnp.mean(x, axis=-1, keepdims=True)
            var = jnp.mean(jnp.square(x - mu), axis=-1, keepdims=True)
            return (x - mu) * jax.lax.rsqrt(var + LN_EPS) * w + b
        key = jax.random.key(seed)
        ks = jax.random.split(key, 6)
        x = jax.random.normal(ks[0], (B, S, H), dtype=jnp.float32)
        Wg = jax.random.normal(ks[1], (H, E), dtype=jnp.float32) * 0.02
        alpha = jax.random.normal(ks[2], (E,), dtype=jnp.float32)
        ln_w = jnp.ones((E, H), dtype=jnp.float32)
        ln_b = jnp.zeros((E, H), dtype=jnp.float32)
        fc1_w = jax.random.normal(ks[3], (E, H, F), dtype=jnp.float32) * 0.02
        fc1_b = jnp.zeros((E, F), dtype=jnp.float32)
        fc2_w = jax.random.normal(ks[4], (E, F, H), dtype=jnp.float32) * 0.02
        fc2_b = jnp.zeros((E, H), dtype=jnp.float32)
        return {'x': x, 'Wg': Wg, 'alpha': alpha, 'ln_w': ln_w, 'ln_b': ln_b, 'fc1_w': fc1_w, 'fc1_b': fc1_b, 'fc2_w': fc2_w, 'fc2_b': fc2_b}
    _L0_ffn_all = _L0_ffn_setup()
    _L0_ffn_in = {k: v for k, v in _L0_ffn_all.items() if k in ('Wg', 'alpha', 'ln_w', 'ln_b', 'fc1_w', 'fc1_b', 'fc2_w', 'fc2_b')}
    del _L0_ffn_all

    def _L1_xattn_setup():
        import jax, jax.numpy as jnp
        import numpy as np
        D_MODEL = 128
        NUM_HEADS = 16
        D_K = D_MODEL // NUM_HEADS

        def _split_heads(x):
            B, S, D = x.shape
            return x.reshape(B, S, NUM_HEADS, D_K).transpose(0, 2, 1, 3)
        key = jax.random.key(seed)
        ks = jax.random.split(key, 11)
        B, S, D = (2, 256, D_MODEL)
        s = 1.0 / np.sqrt(D)
        return {'Q': jax.random.normal(ks[0], (B, S, D), jnp.float32), 'K': jax.random.normal(ks[1], (B, S, D), jnp.float32), 'V': jax.random.normal(ks[2], (B, S, D), jnp.float32), 'Wq': jax.random.normal(ks[3], (D, D), jnp.float32) * s, 'bq': jax.random.normal(ks[4], (D,), jnp.float32) * s, 'Wk': jax.random.normal(ks[5], (D, D), jnp.float32) * s, 'bk': jax.random.normal(ks[6], (D,), jnp.float32) * s, 'Wv': jax.random.normal(ks[7], (D, D), jnp.float32) * s, 'bv': jax.random.normal(ks[8], (D,), jnp.float32) * s, 'Wo': jax.random.normal(ks[9], (D, D), jnp.float32) * s, 'bo': jax.random.normal(ks[10], (D,), jnp.float32) * s}
    _L1_xattn_all = _L1_xattn_setup()
    _L1_xattn_in = {k: v for k, v in _L1_xattn_all.items() if k in ('Wq', 'bq', 'Wk', 'bk', 'Wv', 'bv', 'Wo', 'bo')}
    del _L1_xattn_all

    def _L1_ffn_setup():
        import jax, jax.numpy as jnp
        import numpy as np
        EPS = 1e-05

        def _ln(x, g, b):
            mu = jnp.mean(x, axis=-1, keepdims=True)
            var = jnp.mean(jnp.square(x - mu), axis=-1, keepdims=True)
            return (x - mu) * jax.lax.rsqrt(var + EPS) * g + b

        def _forward(x, index_b, index_t, sw1, sb1, sw2, sb2, sw3, sb3, s_ln_g, s_ln_b, sg_w, sg_b, eg_w, eg_b, exp_bias, ew1, eb1, ew2, eb2, ew3, eb3, sel_ln_g, sel_ln_b):
            x1 = jnp.einsum('btd,hd->bth', x, sw1) + sb1
            x2 = jnp.einsum('btd,hd->bth', x, sw2) + sb2
            sh = _ln(jax.nn.silu(x1) * x2, s_ln_g, s_ln_b)
            shared_out = jnp.einsum('bth,dh->btd', sh, sw3) + sb3
            x_moe = x[index_b, index_t]
            shared_scores = jax.nn.sigmoid(x_moe @ sg_w.T + sg_b)
            expert_scores = jax.nn.sigmoid(x_moe @ eg_w.T + eg_b)
            top1_idx = jnp.argmax(expert_scores + exp_bias, axis=-1)
            top1_score = jnp.take_along_axis(expert_scores, top1_idx[:, None], axis=-1)
            weights = jax.nn.softmax(jnp.concatenate([shared_scores, top1_score], axis=-1), axis=-1)
            shared_w, expert_w = (weights[:, 0], weights[:, 1])
            shared_moe_out = shared_out[index_b, index_t] * shared_w[:, None]
            h1 = jnp.einsum('md,ehd->meh', x_moe, ew1) + eb1
            h2 = jnp.einsum('md,ehd->meh', x_moe, ew2) + eb2
            z = _ln(jax.nn.silu(h1) * h2, sel_ln_g, sel_ln_b)
            out_all = jnp.einsum('meh,edh->med', z, ew3) + eb3
            expert_out = jnp.take_along_axis(out_all, top1_idx[:, None, None], axis=1)[:, 0]
            expert_moe_out = expert_out * expert_w[:, None]
            final_out = shared_out.at[index_b, index_t].set(shared_moe_out + expert_moe_out)
            return final_out
        B, T, D, E, H, M = (2, 256, 128, 8, 64, 256)
        key = jax.random.key(seed)
        ks = jax.random.split(key, 24)
        s = 0.02
        inp = {}
        inp['x'] = jax.random.normal(ks[0], (B, T, D), jnp.float32)
        flat = jnp.arange(M, dtype=jnp.int32) * 2
        inp['index_b'] = flat // T
        inp['index_t'] = flat % T
        inp['sw1'] = jax.random.normal(ks[1], (H, D), jnp.float32) * s
        inp['sb1'] = jnp.zeros((H,), jnp.float32)
        inp['sw2'] = jax.random.normal(ks[2], (H, D), jnp.float32) * s
        inp['sb2'] = jnp.zeros((H,), jnp.float32)
        inp['sw3'] = jax.random.normal(ks[3], (D, H), jnp.float32) * s
        inp['sb3'] = jnp.zeros((D,), jnp.float32)
        inp['s_ln_g'] = jnp.ones((H,), jnp.float32)
        inp['s_ln_b'] = jnp.zeros((H,), jnp.float32)
        inp['sg_w'] = jax.random.normal(ks[4], (1, D), jnp.float32) * s
        inp['sg_b'] = jnp.zeros((1,), jnp.float32)
        inp['eg_w'] = jax.random.normal(ks[5], (E, D), jnp.float32) * s
        inp['eg_b'] = jnp.zeros((E,), jnp.float32)
        inp['exp_bias'] = jnp.zeros((E,), jnp.float32)
        inp['ew1'] = jax.random.normal(ks[6], (E, H, D), jnp.float32) * s
        inp['eb1'] = jnp.zeros((E, H), jnp.float32)
        inp['ew2'] = jax.random.normal(ks[7], (E, H, D), jnp.float32) * s
        inp['eb2'] = jnp.zeros((E, H), jnp.float32)
        inp['ew3'] = jax.random.normal(ks[8], (E, D, H), jnp.float32) * s
        inp['eb3'] = jnp.zeros((E, D), jnp.float32)
        inp['sel_ln_g'] = jnp.ones((H,), jnp.float32)
        inp['sel_ln_b'] = jnp.zeros((H,), jnp.float32)
        return inp
    _L1_ffn_all = _L1_ffn_setup()
    _L1_ffn_in = {k: v for k, v in _L1_ffn_all.items() if k in ('index_b', 'index_t', 'sw1', 'sb1', 'sw2', 'sb2', 'sw3', 'sb3', 's_ln_g', 's_ln_b', 'sg_w', 'sg_b', 'eg_w', 'eg_b', 'exp_bias', 'ew1', 'eb1', 'ew2', 'eb2', 'ew3', 'eb3', 'sel_ln_g', 'sel_ln_b')}
    del _L1_ffn_all

    def _L2_xattn_setup():
        import jax, jax.numpy as jnp
        import numpy as np
        HIDDEN = 128
        key = jax.random.key(seed)
        kq, kk, kwq, kwk, kwv = jax.random.split(key, 5)
        B, S, D = (4, 256, HIDDEN)
        query = jax.random.normal(kq, (B, S, D), dtype=jnp.float32)
        key_t = jax.random.normal(kk, (B, S, D), dtype=jnp.float32)
        scale = 1.0 / np.sqrt(D)
        Wq = jax.random.normal(kwq, (D, D), dtype=jnp.float32) * scale
        Wk = jax.random.normal(kwk, (D, D), dtype=jnp.float32) * scale
        Wv = jax.random.normal(kwv, (D, D), dtype=jnp.float32) * scale
        return {'query': query, 'key': key_t, 'Wq': Wq, 'Wk': Wk, 'Wv': Wv}
    _L2_xattn_all = _L2_xattn_setup()
    _L2_xattn_in = {k: v for k, v in _L2_xattn_all.items() if k in ('Wq', 'Wk', 'Wv')}
    del _L2_xattn_all

    def _L2_ffn_setup():
        import jax, jax.numpy as jnp
        import numpy as np
        QMAX = 127.0

        def _ste_round(v):
            return v + jax.lax.stop_gradient(jnp.round(v) - v)

        def _act_fake_quant(x, clip_factor):
            scale = jax.nn.sigmoid(clip_factor) * jnp.max(jnp.abs(x)) / QMAX
            return jnp.clip(_ste_round(x / scale), -QMAX - 1.0, QMAX) * scale

        def _weight_fake_quant(w):
            scale = jnp.max(jnp.abs(w), axis=1, keepdims=True) / QMAX
            return jnp.clip(_ste_round(w / scale), -QMAX - 1.0, QMAX) * scale
        key = jax.random.key(seed)
        k1, k2, k3, k4 = jax.random.split(key, 4)
        B, S, H, I = (8, 1024, 128, 352)
        return {'x': jax.random.normal(k1, (B, S, H), dtype=jnp.float32), 'clip_x': jnp.full((1,), 4.0, dtype=jnp.float32), 'clip_down': jnp.full((1,), 4.0, dtype=jnp.float32), 'w_gate': jax.random.normal(k2, (I, H), dtype=jnp.float32) * 0.02, 'w_up': jax.random.normal(k3, (I, H), dtype=jnp.float32) * 0.02, 'w_down': jax.random.normal(k4, (H, I), dtype=jnp.float32) * 0.02}
    _L2_ffn_all = _L2_ffn_setup()
    _L2_ffn_in = {k: v for k, v in _L2_ffn_all.items() if k in ('clip_x', 'clip_down', 'w_gate', 'w_up', 'w_down')}
    del _L2_ffn_all

    def _L3_xattn_setup():
        import jax, jax.numpy as jnp
        import numpy as np
        key = jax.random.key(seed)
        ks = jax.random.split(key, 8)
        B, L, D, H, Dh = (2, 256, 128, 16, 64)
        scale = 1.0 / np.sqrt(D)
        return {'inputs_q': jax.random.normal(ks[0], (B, L, D), jnp.float32), 'inputs_kv': jax.random.normal(ks[1], (B, L, D), jnp.float32), 'mask_k': jax.random.uniform(ks[2], (B, L), jnp.float32), 'Wq': jax.random.normal(ks[3], (D, H, Dh), jnp.float32) * scale, 'bq': jnp.zeros((H, Dh), jnp.float32), 'Wk': jax.random.normal(ks[4], (D, H, Dh), jnp.float32) * scale, 'bk': jnp.zeros((H, Dh), jnp.float32), 'Wv': jax.random.normal(ks[5], (D, H, Dh), jnp.float32) * scale, 'bv': jnp.zeros((H, Dh), jnp.float32), 'Wo': jax.random.normal(ks[6], (H, Dh, D), jnp.float32) * (1.0 / np.sqrt(D)), 'bo': jnp.zeros((D,), jnp.float32)}
    _L3_xattn_all = _L3_xattn_setup()
    _L3_xattn_in = {k: v for k, v in _L3_xattn_all.items() if k in ('Wq', 'bq', 'Wk', 'bk', 'Wv', 'bv', 'Wo', 'bo')}
    del _L3_xattn_all

    def _L3_ffn_setup():
        import jax, jax.numpy as jnp
        import numpy as np
        HID = 128
        NH = 16
        NKV = 4
        HD = HID // NH
        E = 8
        TOPK = 2
        FFN = 256
        EPS = 1e-05
        THETA = 10000.0

        def _rmsnorm(x, w):
            var = jnp.mean(x * x, axis=-1, keepdims=True)
            return x * jax.lax.rsqrt(var + EPS) * w

        def _rope_tables(S):
            inv_freq = 1.0 / THETA ** (jnp.arange(0, HD, 2, dtype=jnp.float32) / HD)
            freqs = jnp.arange(S, dtype=jnp.float32)[:, None] * inv_freq[None, :]
            emb = jnp.concatenate([freqs, freqs], axis=-1)
            return (jnp.cos(emb), jnp.sin(emb))

        def _apply_rope(t, cos, sin):
            t1, t2 = jnp.split(t, 2, axis=-1)
            rot = jnp.concatenate([-t2, t1], axis=-1)
            return t * cos[None, :, None, :] + rot * sin[None, :, None, :]
        key = jax.random.key(seed)
        ks = jax.random.split(key, 6)
        B, S = (1, 256)
        x = jax.random.normal(ks[0], (B, S, HID), dtype=jnp.float32)
        wqkv = jax.random.normal(ks[1], ((NH + 2 * NKV) * HD, HID), dtype=jnp.float32) * 0.02
        wo = jax.random.normal(ks[2], (HID, NH * HD), dtype=jnp.float32) * 0.02
        gate_w = jax.random.normal(ks[3], (E, HID), dtype=jnp.float32) * 0.02
        w13 = jax.random.normal(ks[4], (E, 2 * FFN, HID), dtype=jnp.float32) * 0.02
        w2 = jax.random.normal(ks[5], (E, HID, FFN), dtype=jnp.float32) * 0.02
        return {'x': x, 'ln1_w': jnp.ones((HID,), jnp.float32), 'ln2_w': jnp.ones((HID,), jnp.float32), 'wqkv': wqkv, 'wo': wo, 'gate_w': gate_w, 'w13': w13, 'w2': w2}
    _L3_ffn_all = _L3_ffn_setup()
    _L3_ffn_in = {k: v for k, v in _L3_ffn_all.items() if k in ('ln1_w', 'ln2_w', 'wqkv', 'wo', 'gate_w', 'w13', 'w2')}
    del _L3_ffn_all
    return {'x': x, 'ctx_1024': ctx_1024, 'fside_BxS2_0': fside_BxS2_0, 'L0_xattn_w_out': _L0_xattn_in['w_out'], 'L0_xattn_b_out': _L0_xattn_in['b_out'], 'L0_ffn_Wg': _L0_ffn_in['Wg'], 'L0_ffn_alpha': _L0_ffn_in['alpha'], 'L0_ffn_ln_w': _L0_ffn_in['ln_w'], 'L0_ffn_ln_b': _L0_ffn_in['ln_b'], 'L0_ffn_fc1_w': _L0_ffn_in['fc1_w'], 'L0_ffn_fc1_b': _L0_ffn_in['fc1_b'], 'L0_ffn_fc2_w': _L0_ffn_in['fc2_w'], 'L0_ffn_fc2_b': _L0_ffn_in['fc2_b'], 'L1_xattn_Wq': _L1_xattn_in['Wq'], 'L1_xattn_bq': _L1_xattn_in['bq'], 'L1_xattn_Wk': _L1_xattn_in['Wk'], 'L1_xattn_bk': _L1_xattn_in['bk'], 'L1_xattn_Wv': _L1_xattn_in['Wv'], 'L1_xattn_bv': _L1_xattn_in['bv'], 'L1_xattn_Wo': _L1_xattn_in['Wo'], 'L1_xattn_bo': _L1_xattn_in['bo'], 'L1_ffn_index_b': _L1_ffn_in['index_b'], 'L1_ffn_index_t': _L1_ffn_in['index_t'], 'L1_ffn_sw1': _L1_ffn_in['sw1'], 'L1_ffn_sb1': _L1_ffn_in['sb1'], 'L1_ffn_sw2': _L1_ffn_in['sw2'], 'L1_ffn_sb2': _L1_ffn_in['sb2'], 'L1_ffn_sw3': _L1_ffn_in['sw3'], 'L1_ffn_sb3': _L1_ffn_in['sb3'], 'L1_ffn_s_ln_g': _L1_ffn_in['s_ln_g'], 'L1_ffn_s_ln_b': _L1_ffn_in['s_ln_b'], 'L1_ffn_sg_w': _L1_ffn_in['sg_w'], 'L1_ffn_sg_b': _L1_ffn_in['sg_b'], 'L1_ffn_eg_w': _L1_ffn_in['eg_w'], 'L1_ffn_eg_b': _L1_ffn_in['eg_b'], 'L1_ffn_exp_bias': _L1_ffn_in['exp_bias'], 'L1_ffn_ew1': _L1_ffn_in['ew1'], 'L1_ffn_eb1': _L1_ffn_in['eb1'], 'L1_ffn_ew2': _L1_ffn_in['ew2'], 'L1_ffn_eb2': _L1_ffn_in['eb2'], 'L1_ffn_ew3': _L1_ffn_in['ew3'], 'L1_ffn_eb3': _L1_ffn_in['eb3'], 'L1_ffn_sel_ln_g': _L1_ffn_in['sel_ln_g'], 'L1_ffn_sel_ln_b': _L1_ffn_in['sel_ln_b'], 'L2_xattn_Wq': _L2_xattn_in['Wq'], 'L2_xattn_Wk': _L2_xattn_in['Wk'], 'L2_xattn_Wv': _L2_xattn_in['Wv'], 'L2_ffn_clip_x': _L2_ffn_in['clip_x'], 'L2_ffn_clip_down': _L2_ffn_in['clip_down'], 'L2_ffn_w_gate': _L2_ffn_in['w_gate'], 'L2_ffn_w_up': _L2_ffn_in['w_up'], 'L2_ffn_w_down': _L2_ffn_in['w_down'], 'L3_xattn_Wq': _L3_xattn_in['Wq'], 'L3_xattn_bq': _L3_xattn_in['bq'], 'L3_xattn_Wk': _L3_xattn_in['Wk'], 'L3_xattn_bk': _L3_xattn_in['bk'], 'L3_xattn_Wv': _L3_xattn_in['Wv'], 'L3_xattn_bv': _L3_xattn_in['bv'], 'L3_xattn_Wo': _L3_xattn_in['Wo'], 'L3_xattn_bo': _L3_xattn_in['bo'], 'L3_ffn_ln1_w': _L3_ffn_in['ln1_w'], 'L3_ffn_ln2_w': _L3_ffn_in['ln2_w'], 'L3_ffn_wqkv': _L3_ffn_in['wqkv'], 'L3_ffn_wo': _L3_ffn_in['wo'], 'L3_ffn_gate_w': _L3_ffn_in['gate_w'], 'L3_ffn_w13': _L3_ffn_in['w13'], 'L3_ffn_w2': _L3_ffn_in['w2']}

def reference(x, ctx_1024, fside_BxS2_0, L0_xattn_w_out, L0_xattn_b_out, L0_ffn_Wg, L0_ffn_alpha, L0_ffn_ln_w, L0_ffn_ln_b, L0_ffn_fc1_w, L0_ffn_fc1_b, L0_ffn_fc2_w, L0_ffn_fc2_b, L1_xattn_Wq, L1_xattn_bq, L1_xattn_Wk, L1_xattn_bk, L1_xattn_Wv, L1_xattn_bv, L1_xattn_Wo, L1_xattn_bo, L1_ffn_index_b, L1_ffn_index_t, L1_ffn_sw1, L1_ffn_sb1, L1_ffn_sw2, L1_ffn_sb2, L1_ffn_sw3, L1_ffn_sb3, L1_ffn_s_ln_g, L1_ffn_s_ln_b, L1_ffn_sg_w, L1_ffn_sg_b, L1_ffn_eg_w, L1_ffn_eg_b, L1_ffn_exp_bias, L1_ffn_ew1, L1_ffn_eb1, L1_ffn_ew2, L1_ffn_eb2, L1_ffn_ew3, L1_ffn_eb3, L1_ffn_sel_ln_g, L1_ffn_sel_ln_b, L2_xattn_Wq, L2_xattn_Wk, L2_xattn_Wv, L2_ffn_clip_x, L2_ffn_clip_down, L2_ffn_w_gate, L2_ffn_w_up, L2_ffn_w_down, L3_xattn_Wq, L3_xattn_bq, L3_xattn_Wk, L3_xattn_bk, L3_xattn_Wv, L3_xattn_bv, L3_xattn_Wo, L3_xattn_bo, L3_ffn_ln1_w, L3_ffn_ln2_w, L3_ffn_wqkv, L3_ffn_wo, L3_ffn_gate_w, L3_ffn_w13, L3_ffn_w2):
    import jax
    import jax.numpy as jnp

    def _L0_xattn_ref(values, keys, query, w_out, b_out):
        import jax, jax.numpy as jnp
        import numpy as np
        EMBED_SIZE = 128
        HEADS = 16
        HEAD_DIM = EMBED_SIZE // HEADS
        N, q_len, _ = query.shape
        v_len = values.shape[1]
        k_len = keys.shape[1]
        v = values.reshape(N, v_len, HEADS, HEAD_DIM)
        k = keys.reshape(N, k_len, HEADS, HEAD_DIM)
        q = query.reshape(N, q_len, HEADS, HEAD_DIM)
        energy = jnp.einsum('nqhd,nkhd->nhqk', q, k)
        attn = jax.nn.softmax(energy / jnp.sqrt(jnp.float32(EMBED_SIZE)), axis=3)
        out = jnp.einsum('nhql,nlhd->nqhd', attn, v).reshape(N, q_len, EMBED_SIZE)
        return out @ w_out.T + b_out

    def _L0_ffn_ref(x, Wg, alpha, ln_w, ln_b, fc1_w, fc1_b, fc2_w, fc2_b):
        import jax, jax.numpy as jnp
        import numpy as np
        TOP_K = 2
        LN_EPS = 1e-05
        B, S, H, E, F = (2, 256, 128, 8, 512)

        def _layernorm(x, w, b):
            mu = jnp.mean(x, axis=-1, keepdims=True)
            var = jnp.mean(jnp.square(x - mu), axis=-1, keepdims=True)
            return (x - mu) * jax.lax.rsqrt(var + LN_EPS) * w + b
        b, s, h = x.shape
        xf = x.reshape(-1, h)
        logits = xf @ Wg
        top_vals, top_idx = jax.lax.top_k(logits, TOP_K)
        gate_score = jax.nn.softmax(top_vals, axis=-1)
        one_hot = jax.nn.one_hot(top_idx, Wg.shape[1], dtype=xf.dtype)
        comb = jnp.einsum('tke,tk->te', one_hot, gate_score) * alpha
        out = jnp.zeros_like(xf)
        for e in range(Wg.shape[1]):
            hdn = _layernorm(xf, ln_w[e], ln_b[e])
            a = jax.nn.gelu(hdn @ fc1_w[e] + fc1_b[e], approximate=True)
            y = a @ fc2_w[e] + fc2_b[e]
            out = out + y * comb[:, e:e + 1]
        return out.reshape(b, s, h)

    def _L1_xattn_ref(Q, K, V, Wq, bq, Wk, bk, Wv, bv, Wo, bo):
        import jax, jax.numpy as jnp
        import numpy as np
        D_MODEL = 128
        NUM_HEADS = 16
        D_K = D_MODEL // NUM_HEADS

        def _split_heads(x):
            B, S, D = x.shape
            return x.reshape(B, S, NUM_HEADS, D_K).transpose(0, 2, 1, 3)
        q = _split_heads(Q @ Wq + bq)
        k = _split_heads(K @ Wk + bk)
        v = _split_heads(V @ Wv + bv)
        scale = 1.0 / np.sqrt(D_K)
        scores = jnp.einsum('bhqd,bhkd->bhqk', q, k) * scale
        P = jax.nn.softmax(scores, axis=-1)
        O = jnp.einsum('bhqk,bhkd->bhqd', P, v)
        B, H, S, dk = O.shape
        O = O.transpose(0, 2, 1, 3).reshape(B, S, H * dk)
        return O @ Wo + bo

    def _L1_ffn_ref(x, index_b, index_t, sw1, sb1, sw2, sb2, sw3, sb3, s_ln_g, s_ln_b, sg_w, sg_b, eg_w, eg_b, exp_bias, ew1, eb1, ew2, eb2, ew3, eb3, sel_ln_g, sel_ln_b):
        import jax, jax.numpy as jnp
        import numpy as np
        EPS = 1e-05

        def _ln(x, g, b):
            mu = jnp.mean(x, axis=-1, keepdims=True)
            var = jnp.mean(jnp.square(x - mu), axis=-1, keepdims=True)
            return (x - mu) * jax.lax.rsqrt(var + EPS) * g + b

        def _forward(x, index_b, index_t, sw1, sb1, sw2, sb2, sw3, sb3, s_ln_g, s_ln_b, sg_w, sg_b, eg_w, eg_b, exp_bias, ew1, eb1, ew2, eb2, ew3, eb3, sel_ln_g, sel_ln_b):
            x1 = jnp.einsum('btd,hd->bth', x, sw1) + sb1
            x2 = jnp.einsum('btd,hd->bth', x, sw2) + sb2
            sh = _ln(jax.nn.silu(x1) * x2, s_ln_g, s_ln_b)
            shared_out = jnp.einsum('bth,dh->btd', sh, sw3) + sb3
            x_moe = x[index_b, index_t]
            shared_scores = jax.nn.sigmoid(x_moe @ sg_w.T + sg_b)
            expert_scores = jax.nn.sigmoid(x_moe @ eg_w.T + eg_b)
            top1_idx = jnp.argmax(expert_scores + exp_bias, axis=-1)
            top1_score = jnp.take_along_axis(expert_scores, top1_idx[:, None], axis=-1)
            weights = jax.nn.softmax(jnp.concatenate([shared_scores, top1_score], axis=-1), axis=-1)
            shared_w, expert_w = (weights[:, 0], weights[:, 1])
            shared_moe_out = shared_out[index_b, index_t] * shared_w[:, None]
            h1 = jnp.einsum('md,ehd->meh', x_moe, ew1) + eb1
            h2 = jnp.einsum('md,ehd->meh', x_moe, ew2) + eb2
            z = _ln(jax.nn.silu(h1) * h2, sel_ln_g, sel_ln_b)
            out_all = jnp.einsum('meh,edh->med', z, ew3) + eb3
            expert_out = jnp.take_along_axis(out_all, top1_idx[:, None, None], axis=1)[:, 0]
            expert_moe_out = expert_out * expert_w[:, None]
            final_out = shared_out.at[index_b, index_t].set(shared_moe_out + expert_moe_out)
            return final_out
        return _forward(x, index_b, index_t, sw1, sb1, sw2, sb2, sw3, sb3, s_ln_g, s_ln_b, sg_w, sg_b, eg_w, eg_b, exp_bias, ew1, eb1, ew2, eb2, ew3, eb3, sel_ln_g, sel_ln_b)

    def _L2_xattn_ref(query, key, Wq, Wk, Wv):
        import jax, jax.numpy as jnp
        import numpy as np
        HIDDEN = 128
        Q = jnp.einsum('bsd,ed->bse', query, Wq)
        K = jnp.einsum('bsd,ed->bse', key, Wk)
        V = jnp.einsum('bsd,ed->bse', key, Wv)
        alpha = jnp.einsum('bqd,bkd->bqk', Q, K)
        alpha = jax.nn.softmax(alpha, axis=2)
        out = jnp.einsum('bqk,bkd->bqd', alpha, V)
        return out

    def _L2_ffn_ref(x, clip_x, clip_down, w_gate, w_up, w_down):
        import jax, jax.numpy as jnp
        import numpy as np
        QMAX = 127.0

        def _ste_round(v):
            return v + jax.lax.stop_gradient(jnp.round(v) - v)

        def _act_fake_quant(x, clip_factor):
            scale = jax.nn.sigmoid(clip_factor) * jnp.max(jnp.abs(x)) / QMAX
            return jnp.clip(_ste_round(x / scale), -QMAX - 1.0, QMAX) * scale

        def _weight_fake_quant(w):
            scale = jnp.max(jnp.abs(w), axis=1, keepdims=True) / QMAX
            return jnp.clip(_ste_round(w / scale), -QMAX - 1.0, QMAX) * scale
        xq = _act_fake_quant(x, clip_x[0])
        gate = jnp.einsum('bsh,ih->bsi', xq, _weight_fake_quant(w_gate))
        up = jnp.einsum('bsh,ih->bsi', xq, _weight_fake_quant(w_up))
        h = _act_fake_quant(jax.nn.silu(gate) * up, clip_down[0])
        return jnp.einsum('bsi,hi->bsh', h, _weight_fake_quant(w_down))

    def _L3_xattn_ref(inputs_q, inputs_kv, mask_k, Wq, bq, Wk, bk, Wv, bv, Wo, bo):
        import jax, jax.numpy as jnp
        import numpy as np
        q = jnp.einsum('bld,dhk->blhk', inputs_q, Wq) + bq
        k = jnp.einsum('bld,dhk->blhk', inputs_kv, Wk) + bk
        v = jnp.einsum('bld,dhk->blhk', inputs_kv, Wv) + bv
        v = mask_k[:, :, None, None] * v
        head_dim = q.shape[-1]
        q = q / jnp.sqrt(jnp.asarray(head_dim, q.dtype))
        scores = jnp.einsum('bqhk,bshk->bhqs', q, k)
        probs = jax.nn.softmax(scores, axis=-1)
        x = jnp.einsum('bhqs,bshk->bqhk', probs, v)
        out = jnp.einsum('bqhk,hkd->bqd', x, Wo) + bo
        return out

    def _L3_ffn_ref(x, ln1_w, ln2_w, wqkv, wo, gate_w, w13, w2):
        import jax, jax.numpy as jnp
        import numpy as np
        HID = 128
        NH = 16
        NKV = 4
        HD = HID // NH
        E = 8
        TOPK = 2
        FFN = 256
        EPS = 1e-05
        THETA = 10000.0

        def _rmsnorm(x, w):
            var = jnp.mean(x * x, axis=-1, keepdims=True)
            return x * jax.lax.rsqrt(var + EPS) * w

        def _rope_tables(S):
            inv_freq = 1.0 / THETA ** (jnp.arange(0, HD, 2, dtype=jnp.float32) / HD)
            freqs = jnp.arange(S, dtype=jnp.float32)[:, None] * inv_freq[None, :]
            emb = jnp.concatenate([freqs, freqs], axis=-1)
            return (jnp.cos(emb), jnp.sin(emb))

        def _apply_rope(t, cos, sin):
            t1, t2 = jnp.split(t, 2, axis=-1)
            rot = jnp.concatenate([-t2, t1], axis=-1)
            return t * cos[None, :, None, :] + rot * sin[None, :, None, :]
        B, S, _ = x.shape
        h = _rmsnorm(x, ln1_w)
        qkv = jnp.einsum('bsh,oh->bso', h, wqkv)
        q = qkv[..., :NH * HD].reshape(B, S, NH, HD)
        k = qkv[..., NH * HD:(NH + NKV) * HD].reshape(B, S, NKV, HD)
        v = qkv[..., (NH + NKV) * HD:].reshape(B, S, NKV, HD)
        cos, sin = _rope_tables(S)
        q = _apply_rope(q, cos, sin)
        k = _apply_rope(k, cos, sin)
        groups = NH // NKV
        k = jnp.repeat(k, groups, axis=2)
        v = jnp.repeat(v, groups, axis=2)
        scale = HD ** (-0.5)
        scores = jnp.einsum('bqhd,bkhd->bhqk', q, k) * scale
        causal = jnp.tril(jnp.ones((S, S), dtype=bool))
        scores = jnp.where(causal[None, None], scores, jnp.finfo(scores.dtype).min)
        probs = jax.nn.softmax(scores, axis=-1)
        attn = jnp.einsum('bhqk,bkhd->bqhd', probs, v).reshape(B, S, NH * HD)
        x = x + jnp.einsum('bso,ho->bsh', attn, wo)
        h = _rmsnorm(x, ln2_w).reshape(-1, HID)
        T = h.shape[0]
        logits = jnp.einsum('th,eh->te', h, gate_w)
        rprobs = jax.nn.softmax(logits.astype(jnp.float32), axis=-1)
        topw, topi = jax.lax.top_k(rprobs, TOPK)
        topw = topw / jnp.sum(topw, axis=-1, keepdims=True)
        wfull = jnp.zeros((T, E), jnp.float32).at[jnp.arange(T)[:, None], topi].set(topw)
        wfull = wfull.astype(h.dtype)
        out = jnp.zeros((T, HID), h.dtype)
        for e in range(E):
            w1 = w13[e, :FFN]
            w3 = w13[e, FFN:]
            g = jax.nn.silu(h @ w1.T) * (h @ w3.T)
            out = out + jnp.einsum('tf,hf->th', g, w2[e]) * wfull[:, e:e + 1]
        return x + out.reshape(B, S, HID)
    x = x + _L0_xattn_ref(ctx_1024, ctx_1024, _layernorm(x, axis=-1), L0_xattn_w_out, L0_xattn_b_out)
    x = x + _L0_ffn_ref(_layernorm(x, axis=-1), L0_ffn_Wg, L0_ffn_alpha, L0_ffn_ln_w, L0_ffn_ln_b, L0_ffn_fc1_w, L0_ffn_fc1_b, L0_ffn_fc2_w, L0_ffn_fc2_b)
    x = x + _L1_xattn_ref(_layernorm(x, axis=-1), ctx_1024, ctx_1024, L1_xattn_Wq, L1_xattn_bq, L1_xattn_Wk, L1_xattn_bk, L1_xattn_Wv, L1_xattn_bv, L1_xattn_Wo, L1_xattn_bo)
    x = x + _L1_ffn_ref(_layernorm(x, axis=-1), L1_ffn_index_b, L1_ffn_index_t, L1_ffn_sw1, L1_ffn_sb1, L1_ffn_sw2, L1_ffn_sb2, L1_ffn_sw3, L1_ffn_sb3, L1_ffn_s_ln_g, L1_ffn_s_ln_b, L1_ffn_sg_w, L1_ffn_sg_b, L1_ffn_eg_w, L1_ffn_eg_b, L1_ffn_exp_bias, L1_ffn_ew1, L1_ffn_eb1, L1_ffn_ew2, L1_ffn_eb2, L1_ffn_ew3, L1_ffn_eb3, L1_ffn_sel_ln_g, L1_ffn_sel_ln_b)
    x = x + _L2_xattn_ref(_layernorm(x, axis=-1), ctx_1024, L2_xattn_Wq, L2_xattn_Wk, L2_xattn_Wv)
    x = x + _L2_ffn_ref(_layernorm(x, axis=-1), L2_ffn_clip_x, L2_ffn_clip_down, L2_ffn_w_gate, L2_ffn_w_up, L2_ffn_w_down)
    x = x + _L3_xattn_ref(_layernorm(x, axis=-1), ctx_1024, fside_BxS2_0, L3_xattn_Wq, L3_xattn_bq, L3_xattn_Wk, L3_xattn_bk, L3_xattn_Wv, L3_xattn_bv, L3_xattn_Wo, L3_xattn_bo)
    x = x + _L3_ffn_ref(_layernorm(x, axis=-1), L3_ffn_ln1_w, L3_ffn_ln2_w, L3_ffn_wqkv, L3_ffn_wo, L3_ffn_gate_w, L3_ffn_w13, L3_ffn_w2)
    return x

_drawn_inputs = setup_inputs


def setup_inputs(seed=0):
    import zlib

    import numpy as np

    out = dict(_drawn_inputs(seed))
    spreads = {'L0_xattn_b_out': (0.0, 0.1),
     'L0_ffn_ln_w': (1.0, 0.6),
     'L0_ffn_ln_b': (0.0, 0.8),
     'L0_ffn_fc1_b': (0.0, 0.418),
     'L0_ffn_fc2_b': (0.0, 0.1),
     'L1_ffn_sb1': (0.0, 0.1),
     'L1_ffn_sb2': (0.0, 0.1),
     'L1_ffn_sb3': (0.0, 0.1),
     'L1_ffn_s_ln_g': (1.0, 0.2),
     'L1_ffn_s_ln_b': (0.0, 0.61),
     'L1_ffn_eg_b': (0.0, 0.8),
     'L1_ffn_exp_bias': (0.0, 0.1),
     'L1_ffn_eb1': (0.0, 0.267),
     'L1_ffn_eb2': (0.0, 0.1),
     'L1_ffn_eb3': (0.0, 0.1),
     'L1_ffn_sel_ln_g': (1.0, 0.6),
     'L1_ffn_sel_ln_b': (0.0, 0.8),
     'L3_xattn_bq': (0.0, 0.424),
     'L3_xattn_bk': (0.0, 0.8),
     'L3_xattn_bv': (0.0, 0.1),
     'L3_xattn_bo': (0.0, 0.1),
     'L3_ffn_ln1_w': (1.0, 0.6),
     'L3_ffn_ln2_w': (1.0, 0.6)}
    factors = {'L1_xattn_bk': 8.0,
     'L1_ffn_sg_w': 8.0,
     'L1_ffn_eg_w': 8.0,
     'L2_ffn_w_gate': 8.0,
     'L2_ffn_w_up': 8.0,
     'L2_ffn_w_down': 8.0,
     'L3_ffn_wqkv': 4.47,
     'L3_ffn_wo': 4.912,
     'L3_ffn_gate_w': 8.0,
     'L3_ffn_w13': 8.0,
     'L3_ffn_w2': 8.0}
    for name, (base, spread) in spreads.items():
        noise = np.random.default_rng([zlib.crc32(name.encode()), seed]).standard_normal(out[name].shape)
        drawn = base * np.exp(spread * noise) if base else spread * noise
        out[name] = jnp.asarray(drawn.astype(out[name].dtype))
    for name, factor in factors.items():
        out[name] = (out[name] * factor).astype(out[name].dtype)
    return out
```

```python
from contextlib import ExitStack

import numpy as np

import concourse.bass as bass
from concourse import mybir

F32 = mybir.dt.float32
BF16 = mybir.dt.bfloat16
I32 = mybir.dt.int32
U32 = mybir.dt.uint32
ALU = mybir.AluOpType
ACT = mybir.ActivationFunctionType
AX_X = mybir.AxisListType.X
ABSMAX = bass.bass_isa.ReduceOp.absmax

P = 128
NT = 4
T = NT * P
B = 2
SQ = T // B
SK = 512
NK = B * SK
KT = NK // P
H = 16
HD = 8
NPART = 3
PAD = 96
MROW = PAD + 4 * NPART
VW = 32
G = 8
E = 8
F0 = 512
H1 = 64
NU = E + 1
I2 = 352
I2R = I2 - 2 * P
DH3 = 64
KV3 = 4
F3 = 256
EPS = 1e-5
ROUND = 1.5 * 2.0 ** 23
QMAX = 127.0
NEG = -1e30

CONST = dict(ident=P, mask_n=P, mask_t=P, cos=NT * HD, sin=NT * HD, tokpos=2, eidx=E)
COLS = dict(ln0_w=E, ln0_b=E, fc1_b=E * 4, gcol=5, bq3=8, bk3=8, rms1=1, rms2=1, maskk=KT,
            bsel=5 * NU, fc2_b=P, b9=P)
ROWS = dict(bo0=P, alpha=E, bq1=P, bk1=P, bv1=P, bo1=P, gb=NU, ebias=E, bo3=P,
            clip=2, bv3=1024)
W_A = dict(wo0=P, wg0=E)
W_B = dict(wq1=P, wk1=P, wv1=P, wo1=P)
W_C = dict(w12=NU * P, w3=5 * P)
W_D = dict(wg1=NU, wq2=P, wk2=P, wv2=P, wqkv=192, wo3f=P,
           gate3=E, wo3=8 * P)


def columns(widths):
    at, out = 0, {}
    for name, width in widths.items():
        out[name] = (at, at + width)
        at += width
    return out, at


def mega_kernel(nc, d, out_dram, stop=99):
    ctx = ExitStack()
    with ctx:
        def sb(name, shape, dt=F32):
            return ctx.enter_context(nc.sbuf_tensor(name, shape, dt))

        def sem(name):
            return ctx.enter_context(nc.semaphore(name))

        def pack(name, widths):
            at, width = columns(widths)
            t = sb(name, [P, width])
            return t, {k: t[:, a:b] for k, (a, b) in at.items()}

        const_t, C = pack("const_t", CONST)
        cols_t, CB = pack("cols_t", COLS)
        rows_t, RB = pack("rows_t", ROWS)
        wa_t, WA = pack("wa_t", W_A)
        wb_t, WB = pack("wb_t", W_B)
        wd_t, WD = pack("wd_t", W_D)
        Kst = sb("Kst", [P, H, NK], BF16)
        Qst = sb("Qst", [P, H, T], BF16)
        REP = sb("REP", [P, 4 * H * PAD], BF16)
        REPv = REP[:, :].rearrange("p (t h r) -> p t h r", t=4, h=H)
        VX = sb("VX", [P, 8192])
        Vaug = VX[:, 0:4096].rearrange("p (k h w) -> p k h w", k=KT, h=H)
        w12 = VX[:, 4096:4096 + NU * P]
        b12 = VX[:, 5888:5888 + NU * P]
        w3s = VX[:, 5248:5248 + 5 * P].rearrange("p (u n) -> p u n", u=5)
        K3 = VX[:, :].rearrange("p (r k) -> p r k", r=8)
        V3 = Kst[:, :, :].rearrange("p h k -> p (h k)").bitcast(F32).rearrange("p (k n) -> p k n", k=KT)
        FC = sb("FC", [P, 8192])
        fc1 = FC[:, 0:4096].rearrange("p (e f) -> p e f", e=E)
        fc2 = FC[:, 4096:8192].rearrange("p (e c n) -> p e c n", e=E, c=4)
        Q3 = FC[:, :].rearrange("p (h t) -> p h t", h=H)
        w13 = FC[:, 0:4096].rearrange("p (e f) -> p e f", e=E)
        w2e = FC[:, 4096:6144].rearrange("p (e c n) -> p e c n", e=E, c=2)
        W3 = REP[:, :].bitcast(F32).rearrange("p (m n) -> p m n", m=3)
        OT3 = REP[:, 0:4096].bitcast(F32).rearrange("p (r q) -> p r q", r=8)
        PR = sb("PR", [P, 8192])
        PRg = PR[:, :].rearrange("p (s n) -> p s n", s=2)
        actT = PR[:, 0:4096].rearrange("p (s c t) -> p s c t", s=2, c=4)
        hdT = PR[:, 4096:5120].rearrange("p (s t) -> p s t", s=2)
        HH = PR[:, 0:NT * NU * P].rearrange("p (t u n) -> p t u n", t=NT, u=NU)
        U = PR[:, 4608:4608 + NT * 10 * H1].rearrange("p (t u n) -> p t u n", t=NT, u=10)
        SL = FC[:, 0:NT * NU * H1].rearrange("p (t u n) -> p t u n", t=NT, u=NU)
        idf = FC[:, 2304:3328].rearrange("p (a n) -> p a n", a=4)
        eqm = FC[:, 3328:4352].rearrange("p (a n) -> p a n", a=NT)
        KT2 = FC[:, 4608:5632]
        V2 = FC[:, 5632:6656].rearrange("p (k n) -> p k n", k=KT)
        w2_t = FC[:, 6656:6656 + 6 * P + I2]
        WD2 = dict(gate2=w2_t[:, 0:3 * P], up2=w2_t[:, 3 * P:6 * P], down2=w2_t[:, 6 * P:])
        bf = FC[:, 0:2304].bitcast(BF16)
        wq2i = bf[:, 0:768].rearrange("p (m c n) -> p m c n", m=2, c=3)
        wgT = bf[:, 768:1536].rearrange("p (m c n) -> p m c n", m=2, c=3)
        wdT = bf[:, 1536:1920].rearrange("p (c n) -> p c n", c=3)
        wd2i = bf[:, 1920:1920 + I2]
        xqi = bf[:, 2304:2816].rearrange("p (t n) -> p t n", t=NT)
        xqT = bf[:, 2816:3328]
        hqT = FC[:, 2304:3072].bitcast(BF16).rearrange("p (c t) -> p c t", c=3)
        K4 = FC[:, 6144:7168].bitcast(BF16).rearrange("p (h t) -> p h t", h=KV3)
        V4 = FC[:, 7168:7680].rearrange("p (t h w) -> p t h w", t=NT, h=KV3)
        ZT = PR[:, 0:5 * T].rearrange("p (r t) -> p r t", r=5)
        P2 = PR[:, 0:2048].rearrange("p (t k) -> p t k", t=NT)
        PT2 = PR[:, 2048:4096].rearrange("p (t k q) -> p t k q", t=NT, k=4)
        SG = PR[:, 4096:5632].rearrange("p (c t) -> p c t", c=3)
        h2T = PR[:, 5632:7168].rearrange("p (c t) -> p c t", c=3)
        qrope = PR[:, 0:NT * 160].rearrange("p (t n) -> p t n", t=NT)
        qrot = PR[:, 1024:1024 + NT * 160].rearrange("p (t n) -> p t n", t=NT)
        x = sb("x", [P, NT, P])
        xn = sb("xn", [P, NT, P])
        scr = sb("scr", [P, 4 * T])
        lnT = scr[:, 0:T]
        zT = scr[:, T:2 * T]
        Onat = scr[:, 2 * T:3 * T].rearrange("p (t n) -> p t n", t=NT)
        OT = scr[:, 3 * T:4 * T]
        OT3b = [OT3, scr[:, :].rearrange("p (r q) -> p r q", r=8)]
        parts = sb("parts", [P, NPART, T], BF16)
        rest = sb("rest", [P, T])
        ctxT = sb("ctxT", [P, NK])
        CTXN = PR[:, 0:1024].rearrange("p (k n) -> p k n", k=KT)
        identb = sb("identb", [P, P], BF16)
        maskb = sb("maskb", [P, 2, P], BF16)
        onesel = sb("onesel", [P, 4, P], BF16)
        ones = sb("ones", [P, VW])
        st6 = sb("st6", [P, NT, 6])
        mv = sb("mv", [P, NT, 2])
        ve = sb("ve", [P, 64])
        nhalf = sb("nhalf", [P, 64])
        rstd = sb("rstd", [P, 64])
        mxs = sb("mxs", [P, 2, 2, 4])
        mr = sb("mr", [P, 8])
        mp = sb("mp", [P, 2, 2, NPART, 4], BF16)
        rden = sb("rden", [P, 2, 4])
        rden3 = sb("rden3", [P, SQ])
        lg = sb("lg", [P, NT, NU])
        v8 = sb("v8", [P, NT, E])
        i8 = sb("i8", [P, NT, E], U32)
        i8f = sb("i8f", [P, NT, E])
        gt = sb("gt", [P, NT, 8])
        oh = sb("oh", [P, 2, NT, E])
        comb = sb("comb", [P, NT, NU])
        combT = sb("combT", [NU, T])
        b9s = sb("b9s", [NU, P])
        idx = sb("idx", [P, 2, 256], I32)
        tmask = sb("tmask", [P, NT])
        qs = sb("qs", [P, 48])

        ps = ctx.enter_context(nc.psum_tensor("ps", [P, 8, 512], F32))

        def bank(b, n=1):
            return ps[:, b:b + n, :].rearrange("p b n -> p (b n)")

        def bankb(b):
            return ps[:, b, :].bitcast(BF16)

        names = """ld_const ld_x ld_ctxT ld_ctx ld_cols ld_rows ld_sel ld_wa ld_wb ld_fc1 ld_fc2
            ld_w12 ld_w3s ld_b12 ld_w2 ld_wd ld_w3 ld_idx ld_w13 ld_w2e
            dve_done pool_done act_done setup_dve setup_pool
            rep_ready rep_turned stack_dve stack_act
            var_ready rstd_ready xn_ready xn_turned lnT_ready
            smax_ready smax_read m_ready m_turned mrow_ready st_ready p_ready pv_ready ot_ready
            ot_turned o_ready onat_turned onatT_ready proj_ready x_ready
            kv1_ready kv1_read logit_ready comb_ready comb_turned combT_ready hd_ready hd_used
            h_ready act_ready y_ready y_added gate_exp gate_diff
            u_ready hh_ready silu_ready c_ready sq_ready sqr_ready var1_ready rstd1_ready z_ready z_turned zT_dve zT_act
            b9_ready b9_read
            kv2_ready kv2_read q2_ready q2_read s2_ready nm2_ready p2_ready p2_turned pt2_ready
            wq_ready wq_turned wq_read ax_ready ax_all scales_ready clip_ready clip_exp xq_ready xq_turned
            xqT_ready g2_ready sg_ready h2_ready hq_ready y2_ready y2_read y2_turned
            k3_ready k3_dve k3_act v3_ready v3_read v3_masked q3_ready q3_dve q3_act
            rope_turned rope_read qkv_ready v4_ready
            stored""".split()
        S = {n: sem(n) for n in names}
        s = type("Sems", (), S)

        block = ctx.enter_context(nc.Block())

        tiles = []
        for layer in (0, 1):
            tiles += [("k", t, H) for t in range(4)] + [("q", t, H) for t in range(2)]
            tiles += [("k", t, H) for t in range(4, 8)] + [("q", t, H) for t in range(2, 4)]
        for t in range(NT):
            tiles += [("4", t, KV3), ("q", t, H)]
        lots = []
        lots_till = []
        for n, (_, _, heads) in enumerate(tiles):
            for h in range(0, heads, 8):
                lots.append((n, h, min(8, heads)))
            lots_till.append(len(lots))
        PHASE_TILES = [range(0, 12), range(12, 24), range(24, 32)]

        def stacked(eng, till_tile):
            n = lots_till[till_tile]
            eng.wait_ge(s.stack_dve, (n + 1) // 2)
            eng.wait_ge(s.stack_act, n // 2)

        MAXB = [0, 64, 128, 192, 192 + 24]
        UNIT = [0, 32, 64, 96, 96 + 16]

        TURNS = [1, 2, 3, 4, 5, 7, 9, 10]

        def groups(a, g):
            return a * G + g

        def stack_copy(eng, n, tl, h0, nh):
            kind, t, _ = tiles[tl]
            dst = {"k": Kst, "q": Qst, "4": K4}[kind]
            src = bankb(3 + n % 4)[0:PAD, 0:nh * P].rearrange("p (h t) -> p h t", h=nh)
            to = dst[0:PAD, h0:h0 + nh, t * P:(t + 1) * P]
            return eng.tensor_copy(to, src) if eng is nc.vector else eng.copy(to, src)

        SCALES = [float(P) ** -0.5, float(HD) ** -0.5, float(DH3) ** -0.5, float(HD) ** -0.5]

        def group_heads(a, g):
            return g // 4, 4 * (g % 4)

        def ot_index(a, g):
            return (a if a < 2 else 2) * G + g

        def add_expert(dve, e, count, b0, y_base=0):
            dve.wait_ge(s.y_ready, y_base + e + 1)
            if count:
                dve.wait_ge(s.y_added, count)
            y = bank(b0 + e % 2).rearrange("p (t n) -> p t n", t=NT)
            for t in range(NT):
                i = dve.scalar_tensor_tensor(out=x[:, t, :], in0=y[:, t, :], scalar=comb[:, t, e:e + 1],
                                             in1=x[:, t, :], op0=ALU.mult, op1=ALU.add)
            i.then_inc(s.y_added, 1)

        @block.sync
        def _(sp):
            sp.dma_start(const_t[:, :], d["const"]).then_inc(s.ld_const, 16)
            sp.dma_start(x[:, :, :], d["x"]).then_inc(s.ld_x, 16)
            sp.dma_start(CTXN, d["ctx"]).then_inc(s.ld_ctx, 16)
            sp.dma_start(rows_t[:, :], d["rows"]).then_inc(s.ld_rows, 16)
            sp.dma_start(Kst[PAD:MROW, :, :], d["sel"]).then_inc(s.ld_sel, 16)
            sp.dma_start(onesel[:, :, :], d["onesel"]).then_inc(s.ld_sel, 16)
            sp.dma_start(wa_t[:, :], d["w_a"]).then_inc(s.ld_wa, 16)
            sp.dma_start(cols_t[:, :], d["cols"]).then_inc(s.ld_cols, 16)
            sp.dma_start(ctxT[:, :], d["ctxT"]).then_inc(s.ld_ctxT, 16)
            sp.dma_start(wb_t[:, :], d["w_b"]).then_inc(s.ld_wb, 16)
            sp.dma_start(fc1, d["fc1"]).then_inc(s.ld_fc1, 16)
            sp.dma_start(fc2, d["fc2"]).then_inc(s.ld_fc2, 16)
            sp.dma_start(w12, d["w12"]).then_inc(s.ld_w12, 16)
            sp.dma_start(w3s, d["w3s"]).then_inc(s.ld_w3s, 16)
            sp.dma_start(b12, d["b12"]).then_inc(s.ld_b12, 16)
            sp.dma_start(wd_t[:, :], d["w_d"]).then_inc(s.ld_wd, 16)
            sp.dma_start(idx[:, :, :], d["idx"]).then_inc(s.ld_idx, 16)
            if stop > 5:
                sp.wait_ge(s.y_ready, E + 1)
                sp.dma_start(w2_t, d["w_2"]).then_inc(s.ld_w2, 16)
            if stop > 2:
                sp.wait_ge(s.rep_turned, lots_till[PHASE_TILES[1][-1]])
                sp.dma_start(W3, d["w3"]).then_inc(s.ld_w3, 16)
            if stop > 7:
                sp.wait_ge(s.pv_ready, 3 * G)
                sp.dma_start(w13, d["w13"]).then_inc(s.ld_w13, 16)
                sp.dma_start(w2e, d["w2e"]).then_inc(s.ld_w2e, 16)
            if stop < 8:
                sp.wait_ge(s.x_ready, stop)
            else:
                sp.wait_ge(s.y_added, 2 * E)
            sp.dma_start(out_dram, x[:, :, :]).then_inc(s.stored, 16)
            sp.wait_ge(s.stored, 16)

        @block.gpsimd
        def _(pool):
            chain = [0]

            def link(ins):
                chain[0] += 1
                ins.then_inc(s.pool_done, 1)
                pool.wait_ge(s.pool_done, chain[0])

            pool.memset(nhalf[:, :], -0.5).then_inc(s.setup_pool, 1)
            pool.memset(REP[:, :], 0.0).then_inc(s.setup_pool, 1)
            pool.memset(VX[:, 0:4096], 0.0).then_inc(s.setup_pool, 1)
            pool.memset(ones[:, :], 1.0).then_inc(s.setup_pool, 1)
            pool.wait_ge(s.setup_pool, 4)
            pool.memset(Vaug[:, :, :, HD:HD + 1], 1.0).then_inc(s.setup_pool, 1)
            pool.wait_ge(s.ld_ctx, 16)
            pool.tensor_copy(Vaug[:, :, :, 0:HD], CTXN.rearrange("p k (h c) -> p k h c", h=H))\
                .then_inc(s.setup_pool, 1)

            def rstd_of(k):
                pool.wait_ge(s.var_ready, k + 1)
                link(pool.tensor_scalar(ve[:, 0:NT], mv[:, :, 1], EPS, None, ALU.add))
                pool.tensor_tensor(rstd[:, 0:NT], ve[:, 0:NT], nhalf[:, 0:NT], ALU.pow)\
                    .then_inc(s.rstd_ready, 1)

            nln = {1: 1, 2: 3, 3: 4, 4: 5, 5: 6, 6: 7, 7: 8, 8: 10}.get(stop, 10)
            for k in range(min(nln, 5)):
                rstd_of(k)
            if stop >= 4:
                pool.wait_ge(s.var1_ready, 1)
                link(pool.tensor_scalar(ve[:, 0:NT * NU], ve[:, 0:NT * NU], 1.0 / H1, EPS, ALU.mult, ALU.add))
                pool.tensor_tensor(rstd[:, 0:NT * NU], ve[:, 0:NT * NU], nhalf[:, 0:NT * NU], ALU.pow)\
                    .then_inc(s.rstd1_ready, 1)
            if stop >= 5:
                rstd_of(5)
            if stop >= 6:
                rstd_of(6)
                for i in range(2):
                    pool.wait_ge(s.ax_ready, i + 1)
                    pool.partition_all_reduce(qs[:, 1 + 2 * i:2 + 2 * i], qs[:, 2 * i:2 * i + 1], P, ABSMAX)\
                        .then_inc(s.ax_all, 1)
            if stop >= 7:
                for k in range(KT):
                    pool.wait_ge(s.v3_read, 2 * k + 2)
                    pool.tensor_scalar(V3[:, k, :], V3[:, k, :], CB["maskk"][:, k:k + 1], None, ALU.mult)\
                        .then_inc(s.v3_masked, 1)
                rstd_of(7)
            if stop >= 8:
                pool.wait_ge(s.proj_ready, 3)
                pool.memset(REP[:, :].bitcast(F32), 0.0).then_inc(s.setup_pool, 1)
                rstd_of(8)
                rstd_of(9)
                rstd_of(10)

        @block.scalar
        def _(act):
            def stack_lots(tile_range):
                for n, (tl, h0, nh) in enumerate(lots):
                    if tl in tile_range and n % 2:
                        act.wait_ge(s.rep_turned, n + 1)
                        stack_copy(act, n, tl, h0, nh).then_inc(s.stack_act, 1)

            def ln_out(k):
                act.wait_ge(s.xn_turned, TURNS.index(k) + 1)
                dst = zT if k == 2 else lnT
                if k in (9, 10):
                    w = CB["rms1"] if k == 9 else CB["rms2"]
                    act.activation(dst[:, :], bank(0), ACT.Copy, scale=w).then_inc(s.lnT_ready, 1)
                else:
                    act.copy(dst[:, :], bank(0)).then_inc(s.lnT_ready, 1)

            def attention(a):
                scale = SCALES[a]
                for step in range(G + 5):
                    g = step - 2
                    n_units = (UNIT[a + 1] - UNIT[a]) // G
                    for part in range(2):
                        if 0 <= g < G:
                            for u in range(part * n_units // 2, (part + 1) * n_units // 2):
                                n = UNIT[a] + g * n_units + u
                                act.wait_ge(s.st_ready, n + 1)
                                if groups(a, g) >= 2:
                                    act.wait_ge(s.pv_ready, groups(a, g) - 1)
                                width = 1024 if a < 3 or u == 0 else 512
                                act.activation(PRg[:, g % 2, u * 1024:u * 1024 + width],
                                               bank(3 + 2 * (n % 2), 2)[:, 0:width], ACT.Exp,
                                               scale=scale).then_inc(s.p_ready, 1)
                        if part == 0 and 0 <= step - 1 < G:
                            m = groups(a, step - 1)
                            gg = step - 1
                            act.wait_ge(s.m_turned, m + 1)
                            b, h0 = group_heads(a, gg)
                            act.copy(Qst[PAD:MROW, h0:h0 + 4, b * SQ:(b + 1) * SQ],
                                     bankb(2)[0:12, 0:SQ].unsqueeze(1).to_broadcast([12, 4, SQ]))\
                               .then_inc(s.mrow_ready, 1)
                    if a != 2 and 0 <= step - 3 < G:
                        m = groups(a, step - 3)
                        act.wait_ge(s.pv_ready, m + 1)
                        if ot_index(a, step - 3) >= 2:
                            act.wait_ge(s.ot_turned, ot_index(a, step - 3) - 1)
                        act.copy(OT[:, (m % 2) * SQ:(m % 2 + 1) * SQ], bank(7)[:, (m % 2) * SQ:(m % 2 + 1) * SQ])\
                            .then_inc(s.ot_ready, 1)

            def onat_out(n):
                act.wait_ge(s.onat_turned, n + 1)
                act.copy(OT[:, :], bank(0)).then_inc(s.onatT_ready, 1)

            stack_lots(PHASE_TILES[0])
            attention(0)
            onat_out(0)
            if stop >= 2:
                act.wait_ge(s.ld_cols, 16)
                ln_out(1)
                act.wait_ge(s.gate_diff, 1)
                act.activation(gt[:, :, 1], gt[:, :, 0], ACT.Exp).then_inc(s.gate_exp, 1)
                ln_out(2)
                for e in range(E):
                    for c in range(4):
                        n = 4 * e + c
                        act.wait_ge(s.h_ready, n + 1)
                        if e >= 2:
                            act.wait_ge(s.y_ready, e - 1)
                        act.activation(actT[:, e % 2, c, :], bank(c), ACT.Gelu_apprx_tanh,
                                       bias=CB["fc1_b"][:, n:n + 1]).then_inc(s.act_ready, 1)
            if stop >= 3:
                ln_out(3)
                stack_lots(PHASE_TILES[1])
                attention(1)
                onat_out(1)
            if stop >= 4:
                ln_out(4)
                act.wait_ge(s.logit_ready, 2)
                act.wait_ge(s.gate_diff, 2)
                act.activation(comb[:, :, :], lg[:, :, :], ACT.Exp, scale=-1.0).then_inc(s.gate_exp, 1)
                act.wait_ge(s.gate_diff, 3)
                act.activation(gt[:, :, 1], gt[:, :, 0], ACT.Exp).then_inc(s.gate_exp, 1)
                for t in range(NT):
                    act.wait_ge(s.hh_ready, t + 1)
                    act.activation(SL[:, t, :, :], HH[:, t, :, 0:H1], ACT.Silu).then_inc(s.silu_ready, 1)
                act.wait_ge(s.c_ready, 1)
                act.activation(SL[:, :, :, :], U[:, :, 0:NU, :], ACT.Square).then_inc(s.sq_ready, 1)
                for r in range(1, 5, 2):
                    act.wait_ge(s.z_turned, r + 1)
                    act.activation(ZT[:, r, :], bank(r), ACT.Copy, scale=CB["gcol"][:, r:r + 1])\
                        .then_inc(s.zT_act, 1)
            if stop >= 5:
                ln_out(5)
                for t in range(NT):
                    act.wait_ge(s.nm2_ready, t + 1)
                    act.activation(P2[:, t, :], bank(t), ACT.Exp, bias=qs[:, 16 + t:17 + t],
                                   accum_out=qs[:, 20 + t:21 + t]).then_inc(s.p2_ready, 1)
                    act.wait_ge(s.p2_turned, t + 1)
                    act.copy(PT2[:, t, :, :].rearrange("p k q -> p (k q)"), bank(4 + t))\
                        .then_inc(s.pt2_ready, 1)
            if stop >= 6:
                act.wait_ge(s.ld_rows, 16)
                act.activation(qs[:, 8:10], RB["clip"], ACT.Exp, scale=-1.0).then_inc(s.clip_exp, 1)
                act.wait_ge(s.xq_turned, 1)
                act.copy(xqT[:, :], bankb(0)[:, 0:T]).then_inc(s.xqT_ready, 1)
                act.wait_ge(s.scales_ready, 1)
                for c in range(3):
                    n = P if c < 2 else I2R
                    act.wait_ge(s.g2_ready, 2 * c + 1)
                    act.activation(SG[0:n, c, :], bank(c)[0:n, :], ACT.Silu, scale=qs[0:n, 28 + c:29 + c])\
                        .then_inc(s.sg_ready, 1)
            if stop >= 7:
                for r in range(8):
                    for hb in range(1, 2):
                        act.wait_ge(s.k3_ready, 2 * r + hb + 1)
                        act.activation(K3[:, r, hb * 512:(hb + 1) * 512], bank(4 + (2 * r + hb) % 4),
                                       ACT.Identity, bias=CB["bk3"][:, r:r + 1]).then_inc(s.k3_act, 1)
                ln_out(7)
                for r in range(8):
                    act.wait_ge(s.q3_ready, r + 1)
                    act.activation(Q3[DH3:P, 2 * r + 1, :], bank(4 + r % 2)[DH3:P, :], ACT.Identity,
                                   bias=CB["bq3"][DH3:P, r:r + 1]).then_inc(s.q3_act, 1)
                attention(2)
            if stop >= 8:
                ln_out(9)
                stack_lots(PHASE_TILES[2])
                attention(3)
                onat_out(2)
                ln_out(10)
                act.wait_ge(s.gate_diff, 4)
                act.activation(lg[:, :, 0:E], lg[:, :, 0:E], ACT.Exp).then_inc(s.gate_exp, 1)
                for e in range(E):
                    for c in range(2):
                        act.wait_ge(s.h_ready, 4 * E + 4 * e + c + 1)
                        if 2 * e + c >= 2:
                            act.wait_ge(s.hd_ready, E + 2 * e + c - 1)
                        act.activation(SG[:, c, :], bank(c), ACT.Silu).then_inc(s.act_ready, 1)

        @block.vector
        def _(dve):
            chain = [0]

            def link(ins):
                chain[0] += 1
                ins.then_inc(s.dve_done, 1)
                dve.wait_ge(s.dve_done, chain[0])

            told = {}

            def signal(ins, name):
                told[name] = told.get(name, 0) + 1
                ins.then_inc(S[name], 1)
                dve.wait_ge(S[name], told[name])

            def normalise(k, to=xn):
                src = xn if k == 2 else x
                for t in range(NT):
                    i = dve.bn_stats(st6[:, t, :], src[:, t, :])
                link(i)
                for t in range(NT):
                    i = dve.bn_aggr(mv[:, t, :], st6[:, t, :])
                i.then_inc(s.var_ready, 1)
                dve.wait_ge(s.rstd_ready, k + 1)
                if k == 2:
                    dve.wait_ge(s.xn_turned, 1)
                for t in range(NT):
                    i = dve.tensor_scalar(to[:, t, :], src[:, t, :], mv[:, t, 0:1], rstd[:, t:t + 1],
                                          ALU.subtract, ALU.mult)
                i.then_inc(s.xn_ready, 1)

            def rms_normalise(k):
                for t in range(NT):
                    i = dve.tensor_tensor_reduce(out=rest[:, t * P:(t + 1) * P], in0=x[:, t, :],
                                                 in1=x[:, t, :], scale=1.0 / P, scalar=0.0, op0=ALU.mult,
                                                 op1=ALU.add, accum_out=mv[:, t, 1:2])
                i.then_inc(s.var_ready, 1)
                dve.wait_ge(s.rstd_ready, k + 1)
                for t in range(NT):
                    i = dve.tensor_scalar(xn[:, t, :], x[:, t, :], rstd[:, t:t + 1], None, ALU.mult)
                i.then_inc(s.xn_ready, 1)

            def split(src, at, n):
                r = rest[:, at:at + n]
                link(dve.tensor_copy(parts[:, 0, at:at + n], src))
                link(dve.tensor_tensor(r, src, parts[:, 0, at:at + n], ALU.subtract))
                link(dve.tensor_copy(parts[:, 1, at:at + n], r))
                link(dve.tensor_tensor(r, r, parts[:, 1, at:at + n], ALU.subtract))
                link(dve.tensor_copy(parts[:, 2, at:at + n], r))

            def spread(n, at):
                kind, _, heads = tiles[n]
                if n >= 4:
                    dve.wait_ge(s.rep_turned, lots_till[n - 4])
                for j in range(NPART):
                    v = REPv[:, n % 4, 0:heads, 0:72].rearrange("p h (i j c) -> p h i j c", i=3, j=3)
                    to = v[:, :, j, :, :] if kind == "q" else v[:, :, :, j, :]
                    src = parts[:, j, at:at + heads * HD].rearrange("p (h o c) -> p h o c", h=heads, o=1)
                    i = dve.tensor_copy(to, src.to_broadcast([P, heads, 3, HD]))
                i.then_inc(s.rep_ready, 1)

            def stack_lots(tile_range):
                for n, (tl, h0, nh) in enumerate(lots):
                    if tl in tile_range and n % 2 == 0:
                        dve.wait_ge(s.rep_turned, n + 1)
                        stack_copy(dve, n, tl, h0, nh).then_inc(s.stack_dve, 1)

            def max_banks(a, g, part):
                n_banks = (MAXB[a + 1] - MAXB[a]) // G
                for u in range(part * n_banks // 2, (part + 1) * n_banks // 2):
                    n = MAXB[a] + g * n_banks + u
                    dve.wait_ge(s.smax_ready, n + 1)
                    m = mxs[:, g % 2, :, :]
                    if a < 3:
                        i = dve.tensor_reduce(m[:, u // 4, u % 4:u % 4 + 1], bank(n % 2), AX_X, ALU.max)
                    elif u == 0:
                        i = dve.tensor_reduce(m[:, 0, :], bank(n % 2).rearrange("p (h k) -> p h k", h=4),
                                              AX_X, ALU.max)
                    else:
                        i = dve.tensor_reduce(m[:, 1, 2 * u - 2:2 * u],
                                              bank(n % 2).rearrange("p (h k) -> p h k", h=2), AX_X, ALU.max)
                    i.then_inc(s.smax_read, 1)
                return MAXB[a] + (g + 1) * n_banks

            def attention(a):
                for step in range(G + 5):
                    if a != 2 and 0 <= step - 5 < G:
                        g = step - 5
                        dve.wait_ge(s.ot_turned, ot_index(a, g) + 1)
                        o = bank(2)[:, 256:512].rearrange("p (t c w) -> p t c w", t=2, c=4)
                        link(dve.reciprocal(rden[:, :, :].unsqueeze(3), o[:, :, :, HD:HD + 1]))
                        b, h0 = group_heads(a, g)
                        to = Onat[:, 2 * b:2 * b + 2, HD * h0:HD * h0 + 4 * HD].rearrange(
                            "p t (c w) -> p t c w", c=4)
                        dve.tensor_tensor(to, o[:, :, :, 0:HD],
                                          rden[:, :, :].unsqueeze(3).to_broadcast([P, 2, 4, HD]), ALU.mult)\
                            .then_inc(s.o_ready, 1)
                    if a == 2 and 0 <= step - 4 < G:
                        g = step - 4
                        dve.wait_ge(s.pv_ready, groups(2, g) + 1)
                        link(dve.reciprocal(rden3[:, :], bank(2)[:, 256:512]))
                        for c in range(4):
                            for half in range(2):
                                p0 = DH3 * (c % 2) + 32 * half
                                i = dve.tensor_tensor(
                                    OT3b[g // 4][p0:p0 + 32, 2 * (g % 4) + c // 2, :],
                                    bank(7)[p0:p0 + 32, (c // 2) * SQ:(c // 2 + 1) * SQ],
                                    rden3[32 * c:32 * c + 32, :], ALU.mult)
                        i.then_inc(s.o_ready, 1)
                    if step < G:
                        n = max_banks(a, step, 0)
                        n = max_banks(a, step, 1)
                        dve.wait_ge(s.smax_read, n)
                        m = mxs[:, step % 2, :, :]
                        to = mp[:, step % 2, :, :, :]
                        r = mr[:, :].rearrange("p (t h) -> p t h", t=2)
                        if groups(a, step) >= 2:
                            dve.wait_ge(s.m_turned, groups(a, step) - 1)
                        link(dve.tensor_scalar(to[:, :, 0, :], m, -1.0, None, ALU.mult))
                        link(dve.scalar_tensor_tensor(out=r, in0=m, scalar=-1.0, in1=to[:, :, 0, :],
                                                      op0=ALU.mult, op1=ALU.subtract))
                        link(dve.tensor_copy(to[:, :, 1, :], r))
                        dve.tensor_tensor(to[:, :, 2, :], r, to[:, :, 1, :], ALU.subtract)\
                            .then_inc(s.m_ready, 1)

            def project(n, last=True):
                dve.wait_ge(s.proj_ready, n + 1)
                i = dve.tensor_tensor(x[:, :, :], x[:, :, :],
                                      bank(1).rearrange("p (t n) -> p t n", t=NT), ALU.add)
                signal(i, 'x_ready') if last else link(i)

            def add_row(row):
                link(dve.tensor_tensor(x[:, :, :], x[:, :, :],
                                       RB[row].unsqueeze(1).to_broadcast([P, NT, P]), ALU.add))

            def one_hots(n_hot):
                link(dve.tensor_copy(i8f[:, :, :], i8[:, :, :]))
                for j in range(n_hot):
                    i = dve.tensor_tensor(oh[:, j, :, :], C["eidx"].unsqueeze(1).to_broadcast([P, NT, E]),
                                          i8f[:, :, j:j + 1].to_broadcast([P, NT, E]), ALU.is_equal)
                link(i)

            def top8(src):
                for t in range(NT):
                    i = dve.max(v8[:, t, :], src[:, t, 0:E])
                link(i)
                for t in range(NT):
                    i = dve.max_index(i8[:, t, :], v8[:, t, :], src[:, t, 0:E])
                link(i)

            def mix(j0, j1):
                for j, w in ((0, j0), (1, j1)):
                    i = dve.tensor_tensor(oh[:, j, :, :], oh[:, j, :, :],
                                          gt[:, :, w:w + 1].to_broadcast([P, NT, E]), ALU.mult)
                link(i)
                link(dve.tensor_tensor(comb[:, :, 0:E], oh[:, 0, :, :], oh[:, 1, :, :], ALU.add))

            dve.wait_ge(s.ld_const, 16)
            dve.tensor_copy(identb[:, :], C["ident"]).then_inc(s.setup_dve, 1)
            dve.tensor_copy(maskb[:, 0, :], C["mask_n"]).then_inc(s.setup_dve, 1)
            dve.tensor_copy(maskb[:, 1, :], C["mask_t"]).then_inc(s.setup_dve, 1)
            dve.wait_ge(s.ld_x, 16)
            normalise(0)
            dve.wait_ge(s.xn_ready, 1)
            dve.wait_ge(s.ld_ctx, 16)
            dve.wait_ge(s.setup_pool, 2)
            tile_no = 0
            xn_f = xn[:, :, :].rearrange("p t n -> p (t n)")
            for b in range(B):
                split(CTXN[:, 4 * b:4 * b + 4, :].rearrange("p k n -> p (k n)"), 0, T)
                for t in range(4):
                    spread(tile_no, t * P)
                    tile_no += 1
                    if t >= 2:
                        stack_lots([tile_no - 3])
                split(xn_f[:, b * SQ:(b + 1) * SQ], 0, SQ)
                for t in range(2):
                    stack_lots([tile_no - 2])
                    spread(tile_no, t * P)
                    tile_no += 1
                stack_lots([tile_no - 2, tile_no - 1])
            dve.wait_ge(s.ld_rows, 16)
            add_row("bo0")
            attention(0)
            project(0)

            if stop >= 2:
                normalise(1)
                dve.wait_ge(s.xn_ready, 2)
                normalise(2)
                dve.wait_ge(s.ld_cols, 16)
                dve.wait_ge(s.logit_ready, 1)
                link(dve.tensor_copy(lg[:, :, 0:E], bank(2)[:, 0:NT * E].rearrange("p (t e) -> p t e", t=NT)))
                top8(lg)
                signal(dve.tensor_tensor(gt[:, :, 0], v8[:, :, 1], v8[:, :, 0], ALU.subtract), 'gate_diff')
                one_hots(2)
                dve.wait_ge(s.gate_exp, 1)
                link(dve.tensor_scalar(gt[:, :, 2], gt[:, :, 1], 1.0, None, ALU.add))
                link(dve.reciprocal(gt[:, :, 2], gt[:, :, 2]))
                link(dve.tensor_tensor(gt[:, :, 1], gt[:, :, 1], gt[:, :, 2], ALU.mult))
                mix(2, 1)
                signal(dve.tensor_tensor(comb[:, :, 0:E], comb[:, :, 0:E],
                                       RB["alpha"].unsqueeze(1).to_broadcast([P, NT, E]), ALU.mult), 'comb_ready')
                dve.wait_ge(s.lnT_ready, 2)
                for e in range(E):
                    if e == 2:
                        dve.wait_ge(s.comb_turned, 1)
                        dve.tensor_copy(combT[0:E, :], bank(6)[0:E, :]).then_inc(s.combT_ready, 1)
                    if e >= 2:
                        dve.wait_ge(s.h_ready, 4 * (e - 1))
                    dve.tensor_scalar(hdT[:, e % 2, :], zT[:, :], CB["ln0_w"][:, e:e + 1],
                                      CB["ln0_b"][:, e:e + 1], ALU.mult, ALU.add).then_inc(s.hd_ready, 1)
                    if e >= 1:
                        add_expert(dve, e - 1, e - 1, 4)
                add_expert(dve, E - 1, E - 1, 4)
                dve.wait_ge(s.y_ready, E + 1)
                dve.wait_ge(s.y_added, E)
                signal(dve.tensor_tensor(x[:, :, :], x[:, :, :], bank(7).rearrange("p (t n) -> p t n", t=NT),
                                       ALU.add), 'x_ready')

            if stop >= 3:
                normalise(3)
                tile_no = 12
                dve.wait_ge(s.ld_wb, 16)
                for b in range(B):
                    for j in range(4):
                        t = 4 * b + j
                        dve.wait_ge(s.kv1_ready, t + 1)
                        kv = bank(t % 2)
                        dve.tensor_tensor(Vaug[:, t, :, 0:HD], kv[:, P:2 * P].rearrange("p (h c) -> p h c", h=H),
                                          RB["bv1"].rearrange("p (h c) -> p h c", h=H), ALU.add)
                        signal(dve.tensor_tensor(zT[:, j * P:(j + 1) * P], kv[:, 0:P], RB["bk1"], ALU.add), 'kv1_read')
                    split(zT[:, :], 0, T)
                    for t in range(4):
                        spread(tile_no, t * P)
                        tile_no += 1
                        if t >= 2:
                            stack_lots([tile_no - 3])
                    if b == 0:
                        dve.wait_ge(s.q2_ready, 1)
                        link(dve.tensor_tensor(Onat[:, :, :], bank(2).rearrange("p (t n) -> p t n", t=NT),
                                               RB["bq1"].unsqueeze(1).to_broadcast([P, NT, P]), ALU.add))
                    split(Onat[:, 2 * b:2 * b + 2, :].rearrange("p t n -> p (t n)"), 0, SQ)
                    for t in range(2):
                        stack_lots([tile_no - 2])
                        spread(tile_no, t * P)
                        tile_no += 1
                    stack_lots([tile_no - 2, tile_no - 1])
                add_row("bo1")
                attention(1)
                project(1)

            if stop >= 4:
                normalise(4)
                dve.wait_ge(s.ld_idx, 16)
                link(dve.tensor_copy(idf[:, 0:2, :], idx[:, :, :]))
                for j, n in ((0, B), (1, SQ)):
                    i = dve.tensor_scalar(idf[:, 2 + j, :], idf[:, j, :], 0.0, float(n), ALU.is_lt, ALU.mult)
                link(i)
                link(dve.tensor_tensor(idf[:, 0:2, :], idf[:, 0:2, :], idf[:, 2:4, :], ALU.add))
                for b in range(B):
                    i = dve.tensor_scalar(idf[:, 2 + b, :], idf[:, 0, :], float(b), None, ALU.is_equal)
                link(i)
                for t in range(NT):
                    i = dve.scalar_tensor_tensor(out=eqm[:, t, :], in0=idf[:, 1, :],
                                                 scalar=C["tokpos"][:, t % 2:t % 2 + 1],
                                                 in1=idf[:, 2 + t // 2, :], op0=ALU.is_equal, op1=ALU.mult)
                link(i)
                link(dve.tensor_reduce(tmask[:, :], eqm[:, :, :], AX_X, ALU.max))
                dve.wait_ge(s.logit_ready, 2)
                signal(dve.tensor_tensor(lg[:, :, :], bank(7)[:, 0:NT * NU].rearrange("p (t e) -> p t e", t=NT),
                                       RB["gb"].unsqueeze(1).to_broadcast([P, NT, NU]), ALU.add), 'gate_diff')
                dve.wait_ge(s.gate_exp, 2)
                link(dve.tensor_scalar(comb[:, :, :], comb[:, :, :], 1.0, None, ALU.add))
                link(dve.reciprocal(lg[:, :, :], comb[:, :, :]))
                link(dve.tensor_tensor(comb[:, :, 0:E], lg[:, :, 0:E],
                                       RB["ebias"].unsqueeze(1).to_broadcast([P, NT, E]), ALU.add))
                top8(comb)
                one_hots(1)
                link(dve.tensor_tensor(oh[:, 1, :, :], oh[:, 0, :, :], lg[:, :, 0:E], ALU.mult))
                link(dve.reduce_sum(gt[:, :, 3:4], oh[:, 1, :, :], AX_X))
                signal(dve.tensor_tensor(gt[:, :, 0], gt[:, :, 3], lg[:, :, E], ALU.subtract), 'gate_diff')
                dve.wait_ge(s.gate_exp, 3)
                link(dve.tensor_scalar(gt[:, :, 2], gt[:, :, 1], 1.0, None, ALU.add))
                link(dve.reciprocal(gt[:, :, 2], gt[:, :, 2]))
                link(dve.tensor_tensor(gt[:, :, 1], gt[:, :, 1], gt[:, :, 2], ALU.mult))
                link(dve.tensor_scalar(gt[:, :, 2], gt[:, :, 2], -1.0, None, ALU.add))
                dve.tensor_tensor(gt[:, :, 2], gt[:, :, 2], tmask[:, :], ALU.mult)
                link(dve.tensor_tensor(gt[:, :, 1], gt[:, :, 1], tmask[:, :], ALU.mult))
                link(dve.tensor_scalar(comb[:, :, E], gt[:, :, 2], 1.0, None, ALU.add))
                signal(dve.tensor_tensor(comb[:, :, 0:E], oh[:, 0, :, :],
                                       gt[:, :, 1:2].to_broadcast([P, NT, E]), ALU.mult), 'comb_ready')
                dve.memset(U[:, :, NU, :], 0.0)
                for t in range(NT):
                    dve.wait_ge(s.u_ready, t + 1)
                    dve.tensor_tensor(HH[:, t, :, :].rearrange("p u n -> p (u n)"),
                                      bank(3 * (t % 2), 3)[:, 0:NU * P], b12, ALU.add)\
                        .then_inc(s.hh_ready, 1)
                    if t >= 1:
                        dve.wait_ge(s.silu_ready, t)
                        dve.tensor_tensor(U[:, t - 1, 0:NU, :], SL[:, t - 1, :, :], HH[:, t - 1, :, H1:P],
                                          ALU.mult)
                dve.wait_ge(s.silu_ready, NT)
                link(dve.tensor_tensor(U[:, NT - 1, 0:NU, :], SL[:, NT - 1, :, :], HH[:, NT - 1, :, H1:P],
                                       ALU.mult))
                m9 = ve[:, 0:NT * NU].rearrange("p (t u) -> p t u", t=NT)
                link(dve.tensor_reduce(m9, U[:, :, 0:NU, :], AX_X, ALU.add))
                link(dve.tensor_scalar(m9, m9, 1.0 / H1, None, ALU.mult))
                for t in range(NT):
                    i = dve.tensor_tensor(U[:, t, 0:NU, :], U[:, t, 0:NU, :],
                                          m9[:, t, :].unsqueeze(2).to_broadcast([P, NU, H1]), ALU.subtract)
                i.then_inc(s.c_ready, 1)
                dve.wait_ge(s.c_ready, 1)
                dve.wait_ge(s.sq_ready, 1)
                dve.tensor_reduce(m9, SL[:, :, :, :], AX_X, ALU.add).then_inc(s.var1_ready, 1)
                dve.wait_ge(s.comb_turned, 2)
                dve.tensor_copy(combT[:, :], bank(6)[0:NU, :]).then_inc(s.combT_ready, 1)
                dve.wait_ge(s.b9_ready, 1)
                dve.tensor_tensor(b9s[:, :], bank(7)[0:NU, 0:P], CB["b9"][0:NU, :], ALU.add).then_inc(s.b9_read, 1)
                dve.wait_ge(s.rstd1_ready, 1)
                r9 = rstd[:, 0:NT * NU].rearrange("p (t u) -> p t u", t=NT)
                link(dve.tensor_tensor(r9, r9, comb[:, :, :], ALU.mult))
                for t in range(NT):
                    i = dve.tensor_tensor(U[:, t, 0:NU, :], U[:, t, 0:NU, :],
                                          r9[:, t, :].unsqueeze(2).to_broadcast([P, NU, H1]), ALU.mult)
                i.then_inc(s.z_ready, 1)
                for r in range(0, 5, 2):
                    dve.wait_ge(s.z_turned, r + 1)
                    dve.tensor_scalar(ZT[:, r, :], bank(r), CB["gcol"][:, r:r + 1], None, ALU.mult)\
                        .then_inc(s.zT_dve, 1)
                dve.wait_ge(s.y_ready, E + 2)
                signal(dve.tensor_tensor(x[:, :, :], x[:, :, :], bank(5).rearrange("p (t n) -> p t n", t=NT),
                                       ALU.add), 'x_ready')

            if stop >= 5:
                normalise(5)
                for n in range(2):
                    dve.wait_ge(s.kv2_ready, n + 1)
                    dve.tensor_copy(KT2[:, n * 512:(n + 1) * 512], bank(6 + n)).then_inc(s.kv2_read, 1)
                for n in range(2):
                    dve.wait_ge(s.kv2_ready, n + 3)
                    dve.tensor_copy(V2[:, 4 * n:4 * n + 4, :].rearrange("p k n -> p (k n)"), bank(6 + n))\
                        .then_inc(s.kv2_read, 1)
                dve.wait_ge(s.q2_ready, 2)
                dve.tensor_copy(rest[:, :], bank(1)).then_inc(s.q2_read, 1)
                for t in range(NT):
                    dve.wait_ge(s.s2_ready, t + 1)
                    dve.tensor_reduce(qs[:, 16 + t:17 + t], bank(t), AX_X, ALU.max, negate=True)\
                        .then_inc(s.nm2_ready, 1)
                dve.wait_ge(s.p2_ready, NT)
                link(dve.reciprocal(qs[:, 24:28], qs[:, 20:24]))
                dve.wait_ge(s.y_ready, E + 3)
                for t in range(NT):
                    i = dve.scalar_tensor_tensor(out=x[:, t, :], in0=bank(0)[:, t * P:(t + 1) * P],
                                                 scalar=qs[:, 24 + t:25 + t], in1=x[:, t, :],
                                                 op0=ALU.mult, op1=ALU.add)
                signal(i, 'x_ready')

            def quantise(dst, src, inv, tmp):
                link(dve.tensor_scalar(tmp, src, inv, ROUND, ALU.mult, ALU.add))
                link(dve.tensor_scalar(tmp, tmp, -ROUND, QMAX, ALU.add, ALU.min))
                return dve.tensor_scalar(dst, tmp, -QMAX - 1.0, None, ALU.max)

            if stop >= 6:
                dve.wait_ge(s.ld_w2, 16)
                for m, name in enumerate(("gate2", "up2")):
                    i = dve.tensor_reduce(qs[:, 32 + 3 * m:35 + 3 * m],
                                          WD2[name].rearrange("p (c n) -> p c n", c=3), AX_X, ALU.max,
                                          apply_absolute_value=True)
                i = dve.tensor_reduce(qs[:, 38:39], WD2["down2"], AX_X, ALU.max, apply_absolute_value=True)
                link(i)
                link(dve.tensor_scalar(qs[:, 32:39], qs[:, 32:39], 1.0 / QMAX, None, ALU.mult))
                link(dve.reciprocal(qs[:, 40:47], qs[:, 32:39]))
                for m, name in enumerate(("gate2", "up2")):
                    for c in range(3):
                        link(quantise(wq2i[:, m, c, :], WD2[name][:, c * P:(c + 1) * P],
                                      qs[:, 40 + 3 * m + c:41 + 3 * m + c], h2T[:, 0, 0:P]))
                quantise(wd2i[:, :], WD2["down2"], qs[:, 46:47], h2T[:, 0, 0:I2]).then_inc(s.wq_ready, 1)
                for n in range(3):
                    dve.wait_ge(s.wq_turned, n + 1)
                    if n < 2:
                        i = dve.tensor_copy(wgT[:, n, :, :].rearrange("p c n -> p (c n)"), bankb(1 + n)[:, 0:3 * P])
                    else:
                        dve.tensor_copy(wdT[:, 0:2, :].rearrange("p c n -> p (c n)"), bankb(3)[:, 0:2 * P])
                        i = dve.tensor_copy(wdT[0:I2R, 2, :], bankb(3)[0:I2R, 2 * P:3 * P])
                    i.then_inc(s.wq_read, 1)
                dve.wait_ge(s.clip_exp, 1)
                link(dve.tensor_scalar(qs[:, 8:10], qs[:, 8:10], 1.0, None, ALU.add))
                link(dve.reciprocal(qs[:, 8:10], qs[:, 8:10]))
                link(dve.tensor_scalar(qs[:, 8:10], qs[:, 8:10], 1.0 / QMAX, None, ALU.mult))
                normalise(6)
                dve.wait_ge(s.xn_ready, 7)
                dve.tensor_reduce(qs[:, 0:1], xn_f, AX_X, ALU.max, apply_absolute_value=True)\
                    .then_inc(s.ax_ready, 1)
                dve.wait_ge(s.ax_all, 1)
                link(dve.tensor_tensor(qs[:, 4:5], qs[:, 1:2], qs[:, 8:9], ALU.mult))
                link(dve.reciprocal(qs[:, 5:6], qs[:, 4:5]))
                quantise(xqi[:, :, :].rearrange("p t n -> p (t n)"), xn_f, qs[:, 5:6], rest[:, :])\
                    .then_inc(s.xq_ready, 1)
                link(dve.tensor_scalar(qs[:, 28:31], qs[:, 32:35], qs[:, 4:5], None, ALU.mult))
                dve.memset(h2T[:, 2, :], 0.0)
                signal(dve.tensor_scalar(qs[:, 12:15], qs[:, 35:38], qs[:, 4:5], None, ALU.mult), 'scales_ready')
                for c in range(3):
                    n = P if c < 2 else I2R
                    dve.wait_ge(s.g2_ready, 2 * c + 2)
                    dve.wait_ge(s.sg_ready, c + 1)
                    i = dve.scalar_tensor_tensor(out=h2T[0:n, c, :], in0=bank(3 + c)[0:n, :],
                                                 scalar=qs[0:n, 12 + c:13 + c], in1=SG[0:n, c, :],
                                                 op0=ALU.mult, op1=ALU.mult)
                link(i)
                h2f = h2T.rearrange("p c t -> p (c t)")
                dve.tensor_reduce(qs[:, 2:3], h2f, AX_X, ALU.max, apply_absolute_value=True)\
                    .then_inc(s.ax_ready, 1)
                dve.wait_ge(s.ax_all, 2)
                link(dve.tensor_tensor(qs[:, 6:7], qs[:, 3:4], qs[:, 9:10], ALU.mult))
                link(dve.reciprocal(qs[:, 7:8], qs[:, 6:7]))
                quantise(hqT[:, :, :].rearrange("p c t -> p (c t)"), h2f, qs[:, 7:8], h2f)\
                    .then_inc(s.hq_ready, 1)
                link(dve.tensor_tensor(qs[:, 10:11], qs[:, 38:39], qs[:, 6:7], ALU.mult))
                dve.wait_ge(s.y2_ready, 1)
                dve.tensor_scalar(rest[:, :], bank(6), qs[:, 10:11], None, ALU.mult).then_inc(s.y2_read, 1)
                dve.wait_ge(s.y2_turned, 1)
                signal(dve.tensor_tensor(x[:, :, :], x[:, :, :], bank(7).rearrange("p (t n) -> p t n", t=NT),
                                       ALU.add), 'x_ready')

            if stop >= 7:
                for h in range(H):
                    p0 = DH3 * ((h + 1) % 2)
                    i = dve.memset(Q3[p0:p0 + DH3, h, :], 0.0)
                link(i)
                for r in range(8):
                    dve.wait_ge(s.k3_ready, 2 * r + 1)
                    dve.tensor_scalar(K3[:, r, 0:512], bank(4 + (2 * r) % 4), CB["bk3"][:, r:r + 1], None,
                                      ALU.add).then_inc(s.k3_dve, 1)
                for n in range(2 * KT):
                    k, half = n // 2, n % 2
                    dve.wait_ge(s.v3_ready, n + 1)
                    dve.tensor_tensor(V3[:, k, half * 512:(half + 1) * 512], bank(4 + n % 4),
                                      RB["bv3"][:, half * 512:(half + 1) * 512], ALU.add)\
                        .then_inc(s.v3_read, 1)
                normalise(7)
                for r in range(8):
                    dve.wait_ge(s.q3_ready, r + 1)
                    dve.tensor_scalar(Q3[0:DH3, 2 * r, :], bank(4 + r % 2)[0:DH3, :], CB["bq3"][0:DH3, r:r + 1],
                                      None, ALU.add).then_inc(s.q3_dve, 1)
                add_row("bo3")
                attention(2)
                dve.wait_ge(s.proj_ready, 3)
                signal(dve.tensor_tensor(x[:, :, :], x[:, :, :], bank(1).rearrange("p (t n) -> p t n", t=NT),
                                       ALU.add), 'x_ready')

            if stop >= 8:
                x_f = x[:, :, :].rearrange("p t n -> p (t n)")
                dve.tensor_copy(zT, x_f)
                normalise(8, x)
                dve.wait_ge(s.xn_ready, 9)
                rms_normalise(9)
                dve.memset(V4[:, :, :, :], 0.0)
                link(dve.memset(rden3[:, 0:1], 0.0))
                dve.memset(V4[:, :, :, HD:HD + 1], 1.0)
                dve.wait_ge(s.setup_pool, 7)
                cos4 = C["cos"].rearrange("p (t c) -> p t c", t=NT)
                sin4 = C["sin"].rearrange("p (t c) -> p t c", t=NT)
                for pair in range(2):
                    dve.wait_ge(s.qkv_ready, pair + 1)
                    src = bank(1 + pair)[:, 0:384].rearrange("p (t n) -> p t n", t=2)
                    for j in range(2):
                        t = 2 * pair + j
                        v = src[:, j, 0:160].rearrange("p (h c) -> p h c", c=HD)
                        a1 = qrope[:, t, :].rearrange("p (h c) -> p h c", c=HD)
                        a2 = qrot[:, t, :].rearrange("p (h c) -> p h c", c=HD)
                        cb = cos4[:, t, :].unsqueeze(1).to_broadcast([P, 20, HD])
                        sb_ = sin4[:, t, :].unsqueeze(1).to_broadcast([P, 20, HD])
                        dve.tensor_tensor(a1, v, cb, ALU.mult)
                        dve.tensor_tensor(a2[:, :, 0:4], v[:, :, 4:8], sb_[:, :, 0:4], ALU.mult)
                        dve.tensor_tensor(a2[:, :, 4:8], v[:, :, 0:4], sb_[:, :, 4:8], ALU.mult)
                        i = dve.tensor_copy(V4[:, t, :, 0:HD],
                                            src[:, j, 160:192].rearrange("p (h c) -> p h c", c=HD))
                signal(i, 'v4_ready')
                link(dve.tensor_tensor(qrope, qrope, qrot, ALU.add))
                tile_no = 24
                for t in range(NT):
                    at = 160 * (t % 3)
                    split(qrope[:, t, :], at, 160)
                    spread(tile_no, at + P)
                    spread(tile_no + 1, at)
                    tile_no += 2
                    if t >= 1:
                        stack_lots([tile_no - 4, tile_no - 3])
                stack_lots([tile_no - 2, tile_no - 1])
                attention(3)
                project(3, last=False)
                rms_normalise(10)
                dve.wait_ge(s.xn_ready, 11)
                link(dve.tensor_tensor(x_f, x_f, zT, ALU.add))
                dve.wait_ge(s.logit_ready, 3)
                link(dve.tensor_copy(lg[:, :, 0:E], bank(2)[:, 0:NT * E].rearrange("p (t e) -> p t e", t=NT)))
                link(dve.tensor_reduce(gt[:, :, 0:1], lg[:, :, 0:E], AX_X, ALU.max))
                signal(dve.tensor_tensor(lg[:, :, 0:E], lg[:, :, 0:E], gt[:, :, 0:1].to_broadcast([P, NT, E]),
                                       ALU.subtract), 'gate_diff')
                dve.wait_ge(s.gate_exp, 4)
                link(dve.reduce_sum(gt[:, :, 1:2], lg[:, :, 0:E], AX_X))
                link(dve.reciprocal(gt[:, :, 1:2], gt[:, :, 1:2]))
                link(dve.tensor_tensor(lg[:, :, 0:E], lg[:, :, 0:E], gt[:, :, 1:2].to_broadcast([P, NT, E]),
                                       ALU.mult))
                top8(lg)
                one_hots(2)
                link(dve.tensor_tensor(gt[:, :, 0], v8[:, :, 0], v8[:, :, 1], ALU.add))
                link(dve.reciprocal(gt[:, :, 0], gt[:, :, 0]))
                link(dve.tensor_tensor(gt[:, :, 1:3], v8[:, :, 0:2], gt[:, :, 0:1].to_broadcast([P, NT, 2]),
                                       ALU.mult))
                mix(1, 2)
                for e in range(E):
                    for c in range(2):
                        dve.wait_ge(s.act_ready, 4 * E + 2 * e + c + 1)
                        dve.wait_ge(s.h_ready, 4 * E + 4 * e + 2 + c + 1)
                        if e >= 2:
                            dve.wait_ge(s.y_ready, E + 3 + e - 1)
                        dve.tensor_tensor(actT[:, e % 2, c, :], SG[:, c, :], bank(2 + c), ALU.mult)\
                            .then_inc(s.hd_ready, 1)
                    if e >= 1:
                        add_expert(dve, e - 1, E + e - 1, 4, E + 3)
                add_expert(dve, E - 1, 2 * E - 1, 4, E + 3)

        @block.tensor
        def _(pe):
            ident = C["ident"]

            def turn_xn(k):
                pe.wait_ge(s.xn_ready, k + 1)
                for t in range(NT):
                    i = pe.transpose(bank(0)[:, t * P:(t + 1) * P], xn[:, t, :], ident)
                i.then_inc(s.xn_turned, 1)

            def stack(tile_range):
                for n, (tl, h0, nh) in enumerate(lots):
                    if tl not in tile_range:
                        continue
                    pe.wait_ge(s.rep_ready, tl + 1)
                    if n >= 4:
                        pe.wait_ge(s.stack_act if n % 2 else s.stack_dve, (n - 4) // 2 + 1)
                    for h in range(nh):
                        i = pe.transpose(bankb(3 + n % 4)[0:PAD, h * P:(h + 1) * P],
                                         REPv[:, tl % 4, h0 + h, :], identb[:, :])
                    i.then_inc(s.rep_turned, 1)

            def scores_max(a, g, part):
                b, h0 = group_heads(a, g)
                n_banks = (MAXB[a + 1] - MAXB[a]) // G
                for u in range(part * n_banks // 2, (part + 1) * n_banks // 2):
                    n = MAXB[a] + g * n_banks + u
                    if n >= 2:
                        pe.wait_ge(s.smax_read, n - 1)
                    if a < 2:
                        q0, h = b * SQ + (u // 4) * P, h0 + u % 4
                        i = pe.matmul(bank(n % 2), Qst[0:PAD, h, q0:q0 + P], Kst[0:PAD, h, b * SK:(b + 1) * SK],
                                      start=True, stop=True)
                    elif a == 2:
                        q0, h = b * SQ + (u // 4) * P, h0 + u % 4
                        i = pe.matmul(bank(n % 2), Q3[:, h, q0:q0 + P], K3[:, h // 2, b * SK:(b + 1) * SK],
                                      start=True, stop=True)
                    elif u == 0:
                        for c in range(4):
                            o = bank(n % 2)[:, c * P:(c + 1) * P]
                            pe.matmul(o, Qst[0:PAD, h0 + c, b * SQ:b * SQ + P], K4[0:PAD, h0 // 4, b * SQ:b * SQ + P],
                                      start=True, stop=False)
                            i = pe.matmul(o, identb[:, :], maskb[:, 0, :], start=False, stop=True)
                    else:
                        for c in range(2):
                            h = h0 + 2 * (u - 1) + c
                            o = bank(n % 2)[:, c * SQ:(c + 1) * SQ]
                            pe.matmul(o, Qst[0:PAD, h, b * SQ + P:(b + 1) * SQ], K4[0:PAD, h0 // 4, b * SQ:(b + 1) * SQ],
                                      start=True, stop=False)
                            i = pe.matmul(o[:, P:SQ], identb[:, :], maskb[:, 0, :], start=False, stop=True)
                    i.then_inc(s.smax_ready, 1)

            def scores_exp(a, g, part):
                b, h0 = group_heads(a, g)
                n_units = (UNIT[a + 1] - UNIT[a]) // G
                pe.wait_ge(s.mrow_ready, groups(a, g) + 1)
                for u in range(part * n_units // 2, (part + 1) * n_units // 2):
                    n = UNIT[a] + g * n_units + u
                    if n >= 2:
                        pe.wait_ge(s.p_ready, n - 1)
                    o = bank(3 + 2 * (n % 2), 2)
                    if a < 3:
                        h = h0 + u
                        for k in range(4):
                            k0 = b * SK + k * P
                            ok = o[:, k * SQ:(k + 1) * SQ]
                            if a < 2:
                                i = pe.matmul(ok, Kst[0:MROW, h, k0:k0 + P], Qst[0:MROW, h, b * SQ:(b + 1) * SQ],
                                              start=True, stop=True)
                            else:
                                pe.matmul(ok, K3[:, h // 2, k0:k0 + P], Q3[:, h, b * SQ:(b + 1) * SQ],
                                          start=True, stop=False)
                                i = pe.matmul(ok, onesel[0:MROW, u, :], Qst[0:MROW, h, b * SQ:(b + 1) * SQ],
                                              start=False, stop=True)
                    elif u == 0:
                        for c in range(0, 4, 2):
                            ok = o[:, c * SQ:(c + 2) * SQ].rearrange("p (c q) -> p c q", c=2)
                            pe.matmul(ok, K4[0:PAD, h0 // 4, b * SQ:b * SQ + P],
                                      Qst[0:PAD, h0 + c:h0 + c + 2, b * SQ:(b + 1) * SQ], start=True, stop=False)
                            for j in range(2):
                                pe.matmul(ok[:, j, :], onesel[0:MROW, c + j, :],
                                          Qst[0:MROW, h0 + c + j, b * SQ:(b + 1) * SQ], start=False, stop=False)
                            i = pe.matmul(ok[:, :, 0:P], identb[:, :],
                                          maskb[:, 1, :].unsqueeze(1).to_broadcast([P, 2, P]),
                                          start=False, stop=True)
                    else:
                        ok = o[:, 0:512].rearrange("p (c q) -> p c q", c=4)
                        pe.matmul(ok, K4[0:PAD, h0 // 4, b * SQ + P:(b + 1) * SQ],
                                  Qst[0:PAD, h0:h0 + 4, b * SQ + P:(b + 1) * SQ], start=True, stop=False)
                        for j in range(4):
                            pe.matmul(ok[:, j, :], onesel[0:MROW, j, :],
                                      Qst[0:MROW, h0 + j, b * SQ + P:(b + 1) * SQ], start=False, stop=False)
                        i = pe.matmul(ok, identb[:, :], maskb[:, 1, :].unsqueeze(1).to_broadcast([P, 4, P]),
                                      start=False, stop=True)
                    i.then_inc(s.st_ready, 1)

            def turn_max(a, g):
                n = groups(a, g)
                pe.wait_ge(s.m_ready, n + 1)
                if n >= 1:
                    pe.wait_ge(s.mrow_ready, n)
                back = g - 4 if a != 2 else g - 3
                if n and (back >= 0 or g == 0):
                    pe.wait_ge(s.o_ready, a * G + back + 1 if g else a * G)
                for t in range(2):
                    i = pe.transpose(bankb(2)[0:12, t * P:(t + 1) * P],
                                     mp[:, g % 2, t, :, :].rearrange("p i h -> p (i h)"), identb[:, :])
                i.then_inc(s.m_turned, 1)

            def probs_values(a, g):
                n = groups(a, g)
                b, h0 = group_heads(a, g)
                pe.wait_ge(s.p_ready, UNIT[a] + (g + 1) * ((UNIT[a + 1] - UNIT[a]) // G))
                pr = PRg[:, g % 2, :]
                if a != 2:
                    if ot_index(a, g) >= 1:
                        pe.wait_ge(s.ot_ready, ot_index(a, g))
                    o = bank(7)[:, (n % 2) * SQ:(n % 2 + 1) * SQ]
                    if a == 3:
                        for c in range(4):
                            pe.matmul(o[32 * c:32 * c + VW, :], V4[:, 2 * b, h0 // 4, :], pr[:, c * SQ:(c + 1) * SQ],
                                      start=True, stop=False)
                        for c in range(4):
                            i = pe.matmul(o[32 * c:32 * c + VW, P:SQ], V4[:, 2 * b + 1, h0 // 4, :],
                                          pr[:, 1024 + c * P:1024 + (c + 1) * P], start=False, stop=True)
                    else:
                        for k in range(4):
                            for c in range(4):
                                i = pe.matmul(o[32 * c:32 * c + VW, :], Vaug[:, 4 * b + k, h0 + c, :],
                                              pr[:, c * 1024 + k * SQ:c * 1024 + (k + 1) * SQ],
                                              start=(k == 0), stop=(k == 3))
                else:
                    if g:
                        pe.wait_ge(s.o_ready, 2 * G + g)
                    pe.wait_ge(s.mrow_ready, min(n + 3, 3 * G))
                    for r in range(2):
                        for k in range(4):
                            for c in range(2):
                                pe.matmul(bank(7)[DH3 * c:DH3 * (c + 1), r * SQ:(r + 1) * SQ],
                                          V3[:, 4 * b + k, DH3 * (h0 + 2 * r + c):DH3 * (h0 + 2 * r + c + 1)],
                                          pr[:, (2 * r + c) * 1024 + k * SQ:(2 * r + c) * 1024 + (k + 1) * SQ],
                                          start=(k == 0), stop=(k == 3))
                    for k in range(4):
                        for c in range(4):
                            i = pe.matmul(bank(2)[32 * c:32 * c + 32, 256:512], ones[:, :],
                                          pr[:, c * 1024 + k * SQ:c * 1024 + (k + 1) * SQ],
                                          start=(k == 0), stop=(k == 3))
                i.then_inc(s.pv_ready, 1)

            def turn_out(a, g):
                n = ot_index(a, g)
                pe.wait_ge(s.ot_ready, n + 1)
                pe.wait_ge(s.mrow_ready, min(groups(a, g) + 4, (a + 1) * G))
                if g:
                    pe.wait_ge(s.o_ready, groups(a, g))
                m = groups(a, g) % 2
                for t in range(2):
                    i = pe.transpose(bank(2)[:, 256 + t * P:256 + (t + 1) * P],
                                     OT[:, m * SQ + t * P:m * SQ + (t + 1) * P], ident)
                i.then_inc(s.ot_turned, 1)

            def attention(a):
                for step in range(G + 4):
                    for part in range(2):
                        if step < G:
                            scores_max(a, step, part)
                        if 0 <= step - 2 < G:
                            scores_exp(a, step - 2, part)
                        if part == 0 and 0 <= step - 1 < G:
                            turn_max(a, step - 1)
                    if 0 <= step - 3 < G:
                        probs_values(a, step - 3)
                    if a != 2 and 0 <= step - 4 < G:
                        turn_out(a, step - 4)

            def project(n, a, w):
                pe.wait_ge(s.o_ready, (a + 1) * G)
                for t in range(NT):
                    i = pe.transpose(bank(0)[:, t * P:(t + 1) * P], Onat[:, t, :], ident)
                i.then_inc(s.onat_turned, 1)
                pe.wait_ge(s.onatT_ready, min(n, 2) + 1)
                for t in range(NT):
                    i = pe.matmul(bank(1)[:, t * P:(t + 1) * P], OT[:, t * P:(t + 1) * P], w, start=True, stop=True)
                i.then_inc(s.proj_ready, 1)

            def project3():
                pe.wait_ge(s.o_ready, 3 * G)
                for t in range(NT):
                    for r in range(8):
                        i = pe.matmul(bank(1)[:, t * P:(t + 1) * P],
                                      OT3b[t // 2][:, r, (t % 2) * P:(t % 2 + 1) * P],
                                      WD["wo3"][:, r * P:(r + 1) * P], start=(r == 0), stop=(r == 7))
                i.then_inc(s.proj_ready, 1)

            pe.wait_ge(s.setup_dve, 3)
            stack(PHASE_TILES[0])
            stacked(pe, PHASE_TILES[0][-1])
            pe.wait_ge(s.ld_sel, 32)
            pe.wait_ge(s.setup_pool, 6)
            attention(0)
            pe.wait_ge(s.ld_wa, 16)
            project(0, 0, WA["wo0"])

            if stop >= 2:
                turn_xn(1)
                pe.wait_ge(s.lnT_ready, 1)
                for t in range(NT):
                    i = pe.matmul(bank(2)[:, t * E:(t + 1) * E], lnT[:, t * P:(t + 1) * P], WA["wg0"],
                                  start=True, stop=True)
                i.then_inc(s.logit_ready, 1)
                turn_xn(2)
                pe.wait_ge(s.ld_cols, 16)
                pe.wait_ge(s.ld_fc1, 16)
                pe.wait_ge(s.ld_fc2, 16)
                pe.wait_ge(s.lnT_ready, 2)

                def expert_up(e):
                    pe.wait_ge(s.hd_ready, e + 1)
                    for c in range(4):
                        if e:
                            pe.wait_ge(s.act_ready, 4 * (e - 1) + c + 1)
                        pe.matmul(bank(c), fc1[:, e, c * P:(c + 1) * P], hdT[:, e % 2, :], start=True, stop=True)\
                            .then_inc(s.h_ready, 1)

                def expert_down(e):
                    pe.wait_ge(s.act_ready, 4 * e + 4)
                    if e >= 2:
                        pe.wait_ge(s.y_added, e - 1)
                    for t in range(NT):
                        for c in range(4):
                            i = pe.matmul(bank(4 + e % 2)[:, t * P:(t + 1) * P], actT[:, e % 2, c, t * P:(t + 1) * P],
                                          fc2[:, e, c, :], start=(c == 0), stop=(c == 3))
                    i.then_inc(s.y_ready, 1)

                expert_up(0)
                for e in range(E):
                    if e == 1:
                        pe.wait_ge(s.comb_ready, 1)
                        for t in range(NT):
                            i = pe.transpose(bank(6)[0:E, t * P:(t + 1) * P], comb[:, t, 0:E], ident)
                        i.then_inc(s.comb_turned, 1)
                    if e + 1 < E:
                        expert_up(e + 1)
                    expert_down(e)
                pe.wait_ge(s.combT_ready, 1)
                for t in range(NT):
                    i = pe.matmul(bank(7)[:, t * P:(t + 1) * P], combT[0:E, t * P:(t + 1) * P],
                                  CB["fc2_b"][0:E, :], start=True, stop=True)
                i.then_inc(s.y_ready, 1)

            if stop >= 3:
                turn_xn(3)
                pe.wait_ge(s.ld_wb, 16)
                pe.wait_ge(s.ld_ctxT, 16)

                def keys_values(b):
                    for t in range(4 * b, 4 * b + 4):
                        pe.wait_ge(s.lnT_ready, 3)
                        if t >= 2:
                            pe.wait_ge(s.kv1_read, t - 1)
                        pe.matmul(bank(t % 2)[:, 0:P], ctxT[:, t * P:(t + 1) * P], WB["wk1"], start=True, stop=True)
                        pe.matmul(bank(t % 2)[:, P:2 * P], ctxT[:, t * P:(t + 1) * P], WB["wv1"],
                                  start=True, stop=True).then_inc(s.kv1_ready, 1)

                keys_values(0)
                for t in range(NT):
                    i = pe.matmul(bank(2)[:, t * P:(t + 1) * P], lnT[:, t * P:(t + 1) * P], WB["wq1"],
                                  start=True, stop=True)
                i.then_inc(s.q2_ready, 1)
                stack(PHASE_TILES[1][0:6])
                keys_values(1)
                stack(PHASE_TILES[1][6:12])
                stacked(pe, PHASE_TILES[1][-1])
                attention(1)
                project(1, 1, WB["wo1"])

            if stop >= 4:
                turn_xn(4)
                pe.wait_ge(s.lnT_ready, 4)
                pe.wait_ge(s.ld_wd, 16)
                pe.wait_ge(s.ld_w12, 16)
                pe.wait_ge(s.ld_w3s, 16)
                for t in range(NT):
                    i = pe.matmul(bank(7)[:, t * NU:(t + 1) * NU], lnT[:, t * P:(t + 1) * P], WD["wg1"],
                                  start=True, stop=True)
                i.then_inc(s.logit_ready, 1)
                for t in range(NT):
                    if t >= 2:
                        pe.wait_ge(s.hh_ready, t - 1)
                    for c in range(3):
                        w = min(512, NU * P - 512 * c)
                        i = pe.matmul(bank(3 * (t % 2) + c)[:, 0:w], lnT[:, t * P:(t + 1) * P],
                                      w12[:, 512 * c:512 * c + w], start=True, stop=True)
                    i.then_inc(s.u_ready, 1)
                pe.wait_ge(s.comb_ready, 2)
                for t in range(NT):
                    i = pe.transpose(bank(6)[0:NU, t * P:(t + 1) * P], comb[:, t, :], ident)
                i.then_inc(s.comb_turned, 1)
                for r in range(5):
                    i = pe.matmul(bank(7)[0:NU, 0:P], CB["bsel"][:, r * NU:(r + 1) * NU], w3s[:, r, :],
                                  start=(r == 0), stop=(r == 4))
                i.then_inc(s.b9_ready, 1)
                pe.wait_ge(s.z_ready, 1)
                for r in range(5):
                    for t in range(NT):
                        i = pe.transpose(bank(r)[:, t * P:(t + 1) * P],
                                         U[:, t, 2 * r:2 * r + 2, :].rearrange("p u n -> p (u n)"), ident)
                    i.then_inc(s.z_turned, 1)
                pe.wait_ge(s.zT_dve, 3)
                pe.wait_ge(s.zT_act, 2)
                pe.wait_ge(s.combT_ready, 2)
                pe.wait_ge(s.b9_read, 1)
                for t in range(NT):
                    o = bank(5)[:, t * P:(t + 1) * P]
                    for r in range(5):
                        pe.matmul(o, ZT[:, r, t * P:(t + 1) * P], w3s[:, r, :], start=(r == 0), stop=False)
                    i = pe.matmul(o, combT[:, t * P:(t + 1) * P], b9s[:, :], start=False, stop=True)
                i.then_inc(s.y_ready, 1)

            if stop >= 5:
                pe.wait_ge(s.combT_ready, 2)
                for n in range(2):
                    pe.matmul(bank(6 + n), WD["wk2"], ctxT[:, n * 512:(n + 1) * 512], start=True, stop=True)\
                        .then_inc(s.kv2_ready, 1)
                for n in range(2):
                    pe.wait_ge(s.kv2_read, n + 1)
                    for k in range(4):
                        i = pe.matmul(bank(6 + n)[:, k * P:(k + 1) * P], ctxT[:, (4 * n + k) * P:(4 * n + k + 1) * P],
                                      WD["wv2"], start=True, stop=True)
                    i.then_inc(s.kv2_ready, 1)
                turn_xn(5)
                pe.wait_ge(s.lnT_ready, 5)
                pe.matmul(bank(1), WD["wq2"], lnT[:, :], start=True, stop=True).then_inc(s.q2_ready, 1)
                pe.wait_ge(s.q2_read, 1)
                pe.wait_ge(s.kv2_read, 4)
                for t in range(NT):
                    pe.matmul(bank(t), rest[:, t * P:(t + 1) * P], KT2[:, (t // 2) * SK:(t // 2 + 1) * SK],
                              start=True, stop=True).then_inc(s.s2_ready, 1)
                for t in range(NT):
                    pe.wait_ge(s.p2_ready, t + 1)
                    for k in range(4):
                        i = pe.transpose(bank(4 + t)[:, k * P:(k + 1) * P], P2[:, t, k * P:(k + 1) * P], ident)
                    i.then_inc(s.p2_turned, 1)
                for t in range(NT):
                    pe.wait_ge(s.pt2_ready, t + 1)
                    for k in range(4):
                        i = pe.matmul(bank(0)[:, t * P:(t + 1) * P], PT2[:, t, k, :], V2[:, 4 * (t // 2) + k, :],
                                      start=(k == 0), stop=(k == 3))
                i.then_inc(s.y_ready, 1)

            if stop >= 6:
                pe.wait_ge(s.wq_ready, 1)
                for m in range(2):
                    for c in range(3):
                        i = pe.transpose(bankb(1 + m)[:, c * P:(c + 1) * P], wq2i[:, m, c, :], identb[:, :])
                    i.then_inc(s.wq_turned, 1)
                for c in range(3):
                    n = P if c < 2 else I2R
                    i = pe.transpose(bankb(3)[0:n, c * P:(c + 1) * P], wd2i[:, c * P:c * P + n], identb[:, :])
                i.then_inc(s.wq_turned, 1)
                pe.wait_ge(s.xq_ready, 1)
                for t in range(NT):
                    i = pe.transpose(bankb(0)[:, t * P:(t + 1) * P], xqi[:, t, :], identb[:, :])
                i.then_inc(s.xq_turned, 1)
                pe.wait_ge(s.xqT_ready, 1)
                pe.wait_ge(s.wq_read, 3)
                for c in range(3):
                    n = P if c < 2 else I2R
                    for m in range(2):
                        pe.matmul(bank(3 * m + c)[0:n, :], wgT[:, m, c, 0:n], xqT[:, :], start=True, stop=True)\
                            .then_inc(s.g2_ready, 1)
                pe.wait_ge(s.hq_ready, 1)
                for c in range(3):
                    n = P if c < 2 else I2R
                    i = pe.matmul(bank(6), wdT[0:n, c, :], hqT[0:n, c, :], start=(c == 0), stop=(c == 2))
                i.then_inc(s.y2_ready, 1)
                pe.wait_ge(s.y2_read, 1)
                for t in range(NT):
                    i = pe.transpose(bank(7)[:, t * P:(t + 1) * P], rest[:, t * P:(t + 1) * P], ident)
                i.then_inc(s.y2_turned, 1)

            if stop >= 7:
                pe.wait_ge(s.ld_w3, 16)
                pe.wait_ge(s.x_ready, 6)
                for n in range(16):
                    if n >= 4:
                        pe.wait_ge(s.k3_act if n % 2 else s.k3_dve, (n - 4) // 2 + 1)
                    r, half = n // 2, n % 2
                    pe.matmul(bank(4 + n % 4), W3[:, 1, r * P:(r + 1) * P], ctxT[:, half * 512:(half + 1) * 512],
                              start=True, stop=True).then_inc(s.k3_ready, 1)
                for n in range(16):
                    if n < 4:
                        pe.wait_ge(s.k3_act if n % 2 else s.k3_dve, (12 + n) // 2 + 1)
                    else:
                        pe.wait_ge(s.v3_read, n - 3)
                    pe.matmul(bank(4 + n % 4), ctxT[:, (n // 2) * P:(n // 2 + 1) * P],
                              W3[:, 2, (n % 2) * 512:(n % 2 + 1) * 512], start=True, stop=True)\
                        .then_inc(s.v3_ready, 1)
                turn_xn(7)
                pe.wait_ge(s.lnT_ready, 6)
                pe.wait_ge(s.v3_read, 16)
                for r in range(8):
                    if r >= 2:
                        pe.wait_ge(s.q3_act, r - 1)
                        pe.wait_ge(s.q3_dve, r - 1)
                    pe.matmul(bank(4 + r % 2), W3[:, 0, r * P:(r + 1) * P], lnT[:, :], start=True, stop=True)\
                        .then_inc(s.q3_ready, 1)
                pe.wait_ge(s.q3_act, 8)
                pe.wait_ge(s.q3_dve, 8)
                pe.wait_ge(s.v3_masked, KT)
                attention(2)
                project3()

            if stop >= 8:
                turn_xn(9)
                pe.wait_ge(s.lnT_ready, 7)
                for pair in range(2):
                    for j in range(2):
                        t = 2 * pair + j
                        i = pe.matmul(bank(1 + pair)[:, 192 * j:192 * (j + 1)], lnT[:, t * P:(t + 1) * P],
                                      WD["wqkv"], start=True, stop=True)
                    i.then_inc(s.qkv_ready, 1)
                stack(PHASE_TILES[2])
                stacked(pe, PHASE_TILES[2][-1])
                attention(3)
                project(3, 3, WD["wo3f"])
                turn_xn(10)
                pe.wait_ge(s.lnT_ready, 8)
                for t in range(NT):
                    i = pe.matmul(bank(2)[:, t * E:(t + 1) * E], lnT[:, t * P:(t + 1) * P], WD["gate3"],
                                  start=True, stop=True)
                i.then_inc(s.logit_ready, 1)
                pe.wait_ge(s.ld_w13, 16)
                pe.wait_ge(s.ld_w2e, 16)
                pe.wait_ge(s.gate_diff, 4)

                def up3(e):
                    for c in range(4):
                        if e:
                            if c < 2:
                                pe.wait_ge(s.act_ready, 4 * E + 2 * (e - 1) + c + 1)
                            else:
                                pe.wait_ge(s.hd_ready, E + 2 * (e - 1) + c - 1)
                        pe.matmul(bank(c), w13[:, e, c * P:(c + 1) * P], lnT[:, :], start=True, stop=True)\
                            .then_inc(s.h_ready, 1)

                def down3(e):
                    pe.wait_ge(s.hd_ready, E + 2 * e + 2)
                    if e >= 2:
                        pe.wait_ge(s.y_added, E + e - 1)
                    for t in range(NT):
                        for c in range(2):
                            i = pe.matmul(bank(4 + e % 2)[:, t * P:(t + 1) * P], actT[:, e % 2, c, t * P:(t + 1) * P],
                                          w2e[:, e, c, :], start=(c == 0), stop=(c == 1))
                    i.then_inc(s.y_ready, 1)

                up3(0)
                for e in range(E):
                    if e + 1 < E:
                        up3(e + 1)
                    down3(e)


def kernel(**inputs):
    import concourse.bacc as bacc
    from concourse.bass_utils import run_bass_kernel_spmd
    from ml_dtypes import bfloat16

    a = {k: np.asarray(v) for k, v in inputs.items()}
    f32 = np.float32

    def pack(widths, parts):
        return np.ascontiguousarray(np.concatenate([np.reshape(parts[k], (P, w)) for k, w in widths.items()], 1))

    def chunks(w):
        return np.moveaxis(w.reshape(*w.shape[:-1], -1, P), -1, 0)

    def row(v):
        return np.broadcast_to(v.reshape(1, -1), (P, v.size))

    def on_top(v):
        return np.concatenate([v, np.zeros((P - v.shape[0], v.shape[1]), v.dtype)], 0)

    i = np.arange(P)
    pos = (np.arange(NT) % 2)[None, :] * P + i[:, None]
    inv_freq = (f32(1.0) / f32(10000.0) ** (np.arange(0, HD, 2, dtype=f32) / f32(HD))).astype(f32)
    angle = pos[:, :, None].astype(f32) * np.concatenate([inv_freq, inv_freq])[None, None, :]
    sign = np.repeat(np.array([-1.0, 1.0], f32), HD // 2)
    const = pack(CONST, dict(
        ident=np.eye(P, dtype=f32), mask_n=np.where(i[None, :] > i[:, None], f32(NEG), f32(0)),
        mask_t=np.where(i[:, None] > i[None, :], f32(NEG), f32(0)), cos=np.cos(angle), sin=np.sin(angle) * sign,
        tokpos=np.stack([i, i + P], 1).astype(f32), eidx=row(np.arange(E, dtype=f32))))
    sel = np.zeros((4 * NPART, H, NK), bfloat16)
    onesel = np.zeros((P, 4, P), bfloat16)
    for c in range(4):
        sel[c::4, c::4] = 1
        onesel[PAD + c:MROW:4, c] = 1

    g, lb = a["L1_ffn_sel_ln_g"], a["L1_ffn_sel_ln_b"]
    gcol = np.stack([np.concatenate([g, g])] * 4 + [np.concatenate([a["L1_ffn_s_ln_g"], np.ones(H1, f32)])], 1)
    bsel = np.zeros((P, 5, NU), f32)
    for u in range(NU):
        bsel[H1 * (u % 2):H1 * (u % 2 + 1), u // 2, u] = lb if u < E else a["L1_ffn_s_ln_b"]
    cols = pack(COLS, dict(
        ln0_w=a["L0_ffn_ln_w"].T, ln0_b=a["L0_ffn_ln_b"].T, fc1_b=chunks(a["L0_ffn_fc1_b"]), gcol=gcol,
        bq3=a["L3_xattn_bq"].reshape(8, P).T, bk3=a["L3_xattn_bk"].reshape(8, P).T,
        rms1=a["L3_ffn_ln1_w"], rms2=a["L3_ffn_ln2_w"], maskk=a["fside_BxS2_0"].reshape(KT, P).T, bsel=bsel,
        fc2_b=on_top(a["L0_ffn_fc2_b"]), b9=on_top(np.concatenate([a["L1_ffn_eb3"], a["L1_ffn_sb3"][None]], 0))))
    rows = pack(ROWS, dict(
        bo0=row(a["L0_xattn_b_out"]), alpha=row(a["L0_ffn_alpha"]), bq1=row(a["L1_xattn_bq"]),
        bk1=row(a["L1_xattn_bk"]), bv1=row(a["L1_xattn_bv"]), bo1=row(a["L1_xattn_bo"]),
        gb=row(np.concatenate([a["L1_ffn_eg_b"], a["L1_ffn_sg_b"]])), ebias=row(a["L1_ffn_exp_bias"]),
        bo3=row(a["L3_xattn_bo"]), clip=row(np.concatenate([a["L2_ffn_clip_x"], a["L2_ffn_clip_down"]])),
        bv3=row(a["L3_xattn_bv"])))
    b1 = np.concatenate([a["L1_ffn_eb1"], a["L1_ffn_sb1"][None]], 0)
    b2 = np.concatenate([a["L1_ffn_eb2"], a["L1_ffn_sb2"][None]], 0)
    w1 = np.concatenate([a["L1_ffn_ew1"], a["L1_ffn_sw1"][None]], 0)
    w2 = np.concatenate([a["L1_ffn_ew2"], a["L1_ffn_sw2"][None]], 0)
    w3 = np.concatenate([a["L1_ffn_ew3"], a["L1_ffn_sw3"][None], np.zeros((1, P, H1), f32)], 0)

    def rows_of_three(w):
        return np.concatenate([w, np.ones((3 * P - I2, P), f32)], 0).reshape(3, P, P).transpose(1, 0, 2)

    arrays = {
        "const": const, "cols": cols, "rows": rows, "sel": sel, "onesel": onesel,
        "x": a["x"].reshape(NT, P, P).transpose(1, 0, 2),
        "ctx": a["ctx_1024"].reshape(KT, P, P).transpose(1, 0, 2),
        "ctxT": a["ctx_1024"].reshape(NK, P).T,
        "w_a": pack(W_A, dict(wo0=a["L0_xattn_w_out"].T, wg0=a["L0_ffn_Wg"])),
        "w_b": pack(W_B, dict(wq1=a["L1_xattn_Wq"], wk1=a["L1_xattn_Wk"], wv1=a["L1_xattn_Wv"],
                              wo1=a["L1_xattn_Wo"])),
        "fc1": a["L0_ffn_fc1_w"].transpose(1, 0, 2),
        "fc2": a["L0_ffn_fc2_w"].reshape(E, 4, P, P).transpose(2, 0, 1, 3),
        "w12": np.concatenate([w1, w2], 1).transpose(2, 0, 1).reshape(P, NU * P),
        "b12": row(np.concatenate([b1, b2], 1)),
        "w3s": w3.transpose(0, 2, 1).reshape(5, P, P).transpose(1, 0, 2),
        "w_d": pack(W_D, dict(
            wg1=np.concatenate([a["L1_ffn_eg_w"], a["L1_ffn_sg_w"]], 0).T, wq2=a["L2_xattn_Wq"].T,
            wk2=a["L2_xattn_Wk"].T, wv2=a["L2_xattn_Wv"].T, wqkv=a["L3_ffn_wqkv"].T, wo3f=a["L3_ffn_wo"].T,
            gate3=a["L3_ffn_gate_w"].T, wo3=a["L3_xattn_Wo"].reshape(8, P, P).transpose(1, 0, 2))),
        "w_2": np.concatenate([rows_of_three(a["L2_ffn_w_gate"]).reshape(P, -1),
                               rows_of_three(a["L2_ffn_w_up"]).reshape(P, -1), a["L2_ffn_w_down"]], 1),
        "w3": np.stack([a["L3_xattn_Wq"].reshape(P, -1), a["L3_xattn_Wk"].reshape(P, -1),
                        a["L3_xattn_Wv"].reshape(P, -1)], 1),
        "w13": a["L3_ffn_w13"].transpose(2, 0, 1),
        "w2e": a["L3_ffn_w2"].reshape(E, P, 2, P).transpose(3, 0, 2, 1),
        "idx": np.broadcast_to(np.stack([a["L1_ffn_index_b"], a["L1_ffn_index_t"]])[None], (P, 2, 256)),
    }
    arrays = {k: np.ascontiguousarray(v) for k, v in arrays.items()}
    nc = bacc.Bacc("TRN2", target_bir_lowering=False, num_devices=1)
    dram = {k: nc.dram_tensor(f"in_{k}", v.shape, mybir.dt.from_np(v.dtype), kind="ExternalInput").ap()
            for k, v in arrays.items()}
    out = nc.dram_tensor("out", (P, NT, P), F32, kind="ExternalOutput").ap()
    mega_kernel(nc, dram, out)
    r = run_bass_kernel_spmd(nc, [{f"in_{k}": v for k, v in arrays.items()}], core_ids=[0])
    got = r.results[0]["out"]
    return np.ascontiguousarray(got.transpose(1, 0, 2)).reshape(B, SQ, P)
```

```python
from contextlib import ExitStack

import numpy as np

import concourse.bass as bass
from concourse import mybir

F32 = mybir.dt.float32
BF16 = mybir.dt.bfloat16
I32 = mybir.dt.int32
U32 = mybir.dt.uint32
ALU = mybir.AluOpType
ACT = mybir.ActivationFunctionType
AX_X = mybir.AxisListType.X
ABSMAX = bass.bass_isa.ReduceOp.absmax

P = 128
NT = 4
T = NT * P
B = 2
SQ = T // B
SK = 512
NK = B * SK
KT = NK // P
H = 16
HD = 8
NPART = 3
PAD = 96
MROW = PAD + 4 * NPART
VW = 32
G = 8
E = 8
F0 = 512
H1 = 64
NU = E + 1
I2 = 352
I2R = I2 - 2 * P
DH3 = 64
KV3 = 4
F3 = 256
EPS = 1e-5
ROUND = 1.5 * 2.0 ** 23
QMAX = 127.0
NEG = -1e30

CONST = dict(ident=P, mask_n=P, mask_t=P, cos=NT * HD, sin=NT * HD, tokpos=2, eidx=E)
COLS = dict(ln0_w=E, ln0_b=E, fc1_b=E * 4, gcol=5, bq3=8, bk3=8, rms1=1, rms2=1, maskk=KT,
            bsel=5 * NU, fc2_b=P, b9=P)
ROWS = dict(bo0=P, alpha=E, bq1=P, bk1=P, bv1=P, bo1=P, gb=NU, ebias=E, bo3=P,
            clip=2, bv3=1024)
W_A = dict(wo0=P, wg0=E)
W_B = dict(wq1=P, wk1=P, wv1=P, wo1=P)
W_C = dict(w12=NU * P, w3=5 * P)
W_D = dict(wg1=NU, wq2=P, wk2=P, wv2=P, wqkv=192, wo3f=P,
           gate3=E, wo3=8 * P)


def columns(widths):
    at, out = 0, {}
    for name, width in widths.items():
        out[name] = (at, at + width)
        at += width
    return out, at


def mega_kernel(nc, d, out_dram):
    ctx = ExitStack()
    with ctx:
        def sb(name, shape, dt=F32):
            return ctx.enter_context(nc.sbuf_tensor(name, shape, dt))

        def sem(name):
            return ctx.enter_context(nc.semaphore(name))

        def pack(name, widths):
            at, width = columns(widths)
            t = sb(name, [P, width])
            return t, {k: t[:, a:b] for k, (a, b) in at.items()}

        const_t, C = pack("const_t", CONST)
        cols_t, CB = pack("cols_t", COLS)
        rows_t, RB = pack("rows_t", ROWS)
        wa_t, WA = pack("wa_t", W_A)
        wb_t, WB = pack("wb_t", W_B)
        wd_t, WD = pack("wd_t", W_D)
        Kst = sb("Kst", [P, H, NK], BF16)
        Qst = sb("Qst", [P, H, T], BF16)
        REP = sb("REP", [P, 4 * H * PAD], BF16)
        REPv = REP[:, :].rearrange("p (t h r) -> p t h r", t=4, h=H)
        VX = sb("VX", [P, 8192])
        Vaug = VX[:, 0:4096].rearrange("p (k h w) -> p k h w", k=KT, h=H)
        w12 = VX[:, 4096:4096 + NU * P]
        b12 = VX[:, 5888:5888 + NU * P]
        w3s = VX[:, 5248:5248 + 5 * P].rearrange("p (u n) -> p u n", u=5)
        K3 = VX[:, :].rearrange("p (r k) -> p r k", r=8)
        V3 = Kst[:, :, :].rearrange("p h k -> p (h k)").bitcast(F32).rearrange("p (k n) -> p k n", k=KT)
        FC = sb("FC", [P, 8192])
        fc1 = FC[:, 0:4096].rearrange("p (e f) -> p e f", e=E)
        fc2 = FC[:, 4096:8192].rearrange("p (e c n) -> p e c n", e=E, c=4)
        Q3 = FC[:, :].rearrange("p (h t) -> p h t", h=H)
        w13 = FC[:, 0:4096].rearrange("p (e f) -> p e f", e=E)
        w2e = FC[:, 4096:6144].rearrange("p (e c n) -> p e c n", e=E, c=2)
        W3 = REP[:, :].bitcast(F32).rearrange("p (m n) -> p m n", m=3)
        OT3 = REP[:, 0:4096].bitcast(F32).rearrange("p (r q) -> p r q", r=8)
        PR = sb("PR", [P, 8192])
        PRg = PR[:, :].rearrange("p (s n) -> p s n", s=2)
        actT = PR[:, 0:4096].rearrange("p (s c t) -> p s c t", s=2, c=4)
        hdT = PR[:, 4096:5120].rearrange("p (s t) -> p s t", s=2)
        HH = PR[:, 0:NT * NU * P].rearrange("p (t u n) -> p t u n", t=NT, u=NU)
        U = PR[:, 4608:4608 + NT * 10 * H1].rearrange("p (t u n) -> p t u n", t=NT, u=10)
        SL = FC[:, 0:NT * NU * H1].rearrange("p (t u n) -> p t u n", t=NT, u=NU)
        idf = PR[:, 5632:6656].rearrange("p (a n) -> p a n", a=4)
        eqm = PR[:, 6656:7680].rearrange("p (a n) -> p a n", a=NT)
        idx = PR[:, 5120:5632].bitcast(I32).rearrange("p (a n) -> p a n", a=2)
        KT2 = FC[:, 4608:5632]
        V2 = FC[:, 5632:6656].rearrange("p (k n) -> p k n", k=KT)
        w2_t = FC[:, 6656:6656 + 6 * P + I2]
        WD2 = dict(gate2=w2_t[:, 0:3 * P], up2=w2_t[:, 3 * P:6 * P], down2=w2_t[:, 6 * P:])
        bf = FC[:, 0:2304].bitcast(BF16)
        wq2i = bf[:, 0:768].rearrange("p (m c n) -> p m c n", m=2, c=3)
        wgT = bf[:, 768:1536].rearrange("p (m c n) -> p m c n", m=2, c=3)
        wdT = bf[:, 1536:1920].rearrange("p (c n) -> p c n", c=3)
        wd2i = bf[:, 1920:1920 + I2]
        xqi = bf[:, 2304:2816].rearrange("p (t n) -> p t n", t=NT)
        xqT = bf[:, 2816:3328]
        hqT = FC[:, 2304:3072].bitcast(BF16).rearrange("p (c t) -> p c t", c=3)
        K4 = FC[:, 6144:7168].bitcast(BF16).rearrange("p (h t) -> p h t", h=KV3)
        V4 = FC[:, 7168:7680].rearrange("p (t h w) -> p t h w", t=NT, h=KV3)
        ZT = PR[:, 0:5 * T].rearrange("p (r t) -> p r t", r=5)
        P2 = PR[:, 0:2048].rearrange("p (t k) -> p t k", t=NT)
        PT2 = PR[:, 2048:4096].rearrange("p (t k q) -> p t k q", t=NT, k=4)
        SG = PR[:, 4096:5632].rearrange("p (c t) -> p c t", c=3)
        h2T = PR[:, 5632:7168].rearrange("p (c t) -> p c t", c=3)
        qrope = PR[:, 0:NT * 160].rearrange("p (t n) -> p t n", t=NT)
        qrot = PR[:, 1024:1024 + NT * 160].rearrange("p (t n) -> p t n", t=NT)
        x = sb("x", [P, NT, P])
        xn = sb("xn", [P, NT, P])
        scr = sb("scr", [P, 4 * T])
        lnT = scr[:, 0:T]
        zT = scr[:, T:2 * T]
        Onat = scr[:, 2 * T:3 * T].rearrange("p (t n) -> p t n", t=NT)
        OT = scr[:, 3 * T:4 * T]
        P3 = Qst[:, :, :].rearrange("p h t -> p (h t)").bitcast(F32).rearrange("p (s k) -> p s k", s=8)
        OT3b = [OT3, scr[:, :].rearrange("p (r q) -> p r q", r=8)]
        parts = sb("parts", [P, NPART, SK + SQ], BF16)
        rest = sb("rest", [P, T])
        ctxT = sb("ctxT", [P, NK])
        CTXN = PR[:, 0:1024].rearrange("p (k n) -> p k n", k=KT)
        identb = sb("identb", [P, P], BF16)
        maskb = sb("maskb", [P, 2, P], BF16)
        onesel = sb("onesel", [P, 4, P], BF16)
        st6 = sb("st6", [P, NT, 6])
        mv = sb("mv", [P, NT, 2])
        ve = sb("ve", [P, 64])
        nhalf = sb("nhalf", [P, 64])
        rstd = sb("rstd", [P, 64])
        mxs = sb("mxs", [P, 2, 2, 4])
        mr = sb("mr", [P, 8])
        mp = sb("mp", [P, 2, 2, NPART, 4], BF16)
        rden = sb("rden", [P, 2, 4])
        warmth = sb("warmth", [P, 2])
        nm3 = sb("nm3", [P, 8])
        sum3 = sb("sum3", [P, 16])
        rsum3 = sb("rsum3", [P, 8])
        rwide3 = sb("rwide3", [P, 8, DH3])
        bq3s = sb("bq3s", [P, 8])
        lg = sb("lg", [P, NT, NU])
        v8 = sb("v8", [P, NT, E])
        i8 = sb("i8", [P, NT, E], U32)
        i8f = sb("i8f", [P, NT, E])
        gt = sb("gt", [P, NT, 8])
        oh = sb("oh", [P, 2, NT, E])
        comb = sb("comb", [P, NT, NU])
        combT = sb("combT", [NU, T])
        b9s = sb("b9s", [NU, P])
        tmask = sb("tmask", [P, NT])
        qs = sb("qs", [P, 48])

        ps = ctx.enter_context(nc.psum_tensor("ps", [P, 8, 512], F32))

        def bank(b, n=1):
            return ps[:, b:b + n, :].rearrange("p b n -> p (b n)")

        def bankb(b):
            return ps[:, b, :].bitcast(BF16)

        names = """ld_const ld_x ld_ctxT ld_ctx ld_cols ld_rows ld_sel ld_wa ld_wb ld_fc1 ld_fc2
            ld_w12 ld_w3s ld_b12 ld_w2 ld_wd ld_w3 ld_idx ld_w13 ld_w2e
            dve_done pool_done setup_dve setup_pool
            parts_ready rep_dve rep_act rep_pool rep_turned stack_dve stack_act
            var_ready rstd_ready xn_ready xn_turned lnT_ready
            smax_ready smax_read m_ready m_turned mrow_ready st_ready p_ready pv_ready ot_ready
            ot_turned o_ready onat_turned onatT_ready proj_ready x_ready
            kv1_ready kv1_read logit_ready comb_ready comb_turned combT_ready hd_ready
            h_ready act_ready y_ready y_added gate_exp gate_diff
            u_ready hh_ready silu_ready c_ready sq_ready var1_ready std1_ready z_ready z_turned zT_dve zT_act
            b9_ready b9_read
            kv2_ready kv2_read q2_ready q2_read s2_ready nm2_ready p2_ready p2_turned pt2_ready
            wscale_ready wq_ready wq_turned wq_read ax_ready ax_all scales_ready clip_exp xq_ready xq_turned
            xqT_ready g2_ready sg_ready hq_ready y2_ready y2_read y2_turned
            k3_ready k3_act v3_ready v3_act v3_biased q3_ready q3_dve q3_act q3_zero bq3_ready
            s3_ready nm3_ready p3_ready t3_ready pt3_ready pv3_ready sums3_read wide3_ready wide3_used o3_ready
            qkv_ready
            stored""".split()
        S = {n: sem(n) for n in names}
        s = type("Sems", (), S)

        block = ctx.enter_context(nc.Block())

        tiles = []
        for b in range(B):
            tiles += [("k", t, H) for t in range(4 * b, 4 * b + 4)] + [("q", t, H) for t in range(2 * b, 2 * b + 2)]
        tiles += [("k", t, H) for t in range(KT)] + [("Q", t, H) for t in range(NT)]
        for t in range(NT):
            tiles += [("4", t, KV3), ("r", t, H)]
        lots = []
        lots_till = []
        for n, (_, _, heads) in enumerate(tiles):
            for h in range(0, heads, 8):
                lots.append((n, h, min(8, heads)))
            lots_till.append(len(lots))
        PARTS_TILL = [n for n in range(4) for _ in range(2 if n % 2 else 4)] + [*range(4, 12)] + [12] * 4 \
            + [13] * 4 + [14] * 4
        OLD_TILES = [0, 0, 4, 6] + [10] * 4 + [13, 14, 15, 16] + [20, 24, 24]
        PHASE_TILES = [range(0, 12), range(12, 24), range(24, 32)]

        def stacked(eng, till_tile):
            n = lots_till[till_tile]
            eng.wait_ge(s.stack_dve, (n + 1) // 2)
            eng.wait_ge(s.stack_act, n // 2)

        MAXB = [0, 64, 128, 128 + 24]
        UNIT = [0, 32, 64, 64 + 16]

        TURNS = [1, 2, 3, 4, 5, 7, 9, 10]

        K1 = range(12, 20)
        K1_LOTS = range(24, 40)

        def lot_bank(n):
            return 6 + n % 2 if n in K1_LOTS else 3 + n % 4

        def groups(a, g):
            return a * G + g

        def stack_copy(eng, n, tl, h0, nh):
            kind, t, _ = tiles[tl]
            dst = {"k": Kst, "q": Qst, "Q": Qst, "r": Qst, "4": K4}[kind]
            src = bankb(lot_bank(n))[0:PAD, 0:nh * P].rearrange("p (h t) -> p h t", h=nh)
            to = dst[0:PAD, h0:h0 + nh, t * P:(t + 1) * P]
            return eng.tensor_copy(to, src) if eng is nc.vector else eng.copy(to, src)

        def spread(eng, n):
            kind, t, heads = tiles[n]
            j, done = {nc.gpsimd: (0, s.rep_pool), nc.scalar: (1, s.rep_act), nc.vector: (2, s.rep_dve)}[eng]
            at = {"k": P * (t % 4), "q": SK + P * (t % 2), "Q": P * t, "4": 160 * t + P, "r": 160 * t}[kind]
            eng.wait_ge(s.parts_ready, NPART * PARTS_TILL[n] + j + 1)
            if n >= 4:
                eng.wait_ge(s.rep_turned, lots_till[n - 4])
            v = REPv[:, n % 4, 0:heads, 0:72].rearrange("p h (i j c) -> p h i j c", i=3, j=3)
            to = v[:, :, j, :, :] if kind in "qQr" else v[:, :, :, j, :]
            src = parts[:, j, at:at + heads * HD].rearrange("p (h o c) -> p h o c", h=heads, o=1)\
                .to_broadcast([P, heads, 3, HD])
            i = eng.copy(to, src) if eng is nc.scalar else eng.tensor_copy(to, src)
            i.then_inc(done, 1)

        def spread_and_stack(eng, to_spread, to_stack):
            odd, done = (1, s.stack_act) if eng is nc.scalar else (0, s.stack_dve)

            def stack_lots(tile):
                for n, (tl, h0, nh) in enumerate(lots):
                    if tl == tile and n % 2 == odd:
                        eng.wait_ge(s.rep_turned, n + 1)
                        stack_copy(eng, n, tl, h0, nh).then_inc(done, 1)

            behind = list(to_stack)
            for n in to_spread:
                spread(eng, n)
                while behind and behind[0] <= n - 2:
                    stack_lots(behind.pop(0))
            for tile in behind:
                stack_lots(tile)

        SCALES = [float(P) ** -0.5, float(HD) ** -0.5, float(HD) ** -0.5]
        N3 = 2 * H * B
        S_BANKS, T_BANKS, O_BANKS = (0, 1, 3), (4, 5), (6, 7)
        LAG = 4
        PV3 = 8 + LAG

        def k3_bank(n):
            return 4 + n % 4 if n < 12 else 6 + n % 2

        def v3_bank(n):
            return n % 3 if n < 12 else 6 + n % 2

        def unit3(n):
            g, u = n // 8, n % 8
            b, h0 = group_heads(2, g)
            return g, u // 2, u % 2, h0 + u // 2, b

        def group_heads(a, g):
            return g // 4, 4 * (g % 4)

        def add_expert(dve, e, count, b0, y_base=0):
            dve.wait_ge(s.y_ready, y_base + e + 1)
            if count:
                dve.wait_ge(s.y_added, count)
            y = bank(b0 + e % 2).rearrange("p (t n) -> p t n", t=NT)
            for t in range(NT):
                i = dve.scalar_tensor_tensor(out=x[:, t, :], in0=y[:, t, :], scalar=comb[:, t, e:e + 1],
                                             in1=x[:, t, :], op0=ALU.mult, op1=ALU.add)
            i.then_inc(s.y_added, 1)

        @block.sync
        def _(sp):
            sp.dma_start(const_t[:, :], d["const"]).then_inc(s.ld_const, 16)
            sp.dma_start(x[:, :, :], d["x"]).then_inc(s.ld_x, 16)
            sp.dma_start(CTXN, d["ctx"]).then_inc(s.ld_ctx, 16)
            sp.dma_start(rows_t[:, :], d["rows"]).then_inc(s.ld_rows, 16)
            sp.dma_start(Kst[PAD:MROW, :, :], d["sel"]).then_inc(s.ld_sel, 16)
            sp.dma_start(onesel[:, :, :], d["onesel"]).then_inc(s.ld_sel, 16)
            sp.dma_start(wa_t[:, :], d["w_a"]).then_inc(s.ld_wa, 16)
            sp.dma_start(cols_t[:, :], d["cols"]).then_inc(s.ld_cols, 16)
            sp.dma_start(ctxT[:, :], d["ctxT"]).then_inc(s.ld_ctxT, 16)
            sp.dma_start(wb_t[:, :], d["w_b"]).then_inc(s.ld_wb, 16)
            sp.dma_start(fc1, d["fc1"]).then_inc(s.ld_fc1, 16)
            sp.dma_start(fc2, d["fc2"]).then_inc(s.ld_fc2, 16)
            sp.dma_start(w12, d["w12"]).then_inc(s.ld_w12, 16)
            sp.dma_start(w3s, d["w3s"]).then_inc(s.ld_w3s, 16)
            sp.dma_start(b12, d["b12"]).then_inc(s.ld_b12, 16)
            sp.dma_start(wd_t[:, :], d["w_d"]).then_inc(s.ld_wd, 16)
            sp.wait_ge(s.pv_ready, G)
            sp.dma_start(idx, d["idx"]).then_inc(s.ld_idx, 16)
            sp.wait_ge(s.y_ready, E + 1)
            sp.dma_start(w2_t, d["w_2"]).then_inc(s.ld_w2, 16)
            sp.wait_ge(s.rep_turned, lots_till[PHASE_TILES[1][-1]])
            sp.dma_start(W3, d["w3"]).then_inc(s.ld_w3, 16)
            sp.wait_ge(s.pv3_ready, G)
            sp.dma_start(w13, d["w13"]).then_inc(s.ld_w13, 16)
            sp.dma_start(w2e, d["w2e"]).then_inc(s.ld_w2e, 16)
            sp.wait_ge(s.y_added, 2 * E)
            sp.dma_start(out_dram, x[:, :, :]).then_inc(s.stored, 16)
            sp.wait_ge(s.stored, 16)

        @block.gpsimd
        def _(pool):
            chain = [0]

            def link(ins):
                chain[0] += 1
                ins.then_inc(s.pool_done, 1)
                pool.wait_ge(s.pool_done, chain[0])

            pool.memset(nhalf[:, :], -0.5).then_inc(s.setup_pool, 1)
            pool.memset(VX[:, 0:4096], 0.0).then_inc(s.setup_pool, 1)
            pool.wait_ge(s.setup_pool, 2)
            pool.memset(Vaug[:, :, :, HD:HD + 1], 1.0).then_inc(s.setup_pool, 1)

            def rstd_of(k):
                pool.wait_ge(s.var_ready, k + 1)
                link(pool.tensor_scalar(ve[:, 0:NT], mv[:, :, 1], EPS, None, ALU.add))
                pool.tensor_tensor(rstd[:, 0:NT], ve[:, 0:NT], nhalf[:, 0:NT], ALU.pow)\
                    .then_inc(s.rstd_ready, 1)

            pool.wait_ge(s.setup_dve, 1)
            spread(pool, 0)
            spread(pool, 1)
            rstd_of(0)
            for n in range(2, 12):
                spread(pool, n)
            pool.wait_ge(s.ld_ctx, 16)
            pool.tensor_copy(Vaug[:, :, :, 0:HD], CTXN.rearrange("p k (h c) -> p k h c", h=H))\
                .then_inc(s.setup_pool, 1)
            rstd_of(1)
            rstd_of(2)
            for n in K1:
                spread(pool, n)
            rstd_of(3)
            for n in PHASE_TILES[1][8:12]:
                spread(pool, n)
            rstd_of(4)
            def bias_values(k):
                pool.wait_ge(s.v3_act, 2 * k + 2)
                link(pool.tensor_tensor(V3[:, k, :], V3[:, k, :], RB["bv3"], ALU.add))
                pool.tensor_scalar(V3[:, k, :], V3[:, k, :], CB["maskk"][:, k:k + 1], None, ALU.mult)\
                    .then_inc(s.v3_biased, 1)

            def quantise(dst, src, inv, tmp):
                link(pool.tensor_scalar(tmp, src, inv, ROUND, ALU.mult, ALU.add))
                link(pool.tensor_scalar(tmp, tmp, -ROUND, QMAX, ALU.add, ALU.min))
                return pool.tensor_scalar(dst, tmp, -QMAX - 1.0, None, ALU.max)

            def clear_q3(heads):
                for h in heads:
                    p0 = DH3 * ((h + 1) % 2)
                    pool.memset(Q3[p0:p0 + DH3, h, :], 0.0).then_inc(s.q3_zero, 1)
                    pool.wait_ge(s.q3_zero, (h - 6) % H + 1)

            bias_values(0)
            bias_values(1)
            rstd_of(5)
            pool.wait_ge(s.wscale_ready, 1)
            for m, name in enumerate(("gate2", "up2")):
                for c in range(3):
                    link(quantise(wq2i[:, m, c, :], WD2[name][:, c * P:(c + 1) * P],
                                  qs[:, 40 + 3 * m + c:41 + 3 * m + c], h2T[:, 0, 0:P]))
            quantise(wd2i[:, :], WD2["down2"], qs[:, 46:47], h2T[:, 0, 0:I2]).then_inc(s.wq_ready, 1)
            rstd_of(6)
            for i in range(2):
                pool.wait_ge(s.ax_ready, i + 1)
                pool.partition_all_reduce(qs[:, 1 + 2 * i:2 + 2 * i], qs[:, 2 * i:2 * i + 1], P, ABSMAX)\
                    .then_inc(s.ax_all, 1)
                pool.wait_ge(s.ax_all, i + 1)
                if i == 0:
                    clear_q3(range(6, H))
            bias_values(2)
            pool.wait_ge(s.y2_ready, 1)
            pool.wait_ge(s.v3_biased, 3)
            clear_q3(range(0, 6))
            rstd_of(7)
            for k in range(3, KT):
                bias_values(k)
            rstd_of(8)
            rstd_of(9)
            pool.wait_ge(s.proj_ready, 3)
            pool.memset(REP[:, :].bitcast(F32), 0.0).then_inc(s.setup_pool, 1)
            pool.wait_ge(s.setup_pool, 5)
            for n in PHASE_TILES[2]:
                spread(pool, n)
            rstd_of(10)

        @block.scalar
        def _(act):
            def ln_out(k):
                act.wait_ge(s.xn_turned, TURNS.index(k) + 1)
                dst = zT if k == 2 else lnT
                if k in (9, 10):
                    w = CB["rms1"] if k == 9 else CB["rms2"]
                    act.activation(dst[:, :], bank(0), ACT.Copy, scale=w).then_inc(s.lnT_ready, 1)
                else:
                    act.copy(dst[:, :], bank(0)).then_inc(s.lnT_ready, 1)

            def attention(a):
                scale = SCALES[a]
                for step in range(G + 5):
                    g = step - 2
                    n_units = (UNIT[a + 1] - UNIT[a]) // G
                    for part in range(2):
                        if 0 <= g < G:
                            for u in range(part * n_units // 2, (part + 1) * n_units // 2):
                                n = UNIT[a] + g * n_units + u
                                act.wait_ge(s.st_ready, n + 1)
                                if groups(a, g) >= 2:
                                    act.wait_ge(s.pv_ready, groups(a, g) - 1)
                                width = 1024 if a < 2 or u == 0 else 512
                                act.activation(PRg[:, g % 2, u * 1024:u * 1024 + width],
                                               bank(3 + 2 * (n % 2), 2)[:, 0:width], ACT.Exp,
                                               scale=scale).then_inc(s.p_ready, 1)
                        if part == 0 and 0 <= step - 1 < G:
                            m = groups(a, step - 1)
                            gg = step - 1
                            act.wait_ge(s.m_turned, m + 1)
                            b, h0 = group_heads(a, gg)
                            act.copy(Qst[PAD:MROW, h0:h0 + 4, b * SQ:(b + 1) * SQ],
                                     bankb(2)[0:12, 0:SQ].unsqueeze(1).to_broadcast([12, 4, SQ]))\
                               .then_inc(s.mrow_ready, 1)
                    if 0 <= step - 3 < G:
                        m = groups(a, step - 3)
                        act.wait_ge(s.pv_ready, m + 1)
                        if groups(a, step - 3) >= 2:
                            act.wait_ge(s.ot_turned, groups(a, step - 3) - 1)
                        act.copy(OT[:, (m % 2) * SQ:(m % 2 + 1) * SQ], bank(7)[:, (m % 2) * SQ:(m % 2 + 1) * SQ])\
                            .then_inc(s.ot_ready, 1)

            def warm(func):
                act.activation(warmth[:, 1:2], warmth[:, 0:1], func)

            def queries3(r):
                act.wait_ge(s.q3_ready, r + 1)
                act.activation(Q3[DH3:P, 2 * r + 1, :], bank(O_BANKS[r % 2])[DH3:P, :], ACT.Identity,
                               bias=bq3s[DH3:P, r:r + 1], scale=float(DH3) ** -0.5).then_inc(s.q3_act, 1)

            def attention3():
                for i in range(N3 + LAG):
                    if i < N3:
                        act.wait_ge(s.nm3_ready, i + 1)
                        if i >= 8:
                            act.wait_ge(s.t3_ready, i - 7)
                        act.activation(P3[:, i % 8, :], bank(S_BANKS[i % 3]), ACT.Exp,
                                       bias=nm3[:, i % 8:i % 8 + 1],
                                       accum_out=sum3[:, i % 16:i % 16 + 1]).then_inc(s.p3_ready, 1)
                        if i < 6:
                            queries3(i + 2)
                    j = i - LAG
                    if j >= 0:
                        g, c, qt, _, _ = unit3(j)
                        act.wait_ge(s.t3_ready, j + 1)
                        if j % 8 == 0 and g >= 2:
                            act.wait_ge(s.pv3_ready, g - 1)
                        to = PRg[:, g % 2, c * 1024:(c + 1) * 1024].rearrange("p (k q) -> p k q", k=4)
                        act.copy(to[:, :, qt * P:(qt + 1) * P],
                                 bank(T_BANKS[j % 2]).rearrange("p (k q) -> p k q", k=4)).then_inc(s.pt3_ready, 1)

            def onat_out(n):
                act.wait_ge(s.onat_turned, n + 1)
                act.copy(OT[:, :], bank(0)).then_inc(s.onatT_ready, 1)

            act.wait_ge(s.setup_dve, 1)
            for b in range(B):
                spread_and_stack(act, range(6 * b, 6 * b + 6), range(6 * b, 6 * b + 6))
            warm(ACT.Exp)
            act.wait_ge(s.setup_pool, 4)
            attention(0)
            onat_out(0)
            act.wait_ge(s.ld_cols, 16)
            ln_out(1)
            act.wait_ge(s.gate_diff, 1)
            act.activation(gt[:, :, 1], gt[:, :, 0], ACT.Exp).then_inc(s.gate_exp, 1)
            ln_out(2)
            for e in range(E):
                for c in range(4):
                    n = 4 * e + c
                    act.wait_ge(s.h_ready, n + 1)
                    if e >= 2:
                        act.wait_ge(s.y_ready, e - 1)
                    act.activation(actT[:, e % 2, c, :], bank(c), ACT.Gelu_apprx_tanh,
                                   bias=CB["fc1_b"][:, n:n + 1]).then_inc(s.act_ready, 1)
                if e >= 1:
                    spread_and_stack(act, [K1[e - 1]], [])
                if e >= 2:
                    spread_and_stack(act, [], [K1[e - 2]])
            spread_and_stack(act, [K1[E - 1]], K1[E - 2:E])
            ln_out(3)
            spread_and_stack(act, PHASE_TILES[1][8:12], PHASE_TILES[1][8:12])
            warm(ACT.Exp)
            attention(1)
            onat_out(1)
            ln_out(4)
            act.wait_ge(s.logit_ready, 2)
            act.wait_ge(s.gate_diff, 2)
            act.activation(comb[:, :, :], lg[:, :, :], ACT.Exp, scale=-1.0).then_inc(s.gate_exp, 1)
            act.wait_ge(s.gate_diff, 3)
            act.activation(gt[:, :, 1], gt[:, :, 0], ACT.Exp).then_inc(s.gate_exp, 1)
            for t in range(NT):
                act.wait_ge(s.hh_ready, t + 1)
                act.activation(SL[:, t, :, :], HH[:, t, :, 0:H1], ACT.Silu).then_inc(s.silu_ready, 1)
            def values3(n0, n1):
                for n in range(n0, n1):
                    k, half = n // 2, n % 2
                    act.wait_ge(s.v3_ready, n + 1)
                    act.copy(V3[:, k, half * 512:(half + 1) * 512], bank(v3_bank(n))).then_inc(s.v3_act, 1)

            values3(0, 6)
            for half in range(2):
                act.wait_ge(s.c_ready, half + 1)
                act.activation(SL[:, 2 * half:2 * half + 2, :, :], U[:, 2 * half:2 * half + 2, 0:NU, :],
                               ACT.Square).then_inc(s.sq_ready, 1)
            warm(ACT.Sqrt)
            values3(6, 9)
            act.wait_ge(s.var1_ready, 1)
            act.activation(rstd[:, 0:NT * NU], ve[:, 0:NT * NU], ACT.Sqrt).then_inc(s.std1_ready, 1)
            values3(9, 12)
            for n in range(4):
                act.wait_ge(s.kv2_ready, n + 1)
                to = KT2[:, n * 512:(n + 1) * 512] if n < 2 else \
                    V2[:, 4 * n - 8:4 * n - 4, :].rearrange("p k n -> p (k n)")
                act.copy(to, bank(6 + n % 2)).then_inc(s.kv2_read, 1)
            for r in range(1, 5, 2):
                act.wait_ge(s.z_turned, r + 1)
                act.activation(ZT[:, r, :], bank(r), ACT.Copy, scale=CB["gcol"][:, r:r + 1])\
                    .then_inc(s.zT_act, 1)
            def keys3(n0, n1):
                for n in range(n0, n1):
                    act.wait_ge(s.k3_ready, n + 1)
                    act.activation(K3[:, n // 2, (n % 2) * 512:(n % 2 + 1) * 512], bank(k3_bank(n)),
                                   ACT.Identity, bias=CB["bk3"][:, n // 2:n // 2 + 1]).then_inc(s.k3_act, 1)

            keys3(0, 4)
            ln_out(5)
            act.wait_ge(s.ld_rows, 16)
            act.activation(qs[:, 8:10], RB["clip"], ACT.Exp, scale=-1.0).then_inc(s.clip_exp, 1)
            for t in range(NT):
                act.wait_ge(s.nm2_ready, t + 1)
                act.activation(P2[:, t, :], bank(t), ACT.Exp, bias=qs[:, 16 + t:17 + t],
                               accum_out=qs[:, 20 + t:21 + t]).then_inc(s.p2_ready, 1)
            for t in range(NT):
                act.wait_ge(s.p2_turned, t + 1)
                act.copy(PT2[:, t, :, :].rearrange("p k q -> p (k q)"), bank(4 + t))\
                    .then_inc(s.pt2_ready, 1)
            keys3(4, 8)
            warm(ACT.Silu)
            for n in range(3):
                act.wait_ge(s.wq_turned, n + 1)
                if n < 2:
                    i = act.copy(wgT[:, n, :, :].rearrange("p c n -> p (c n)"), bankb(1 + n)[:, 0:3 * P])
                else:
                    act.copy(wdT[:, 0:2, :].rearrange("p c n -> p (c n)"), bankb(3)[:, 0:2 * P])
                    i = act.copy(wdT[0:I2R, 2, :], bankb(3)[0:I2R, 2 * P:3 * P])
                i.then_inc(s.wq_read, 1)
            keys3(8, 12)
            act.wait_ge(s.xq_turned, 1)
            act.copy(xqT[:, :], bankb(0)[:, 0:T]).then_inc(s.xqT_ready, 1)
            act.wait_ge(s.scales_ready, 1)
            for c in range(3):
                n = P if c < 2 else I2R
                act.wait_ge(s.g2_ready, 2 * c + 1)
                act.activation(SG[0:n, c, :], bank(c)[0:n, :], ACT.Silu, scale=qs[0:n, 28 + c:29 + c])\
                    .then_inc(s.sg_ready, 1)
            keys3(12, 16)
            values3(12, 16)
            ln_out(7)
            act.wait_ge(s.bq3_ready, 1)
            warm(ACT.Exp)
            queries3(0)
            queries3(1)
            attention3()
            ln_out(9)
            act.wait_ge(s.setup_pool, 5)
            spread_and_stack(act, PHASE_TILES[2], PHASE_TILES[2])
            attention(2)
            onat_out(2)
            ln_out(10)
            for e in range(E):
                for c in range(2):
                    act.wait_ge(s.h_ready, 4 * E + 4 * e + c + 1)
                    if 2 * e + c >= 2:
                        act.wait_ge(s.hd_ready, E + 2 * e + c - 1)
                    act.activation(SG[:, c, :], bank(c), ACT.Silu).then_inc(s.act_ready, 1)
                if e == 0:
                    act.wait_ge(s.gate_diff, 4)
                    act.activation(lg[:, :, 0:E], lg[:, :, 0:E], ACT.Exp).then_inc(s.gate_exp, 1)

        @block.vector
        def _(dve):
            chain = [0]

            def link(ins):
                chain[0] += 1
                ins.then_inc(s.dve_done, 1)
                dve.wait_ge(s.dve_done, chain[0])

            told = {}

            def signal(ins, name):
                told[name] = told.get(name, 0) + 1
                ins.then_inc(S[name], 1)
                dve.wait_ge(S[name], told[name])

            def normalise(k, to=xn, keep=None):
                src = xn if k == 2 else x
                for t in range(NT):
                    i = dve.bn_stats(st6[:, t, :], src[:, t, :])
                link(i)
                for t in range(NT):
                    i = dve.bn_aggr(mv[:, t, :], st6[:, t, :])
                i.then_inc(s.var_ready, 1)
                if keep is not None:
                    link(dve.tensor_copy(keep, x[:, :, :].rearrange("p t n -> p (t n)")))
                dve.wait_ge(s.rstd_ready, k + 1)
                if k == 2:
                    dve.wait_ge(s.xn_turned, 1)
                for t in range(NT):
                    i = dve.tensor_scalar(to[:, t, :], src[:, t, :], mv[:, t, 0:1], rstd[:, t:t + 1],
                                          ALU.subtract, ALU.mult)
                i.then_inc(s.xn_ready, 1)

            def rms_normalise(k):
                for t in range(NT):
                    i = dve.tensor_tensor_reduce(out=rest[:, t * P:(t + 1) * P], in0=x[:, t, :],
                                                 in1=x[:, t, :], scale=1.0 / P, scalar=0.0, op0=ALU.mult,
                                                 op1=ALU.add, accum_out=mv[:, t, 1:2])
                i.then_inc(s.var_ready, 1)
                dve.wait_ge(s.rstd_ready, k + 1)
                for t in range(NT):
                    i = dve.tensor_scalar(xn[:, t, :], x[:, t, :], rstd[:, t:t + 1], None, ALU.mult)
                i.then_inc(s.xn_ready, 1)

            splits = [0]

            def split(src, at, n):
                if OLD_TILES[splits[0]]:
                    dve.wait_ge(s.rep_pool, OLD_TILES[splits[0]])
                    dve.wait_ge(s.rep_act, OLD_TILES[splits[0]])
                splits[0] += 1
                r = rest[:, 0:n]
                signal(dve.tensor_copy(parts[:, 0, at:at + n], src), 'parts_ready')
                link(dve.tensor_tensor(r, src, parts[:, 0, at:at + n], ALU.subtract))
                signal(dve.tensor_copy(parts[:, 1, at:at + n], r), 'parts_ready')
                link(dve.tensor_tensor(r, r, parts[:, 1, at:at + n], ALU.subtract))
                signal(dve.tensor_copy(parts[:, 2, at:at + n], r), 'parts_ready')

            def max_bank(a, g, u):
                n = MAXB[a] + g * (MAXB[a + 1] - MAXB[a]) // G + u
                dve.wait_ge(s.smax_ready, n + 1)
                m = mxs[:, g % 2, :, :]
                if a < 2:
                    i = dve.tensor_reduce(m[:, u // 4, u % 4:u % 4 + 1], bank(n % 2), AX_X, ALU.max)
                elif u == 0:
                    i = dve.tensor_reduce(m[:, 0, :], bank(n % 2).rearrange("p (h k) -> p h k", h=4),
                                          AX_X, ALU.max)
                else:
                    i = dve.tensor_reduce(m[:, 1, 2 * u - 2:2 * u],
                                          bank(n % 2).rearrange("p (h k) -> p h k", h=2), AX_X, ALU.max)
                i.then_inc(s.smax_read, 1)

            def marked(ins):
                chain[0] += 1
                ins.then_inc(s.dve_done, 1)
                return chain[0]

            def attention(a):
                n_banks = (MAXB[a + 1] - MAXB[a]) // G
                for step in range(G + 4):
                    for part in range(8):
                        if step < G:
                            for u in range(part * n_banks // 8, (part + 1) * n_banks // 8):
                                max_bank(a, step, u)
                        g = step - 4
                        if 0 <= g < G:
                            o = bank(2)[:, 256:512].rearrange("p (t c w) -> p t c w", t=2, c=4)
                            b, h0 = group_heads(a, g)
                            to = Onat[:, 2 * b:2 * b + 2, HD * h0:HD * h0 + 4 * HD].rearrange(
                                "p t (c w) -> p t c w", c=4)
                            if part == 2:
                                dve.wait_ge(s.ot_turned, groups(a, g) + 1)
                                mark = marked(dve.reciprocal(rden[:, :, :].unsqueeze(3), o[:, :, :, HD:HD + 1]))
                            elif part == 3:
                                dve.wait_ge(s.dve_done, mark)
                                dve.tensor_tensor(to, o[:, :, :, 0:HD],
                                                  rden[:, :, :].unsqueeze(3).to_broadcast([P, 2, 4, HD]),
                                                  ALU.mult).then_inc(s.o_ready, 1)
                    if step < G:
                        m = mxs[:, step % 2, :, :]
                        to = mp[:, step % 2, :, :, :]
                        r = mr[:, :].rearrange("p (t h) -> p t h", t=2)
                        dve.wait_ge(s.smax_read, MAXB[a] + (step + 1) * n_banks)
                        if groups(a, step) >= 2:
                            dve.wait_ge(s.m_turned, groups(a, step) - 1)
                        link(dve.tensor_scalar(to[:, :, 0, :], m, -1.0, None, ALU.mult))
                        link(dve.scalar_tensor_tensor(out=r, in0=m, scalar=-1.0, in1=to[:, :, 0, :],
                                                      op0=ALU.mult, op1=ALU.subtract))
                        link(dve.tensor_copy(to[:, :, 1, :], r))
                        dve.tensor_tensor(to[:, :, 2, :], r, to[:, :, 1, :], ALU.subtract)\
                            .then_inc(s.m_ready, 1)

            def queries3(r):
                dve.wait_ge(s.q3_ready, r + 1)
                dve.tensor_scalar(Q3[0:DH3, 2 * r, :], bank(O_BANKS[r % 2])[0:DH3, :], float(DH3) ** -0.5,
                                  bq3s[0:DH3, r:r + 1], ALU.mult, ALU.add).then_inc(s.q3_dve, 1)

            def attention3():
                for i in range(PV3 + 8 * G + 3):
                    if i < N3:
                        dve.wait_ge(s.s3_ready, i + 1)
                        dve.tensor_reduce(nm3[:, i % 8:i % 8 + 1], bank(S_BANKS[i % 3]), AX_X, ALU.max,
                                          negate=True).then_inc(s.nm3_ready, 1)
                        if i < 6:
                            queries3(i + 2)
                    g, part = divmod(i - PV3 - 8, 8)
                    if 0 <= g < G and part == 0:
                        dve.wait_ge(s.pv3_ready, g + 1)
                        dve.wait_ge(s.sums3_read, g + 1)
                        for r in range(2):
                            ins = dve.tensor_tensor(OT3b[g // 4][:, 2 * (g % 4) + r, :],
                                                    bank(O_BANKS[g % 2])[:, r * SQ:(r + 1) * SQ],
                                                    rest[:, r * SQ:(r + 1) * SQ], ALU.mult)
                        ins.then_inc(s.o3_ready, 1)
                    g2, q = divmod(i - PV3, 8)
                    if 0 <= g2 < G and q == 4:
                        dve.wait_ge(s.wide3_used, g2 + 1)
                        if g2:
                            dve.wait_ge(s.o3_ready, g2)
                        dve.tensor_copy(rest[:, :], bank(2)).then_inc(s.sums3_read, 1)
                    g1, step = divmod(i - 8, 8)
                    if 0 <= g1 < G and step == 2:
                        dve.wait_ge(s.p3_ready, 8 * (g1 + 1))
                        if g1:
                            dve.wait_ge(s.wide3_used, g1)
                        link(dve.reciprocal(rsum3[:, :], sum3[:, 8 * (g1 % 2):8 * (g1 % 2) + 8]))
                        signal(dve.tensor_copy(rwide3[:, :, :], rsum3[:, :].unsqueeze(2).to_broadcast([P, 8, DH3])),
                               'wide3_ready')

            def project(n, last=True):
                dve.wait_ge(s.proj_ready, n + 1)
                i = dve.tensor_tensor(x[:, :, :], x[:, :, :],
                                      bank(1).rearrange("p (t n) -> p t n", t=NT), ALU.add)
                signal(i, 'x_ready') if last else link(i)

            def add_row(row):
                link(dve.tensor_tensor(x[:, :, :], x[:, :, :],
                                       RB[row].unsqueeze(1).to_broadcast([P, NT, P]), ALU.add))

            def one_hots(n_hot):
                link(dve.tensor_copy(i8f[:, :, :], i8[:, :, :]))
                for j in range(n_hot):
                    i = dve.tensor_tensor(oh[:, j, :, :], C["eidx"].unsqueeze(1).to_broadcast([P, NT, E]),
                                          i8f[:, :, j:j + 1].to_broadcast([P, NT, E]), ALU.is_equal)
                link(i)

            def top8(src):
                for t in range(NT):
                    i = dve.max(v8[:, t, :], src[:, t, 0:E])
                link(i)
                for t in range(NT):
                    i = dve.max_index(i8[:, t, :], v8[:, t, :], src[:, t, 0:E])
                link(i)

            def mix(j0, j1):
                for j, w in ((0, j0), (1, j1)):
                    i = dve.tensor_tensor(oh[:, j, :, :], oh[:, j, :, :],
                                          gt[:, :, w:w + 1].to_broadcast([P, NT, E]), ALU.mult)
                link(i)
                link(dve.tensor_tensor(comb[:, :, 0:E], oh[:, 0, :, :], oh[:, 1, :, :], ALU.add))

            dve.memset(warmth[:, :], 0.0)
            dve.memset(REP[:, :].bitcast(F32), 0.0).then_inc(s.setup_dve, 1)
            dve.wait_ge(s.setup_dve, 1)
            dve.wait_ge(s.ld_const, 16)
            dve.tensor_copy(identb[:, :], C["ident"]).then_inc(s.setup_dve, 1)
            dve.tensor_copy(maskb[:, 0, :], C["mask_n"]).then_inc(s.setup_dve, 1)
            dve.tensor_copy(maskb[:, 1, :], C["mask_t"]).then_inc(s.setup_dve, 1)
            xn_f = xn[:, :, :].rearrange("p t n -> p (t n)")
            for b in range(B):
                dve.wait_ge(s.ld_ctx, 16)
                split(CTXN[:, 4 * b:4 * b + 4, :].rearrange("p k n -> p (k n)"), 0, SK)
                spread_and_stack(dve, range(6 * b, 6 * b + 2), range(0))
                if b == 0:
                    dve.wait_ge(s.ld_x, 16)
                    normalise(0)
                    dve.wait_ge(s.xn_ready, 1)
                spread_and_stack(dve, range(6 * b + 2, 6 * b + 4), range(6 * b, 6 * b + 2))
                split(xn_f[:, b * SQ:(b + 1) * SQ], SK, SQ)
                spread_and_stack(dve, range(6 * b + 4, 6 * b + 6), range(6 * b + 2, 6 * b + 6))
            dve.wait_ge(s.ld_rows, 16)
            add_row("bo0")
            attention(0)
            project(0)

            normalise(1)
            dve.wait_ge(s.xn_ready, 2)
            normalise(2)
            dve.wait_ge(s.ld_cols, 16)
            dve.wait_ge(s.logit_ready, 1)
            link(dve.tensor_copy(lg[:, :, 0:E], bank(2)[:, 0:NT * E].rearrange("p (t e) -> p t e", t=NT)))
            top8(lg)
            signal(dve.tensor_tensor(gt[:, :, 0], v8[:, :, 1], v8[:, :, 0], ALU.subtract), 'gate_diff')
            one_hots(2)
            dve.wait_ge(s.gate_exp, 1)
            link(dve.tensor_scalar(gt[:, :, 2], gt[:, :, 1], 1.0, None, ALU.add))
            link(dve.reciprocal(gt[:, :, 2], gt[:, :, 2]))
            link(dve.tensor_tensor(gt[:, :, 1], gt[:, :, 1], gt[:, :, 2], ALU.mult))
            mix(2, 1)
            signal(dve.tensor_tensor(comb[:, :, 0:E], comb[:, :, 0:E],
                                   RB["alpha"].unsqueeze(1).to_broadcast([P, NT, E]), ALU.mult), 'comb_ready')
            dve.wait_ge(s.lnT_ready, 2)
            def indexed_tokens():
                dve.wait_ge(s.ld_idx, 16)
                link(dve.tensor_copy(idf[:, 0:2, :], idx[:, :, :]))
                for j, n in ((0, B), (1, SQ)):
                    i = dve.tensor_scalar(idf[:, 2 + j, :], idf[:, j, :], 0.0, float(n), ALU.is_lt, ALU.mult)
                link(i)
                link(dve.tensor_tensor(idf[:, 0:2, :], idf[:, 0:2, :], idf[:, 2:4, :], ALU.add))
                for b in range(B):
                    i = dve.tensor_scalar(idf[:, 2 + b, :], idf[:, 0, :], float(b), None, ALU.is_equal)
                link(i)
                for t in range(NT):
                    i = dve.scalar_tensor_tensor(out=eqm[:, t, :], in0=idf[:, 1, :],
                                                 scalar=C["tokpos"][:, t % 2:t % 2 + 1],
                                                 in1=idf[:, 2 + t // 2, :], op0=ALU.is_equal, op1=ALU.mult)
                link(i)
                link(dve.tensor_reduce(tmask[:, :], eqm[:, :, :], AX_X, ALU.max))

            def hidden_input(e):
                if e >= 2:
                    dve.wait_ge(s.h_ready, 4 * (e - 1))
                dve.tensor_scalar(hdT[:, e % 2, :], zT[:, :], CB["ln0_w"][:, e:e + 1],
                                  CB["ln0_b"][:, e:e + 1], ALU.mult, ALU.add).then_inc(s.hd_ready, 1)

            def keys_values(t):
                dve.wait_ge(s.kv1_ready, t + 1)
                kv = bank(6)
                dve.tensor_tensor(Vaug[:, t, :, 0:HD], kv[:, P:2 * P].rearrange("p (h c) -> p h c", h=H),
                                  RB["bv1"].rearrange("p (h c) -> p h c", h=H), ALU.add)
                signal(dve.tensor_tensor(Onat[:, t % 4, :], kv[:, 0:P], RB["bk1"], ALU.add), 'kv1_read')
                split(Onat[:, t % 4, :], P * (t % 4), P)
                spread_and_stack(dve, [K1[t]], [])

            hidden_input(0)
            for e in range(E):
                if e == 2:
                    dve.wait_ge(s.comb_turned, 1)
                    dve.tensor_copy(combT[0:E, :], bank(7)[0:E, :]).then_inc(s.combT_ready, 1)
                if e >= 1:
                    keys_values(e - 1)
                if e + 1 < E:
                    hidden_input(e + 1)
                if e >= 1:
                    add_expert(dve, e - 1, e - 1, 4)
                if e >= 2:
                    spread_and_stack(dve, [], [K1[e - 2]])
                if e == 4:
                    indexed_tokens()
            keys_values(E - 1)
            add_expert(dve, E - 1, E - 1, 4)
            spread_and_stack(dve, [], [K1[E - 2]])
            dve.wait_ge(s.y_ready, E + 1)
            dve.wait_ge(s.y_added, E)
            signal(dve.tensor_tensor(x[:, :, :], x[:, :, :], bank(3).rearrange("p (t n) -> p t n", t=NT),
                                   ALU.add), 'x_ready')

            normalise(3)
            spread_and_stack(dve, [], [K1[E - 1]])
            dve.wait_ge(s.q2_ready, 1)
            link(dve.tensor_tensor(Onat[:, :, :], bank(2).rearrange("p (t n) -> p t n", t=NT),
                                   RB["bq1"].unsqueeze(1).to_broadcast([P, NT, P]), ALU.add))
            split(Onat.rearrange("p t n -> p (t n)"), 0, T)
            spread_and_stack(dve, PHASE_TILES[1][8:12], PHASE_TILES[1][8:12])
            add_row("bo1")
            dve.wait_ge(s.ld_w2, 16)
            for m, name in enumerate(("gate2", "up2")):
                i = dve.tensor_reduce(qs[:, 32 + 3 * m:35 + 3 * m],
                                      WD2[name].rearrange("p (c n) -> p c n", c=3), AX_X, ALU.max,
                                      apply_absolute_value=True)
            i = dve.tensor_reduce(qs[:, 38:39], WD2["down2"], AX_X, ALU.max, apply_absolute_value=True)
            link(i)
            link(dve.tensor_scalar(qs[:, 32:39], qs[:, 32:39], 1.0 / QMAX, None, ALU.mult))
            dve.reciprocal(qs[:, 40:47], qs[:, 32:39]).then_inc(s.wscale_ready, 1)
            attention(1)
            project(1)

            normalise(4)
            dve.wait_ge(s.logit_ready, 2)
            signal(dve.tensor_tensor(lg[:, :, :], bank(7)[:, 0:NT * NU].rearrange("p (t e) -> p t e", t=NT),
                                   RB["gb"].unsqueeze(1).to_broadcast([P, NT, NU]), ALU.add), 'gate_diff')

            def hidden(t):
                dve.wait_ge(s.u_ready, t + 1)
                dve.tensor_tensor(HH[:, t, :, :].rearrange("p u n -> p (u n)"),
                                  bank(3 * (t % 2), 3)[:, 0:NU * P], b12, ALU.add)\
                    .then_inc(s.hh_ready, 1)

            dve.wait_ge(s.ld_b12, 16)
            dve.wait_ge(s.gate_exp, 2)
            link(dve.tensor_scalar(comb[:, :, :], comb[:, :, :], 1.0, None, ALU.add))
            link(dve.reciprocal(lg[:, :, :], comb[:, :, :]))
            link(dve.tensor_tensor(comb[:, :, 0:E], lg[:, :, 0:E],
                                   RB["ebias"].unsqueeze(1).to_broadcast([P, NT, E]), ALU.add))
            top8(comb)
            one_hots(1)
            link(dve.tensor_tensor(oh[:, 1, :, :], oh[:, 0, :, :], lg[:, :, 0:E], ALU.mult))
            link(dve.reduce_sum(gt[:, :, 3:4], oh[:, 1, :, :], AX_X))
            signal(dve.tensor_tensor(gt[:, :, 0], gt[:, :, 3], lg[:, :, E], ALU.subtract), 'gate_diff')
            hidden(0)
            dve.wait_ge(s.gate_exp, 3)
            link(dve.tensor_scalar(gt[:, :, 2], gt[:, :, 1], 1.0, None, ALU.add))
            link(dve.reciprocal(gt[:, :, 2], gt[:, :, 2]))
            link(dve.tensor_tensor(gt[:, :, 1], gt[:, :, 1], gt[:, :, 2], ALU.mult))
            link(dve.tensor_scalar(gt[:, :, 2], gt[:, :, 2], -1.0, None, ALU.add))
            dve.tensor_tensor(gt[:, :, 2], gt[:, :, 2], tmask[:, :], ALU.mult)
            link(dve.tensor_tensor(gt[:, :, 1], gt[:, :, 1], tmask[:, :], ALU.mult))
            link(dve.tensor_scalar(comb[:, :, E], gt[:, :, 2], 1.0, None, ALU.add))
            signal(dve.tensor_tensor(comb[:, :, 0:E], oh[:, 0, :, :],
                                   gt[:, :, 1:2].to_broadcast([P, NT, E]), ALU.mult), 'comb_ready')
            dve.memset(U[:, :, NU, :], 0.0)
            for t in range(NT):
                if t >= 1:
                    hidden(t)
                if t >= 1:
                    dve.wait_ge(s.silu_ready, t)
                    dve.tensor_tensor(U[:, t - 1, 0:NU, :], SL[:, t - 1, :, :], HH[:, t - 1, :, H1:P],
                                      ALU.mult)
            dve.wait_ge(s.silu_ready, NT)
            link(dve.tensor_tensor(U[:, NT - 1, 0:NU, :], SL[:, NT - 1, :, :], HH[:, NT - 1, :, H1:P],
                                   ALU.mult))
            m9 = ve[:, 0:NT * NU].rearrange("p (t u) -> p t u", t=NT)
            link(dve.tensor_reduce(m9, U[:, :, 0:NU, :], AX_X, ALU.add))
            link(dve.tensor_scalar(m9, m9, 1.0 / H1, None, ALU.mult))
            for t in range(NT):
                i = dve.tensor_tensor(U[:, t, 0:NU, :], U[:, t, 0:NU, :],
                                      m9[:, t, :].unsqueeze(2).to_broadcast([P, NU, H1]), ALU.subtract)
                if t % 2:
                    i.then_inc(s.c_ready, 1)
            dve.wait_ge(s.comb_turned, 2)
            dve.tensor_copy(combT[:, :], bank(6)[0:NU, :]).then_inc(s.combT_ready, 1)
            dve.wait_ge(s.b9_ready, 1)
            dve.tensor_tensor(b9s[:, :], bank(7)[0:NU, 0:P], CB["b9"][0:NU, :], ALU.add).then_inc(s.b9_read, 1)
            dve.wait_ge(s.c_ready, 2)
            for half in range(2):
                dve.wait_ge(s.sq_ready, half + 1)
                i = dve.tensor_reduce(m9[:, 2 * half:2 * half + 2, :], SL[:, 2 * half:2 * half + 2, :, :],
                                      AX_X, ALU.add)
            link(i)
            dve.tensor_scalar(m9, m9, 1.0 / H1, EPS, ALU.mult, ALU.add).then_inc(s.var1_ready, 1)
            dve.wait_ge(s.std1_ready, 1)
            r9 = rstd[:, 0:NT * NU].rearrange("p (t u) -> p t u", t=NT)
            link(dve.reciprocal(r9, r9))
            link(dve.tensor_tensor(r9, r9, comb[:, :, :], ALU.mult))
            for t in range(NT):
                i = dve.tensor_tensor(U[:, t, 0:NU, :], U[:, t, 0:NU, :],
                                      r9[:, t, :].unsqueeze(2).to_broadcast([P, NU, H1]), ALU.mult)
            i.then_inc(s.z_ready, 1)
            for r in range(0, 5, 2):
                dve.wait_ge(s.z_turned, r + 1)
                dve.tensor_scalar(ZT[:, r, :], bank(r), CB["gcol"][:, r:r + 1], None, ALU.mult)\
                    .then_inc(s.zT_dve, 1)
            dve.wait_ge(s.y_ready, E + 2)
            signal(dve.tensor_tensor(x[:, :, :], x[:, :, :], bank(5).rearrange("p (t n) -> p t n", t=NT),
                                   ALU.add), 'x_ready')

            normalise(5)
            dve.wait_ge(s.q2_ready, 2)
            dve.tensor_copy(rest[:, :], bank(1)).then_inc(s.q2_read, 1)
            for t in range(NT):
                dve.wait_ge(s.s2_ready, t + 1)
                dve.tensor_reduce(qs[:, 16 + t:17 + t], bank(t), AX_X, ALU.max, negate=True)\
                    .then_inc(s.nm2_ready, 1)
            dve.wait_ge(s.p2_ready, NT)
            link(dve.reciprocal(qs[:, 24:28], qs[:, 20:24]))
            dve.wait_ge(s.y_ready, E + 3)
            for t in range(NT):
                i = dve.scalar_tensor_tensor(out=x[:, t, :], in0=bank(0)[:, t * P:(t + 1) * P],
                                             scalar=qs[:, 24 + t:25 + t], in1=x[:, t, :],
                                             op0=ALU.mult, op1=ALU.add)
            signal(i, 'x_ready')

            def quantise(dst, src, inv, tmp):
                link(dve.tensor_scalar(tmp, src, inv, ROUND, ALU.mult, ALU.add))
                link(dve.tensor_scalar(tmp, tmp, -ROUND, QMAX, ALU.add, ALU.min))
                return dve.tensor_scalar(dst, tmp, -QMAX - 1.0, None, ALU.max)

            dve.wait_ge(s.clip_exp, 1)
            link(dve.tensor_scalar(qs[:, 8:10], qs[:, 8:10], 1.0, None, ALU.add))
            link(dve.reciprocal(qs[:, 8:10], qs[:, 8:10]))
            link(dve.tensor_scalar(qs[:, 8:10], qs[:, 8:10], 1.0 / QMAX, None, ALU.mult))
            normalise(6)
            dve.wait_ge(s.xn_ready, 7)
            dve.tensor_reduce(qs[:, 0:1], xn_f, AX_X, ALU.max, apply_absolute_value=True)\
                .then_inc(s.ax_ready, 1)
            dve.wait_ge(s.ax_all, 1)
            link(dve.tensor_tensor(qs[:, 4:5], qs[:, 1:2], qs[:, 8:9], ALU.mult))
            link(dve.reciprocal(qs[:, 5:6], qs[:, 4:5]))
            quantise(xqi[:, :, :].rearrange("p t n -> p (t n)"), xn_f, qs[:, 5:6], rest[:, :])\
                .then_inc(s.xq_ready, 1)
            link(dve.tensor_scalar(qs[:, 28:31], qs[:, 32:35], qs[:, 4:5], None, ALU.mult))
            dve.memset(h2T[:, 2, :], 0.0)
            dve.memset(qs[:, 26:27], 0.0)
            signal(dve.tensor_scalar(qs[:, 12:15], qs[:, 35:38], qs[:, 4:5], None, ALU.mult), 'scales_ready')
            for c in range(3):
                n = P if c < 2 else I2R
                dve.wait_ge(s.g2_ready, 2 * c + 2)
                dve.wait_ge(s.sg_ready, c + 1)
                i = dve.scalar_tensor_tensor(out=h2T[0:n, c, :], in0=bank(3 + c)[0:n, :],
                                             scalar=qs[0:n, 12 + c:13 + c], in1=SG[0:n, c, :],
                                             op0=ALU.mult, op1=ALU.mult)
                link(i)
                i = dve.tensor_reduce(qs[0:n, 24 + c:25 + c], h2T[0:n, c, :], AX_X, ALU.max,
                                      apply_absolute_value=True)
            link(i)
            h2f = h2T.rearrange("p c t -> p (c t)")
            dve.tensor_reduce(qs[:, 2:3], qs[:, 24:27], AX_X, ALU.max).then_inc(s.ax_ready, 1)
            dve.wait_ge(s.ax_all, 2)
            link(dve.tensor_tensor(qs[:, 6:7], qs[:, 3:4], qs[:, 9:10], ALU.mult))
            link(dve.reciprocal(qs[:, 7:8], qs[:, 6:7]))
            quantise(hqT[:, :, :].rearrange("p c t -> p (c t)"), h2f, qs[:, 7:8], h2f)\
                .then_inc(s.hq_ready, 1)
            link(dve.tensor_tensor(qs[:, 10:11], qs[:, 38:39], qs[:, 6:7], ALU.mult))
            dve.wait_ge(s.y2_ready, 1)
            dve.tensor_scalar(rest[:, :], bank(6), qs[:, 10:11], None, ALU.mult).then_inc(s.y2_read, 1)
            dve.wait_ge(s.y2_turned, 1)
            signal(dve.tensor_tensor(x[:, :, :], x[:, :, :], bank(7).rearrange("p (t n) -> p t n", t=NT),
                                   ALU.add), 'x_ready')

            signal(dve.tensor_scalar(bq3s[:, :], CB["bq3"], float(DH3) ** -0.5, None, ALU.mult), 'bq3_ready')
            normalise(7)
            queries3(0)
            queries3(1)
            dve.wait_ge(s.xn_ready, 8)
            add_row("bo3")
            attention3()
            dve.wait_ge(s.proj_ready, 3)
            signal(dve.tensor_tensor(x[:, :, :], x[:, :, :], bank(1).rearrange("p (t n) -> p t n", t=NT),
                                   ALU.add), 'x_ready')

            x_f = x[:, :, :].rearrange("p t n -> p (t n)")
            normalise(8, x, keep=zT)
            dve.wait_ge(s.xn_ready, 9)
            rms_normalise(9)
            link(dve.memset(V4[:, :, :, :], 0.0))
            dve.memset(V4[:, :, :, HD:HD + 1], 1.0)
            cos4 = C["cos"].rearrange("p (t c) -> p t c", t=NT)
            sin4 = C["sin"].rearrange("p (t c) -> p t c", t=NT)
            for pair in range(2):
                dve.wait_ge(s.qkv_ready, pair + 1)
                src = bank(1 + pair)[:, 0:384].rearrange("p (t n) -> p t n", t=2)
                for j in range(2):
                    t = 2 * pair + j
                    v = src[:, j, 0:160].rearrange("p (h c) -> p h c", c=HD)
                    a1 = qrope[:, t, :].rearrange("p (h c) -> p h c", c=HD)
                    a2 = qrot[:, t, :].rearrange("p (h c) -> p h c", c=HD)
                    cb = cos4[:, t, :].unsqueeze(1).to_broadcast([P, 20, HD])
                    sb_ = sin4[:, t, :].unsqueeze(1).to_broadcast([P, 20, HD])
                    dve.tensor_tensor(a1, v, cb, ALU.mult)
                    dve.tensor_tensor(a2[:, :, 0:4], v[:, :, 4:8], sb_[:, :, 0:4], ALU.mult)
                    dve.tensor_tensor(a2[:, :, 4:8], v[:, :, 0:4], sb_[:, :, 4:8], ALU.mult)
                    i = dve.tensor_copy(V4[:, t, :, 0:HD],
                                        src[:, j, 160:192].rearrange("p (h c) -> p h c", c=HD))
                link(i)
                q2 = qrope[:, 2 * pair:2 * pair + 2, :]
                link(dve.tensor_tensor(q2, q2, qrot[:, 2 * pair:2 * pair + 2, :], ALU.add))
                split(q2.rearrange("p t n -> p (t n)"), 320 * pair, 320)
                if pair == 0:
                    dve.wait_ge(s.setup_pool, 5)
                    spread_and_stack(dve, PHASE_TILES[2][0:4], [])
            spread_and_stack(dve, PHASE_TILES[2][4:8], PHASE_TILES[2])
            attention(2)
            project(3, last=False)
            rms_normalise(10)
            dve.wait_ge(s.xn_ready, 11)
            link(dve.tensor_tensor(x_f, x_f, zT, ALU.add))

            def route():
                dve.wait_ge(s.logit_ready, 3)
                link(dve.tensor_copy(lg[:, :, 0:E], bank(6)[:, 0:NT * E].rearrange("p (t e) -> p t e", t=NT)))
                link(dve.tensor_reduce(gt[:, :, 0:1], lg[:, :, 0:E], AX_X, ALU.max))
                signal(dve.tensor_tensor(lg[:, :, 0:E], lg[:, :, 0:E], gt[:, :, 0:1].to_broadcast([P, NT, E]),
                                       ALU.subtract), 'gate_diff')
                dve.wait_ge(s.gate_exp, 4)
                link(dve.reduce_sum(gt[:, :, 1:2], lg[:, :, 0:E], AX_X))
                link(dve.reciprocal(gt[:, :, 1:2], gt[:, :, 1:2]))
                link(dve.tensor_tensor(lg[:, :, 0:E], lg[:, :, 0:E], gt[:, :, 1:2].to_broadcast([P, NT, E]),
                                       ALU.mult))
                top8(lg)
                one_hots(2)
                link(dve.tensor_tensor(gt[:, :, 0], v8[:, :, 0], v8[:, :, 1], ALU.add))
                link(dve.reciprocal(gt[:, :, 0], gt[:, :, 0]))
                link(dve.tensor_tensor(gt[:, :, 1:3], v8[:, :, 0:2], gt[:, :, 0:1].to_broadcast([P, NT, 2]),
                                       ALU.mult))
                mix(1, 2)

            for e in range(E):
                for c in range(2):
                    dve.wait_ge(s.act_ready, 4 * E + 2 * e + c + 1)
                    dve.wait_ge(s.h_ready, 4 * E + 4 * e + 2 + c + 1)
                    if e >= 2:
                        dve.wait_ge(s.y_ready, E + 3 + e - 1)
                    dve.tensor_tensor(actT[:, e % 2, c, :], SG[:, c, :], bank(2 + c), ALU.mult)\
                        .then_inc(s.hd_ready, 1)
                if e == 0:
                    route()
                if e >= 1:
                    add_expert(dve, e - 1, E + e - 1, 4, E + 3)
            add_expert(dve, E - 1, 2 * E - 1, 4, E + 3)

        @block.tensor
        def _(pe):
            ident = C["ident"]

            def turn_xn(k):
                pe.wait_ge(s.xn_ready, k + 1)
                for t in range(NT):
                    i = pe.transpose(bank(0)[:, t * P:(t + 1) * P], xn[:, t, :], ident)
                i.then_inc(s.xn_turned, 1)

            def stack(tile_range):
                for n, (tl, h0, nh) in enumerate(lots):
                    if tl not in tile_range:
                        continue
                    for spread_by in (s.rep_dve, s.rep_act, s.rep_pool):
                        pe.wait_ge(spread_by, tl + 1)
                    if n >= 4:
                        back = 2 if n in K1_LOTS else 4
                        pe.wait_ge(s.stack_act if n % 2 else s.stack_dve, (n - back) // 2 + 1)
                    for h in range(nh):
                        i = pe.transpose(bankb(lot_bank(n))[0:PAD, h * P:(h + 1) * P],
                                         REPv[:, tl % 4, h0 + h, :], identb[:, :])
                    i.then_inc(s.rep_turned, 1)

            def scores_max(a, g, part):
                b, h0 = group_heads(a, g)
                n_banks = (MAXB[a + 1] - MAXB[a]) // G
                for u in range(part * n_banks // 4, (part + 1) * n_banks // 4):
                    n = MAXB[a] + g * n_banks + u
                    if n >= 2:
                        pe.wait_ge(s.smax_read, n - 1)
                    if a < 2:
                        q0, h = b * SQ + (u // 4) * P, h0 + u % 4
                        i = pe.matmul(bank(n % 2), Qst[0:PAD, h, q0:q0 + P], Kst[0:PAD, h, b * SK:(b + 1) * SK],
                                      start=True, stop=True)
                    elif u == 0:
                        for c in range(4):
                            o = bank(n % 2)[:, c * P:(c + 1) * P]
                            pe.matmul(o, Qst[0:PAD, h0 + c, b * SQ:b * SQ + P], K4[0:PAD, h0 // 4, b * SQ:b * SQ + P],
                                      start=True, stop=False)
                            i = pe.matmul(o, identb[:, :], maskb[:, 0, :], start=False, stop=True)
                    else:
                        for c in range(2):
                            h = h0 + 2 * (u - 1) + c
                            o = bank(n % 2)[:, c * SQ:(c + 1) * SQ]
                            pe.matmul(o, Qst[0:PAD, h, b * SQ + P:(b + 1) * SQ], K4[0:PAD, h0 // 4, b * SQ:(b + 1) * SQ],
                                      start=True, stop=False)
                            i = pe.matmul(o[:, P:SQ], identb[:, :], maskb[:, 0, :], start=False, stop=True)
                    i.then_inc(s.smax_ready, 1)

            def scores_exp(a, g, part):
                b, h0 = group_heads(a, g)
                n_units = (UNIT[a + 1] - UNIT[a]) // G
                pe.wait_ge(s.mrow_ready, groups(a, g) + 1)
                for u in range(part * n_units // 4, (part + 1) * n_units // 4):
                    n = UNIT[a] + g * n_units + u
                    if n >= 2:
                        pe.wait_ge(s.p_ready, n - 1)
                    o = bank(3 + 2 * (n % 2), 2)
                    if a < 2:
                        h = h0 + u
                        for k in range(4):
                            k0 = b * SK + k * P
                            ok = o[:, k * SQ:(k + 1) * SQ]
                            i = pe.matmul(ok, Kst[0:MROW, h, k0:k0 + P], Qst[0:MROW, h, b * SQ:(b + 1) * SQ],
                                          start=True, stop=True)
                    elif u == 0:
                        for c in range(0, 4, 2):
                            ok = o[:, c * SQ:(c + 2) * SQ].rearrange("p (c q) -> p c q", c=2)
                            pe.matmul(ok, K4[0:PAD, h0 // 4, b * SQ:b * SQ + P],
                                      Qst[0:PAD, h0 + c:h0 + c + 2, b * SQ:(b + 1) * SQ], start=True, stop=False)
                            for j in range(2):
                                pe.matmul(ok[:, j, :], onesel[0:MROW, c + j, :],
                                          Qst[0:MROW, h0 + c + j, b * SQ:(b + 1) * SQ], start=False, stop=False)
                            i = pe.matmul(ok[:, :, 0:P], identb[:, :],
                                          maskb[:, 1, :].unsqueeze(1).to_broadcast([P, 2, P]),
                                          start=False, stop=True)
                    else:
                        ok = o[:, 0:512].rearrange("p (c q) -> p c q", c=4)
                        pe.matmul(ok, K4[0:PAD, h0 // 4, b * SQ + P:(b + 1) * SQ],
                                  Qst[0:PAD, h0:h0 + 4, b * SQ + P:(b + 1) * SQ], start=True, stop=False)
                        for j in range(4):
                            pe.matmul(ok[:, j, :], onesel[0:MROW, j, :],
                                      Qst[0:MROW, h0 + j, b * SQ + P:(b + 1) * SQ], start=False, stop=False)
                        i = pe.matmul(ok, identb[:, :], maskb[:, 1, :].unsqueeze(1).to_broadcast([P, 4, P]),
                                      start=False, stop=True)
                    i.then_inc(s.st_ready, 1)

            def turn_max(a, g):
                n = groups(a, g)
                pe.wait_ge(s.m_ready, n + 1)
                if n >= 1:
                    pe.wait_ge(s.mrow_ready, n)
                back = g - 3
                if n and (back >= 0 or g == 0):
                    pe.wait_ge(s.o_ready, a * G + back + 1 if g else a * G)
                for t in range(2):
                    i = pe.transpose(bankb(2)[0:12, t * P:(t + 1) * P],
                                     mp[:, g % 2, t, :, :].rearrange("p i h -> p (i h)"), identb[:, :])
                i.then_inc(s.m_turned, 1)

            def probs_values(a, g, chunks):
                n = groups(a, g)
                b, h0 = group_heads(a, g)
                pe.wait_ge(s.p_ready, UNIT[a] + (g + 1) * ((UNIT[a + 1] - UNIT[a]) // G))
                if n == 0:
                    pe.wait_ge(s.setup_pool, 4)
                pr = PRg[:, g % 2, :]
                if n >= 1 and chunks[0] == 0:
                    pe.wait_ge(s.ot_ready, n)
                o = bank(7)[:, (n % 2) * SQ:(n % 2 + 1) * SQ]
                if a == 2:
                    for c in range(4 if chunks[0] == 0 else 0):
                        pe.matmul(o[32 * c:32 * c + VW, :], V4[:, 2 * b, h0 // 4, :], pr[:, c * SQ:(c + 1) * SQ],
                                  start=True, stop=False)
                    for c in range(4 if chunks[-1] == 3 else 0):
                        i = pe.matmul(o[32 * c:32 * c + VW, P:SQ], V4[:, 2 * b + 1, h0 // 4, :],
                                      pr[:, 1024 + c * P:1024 + (c + 1) * P], start=False, stop=True)
                else:
                    for k in chunks:
                        for c in range(4):
                            i = pe.matmul(o[32 * c:32 * c + VW, :], Vaug[:, 4 * b + k, h0 + c, :],
                                          pr[:, c * 1024 + k * SQ:c * 1024 + (k + 1) * SQ],
                                          start=(k == 0), stop=(k == 3))
                if chunks[-1] == 3:
                    i.then_inc(s.pv_ready, 1)

            def turn_out(a, g):
                n = groups(a, g)
                pe.wait_ge(s.ot_ready, n + 1)
                pe.wait_ge(s.mrow_ready, min(groups(a, g) + 3, (a + 1) * G))
                if g:
                    pe.wait_ge(s.o_ready, groups(a, g))
                m = groups(a, g) % 2
                for t in range(2):
                    i = pe.transpose(bank(2)[:, 256 + t * P:256 + (t + 1) * P],
                                     OT[:, m * SQ + t * P:m * SQ + (t + 1) * P], ident)
                i.then_inc(s.ot_turned, 1)

            def attention(a):
                for step in range(G + 4):
                    for part in range(4):
                        if step < G:
                            scores_max(a, step, part)
                        if 0 <= step - 2 < G:
                            scores_exp(a, step - 2, part)
                        if part == 0 and 0 <= step - 4 < G:
                            turn_out(a, step - 4)
                        if part == 2 and 0 <= step - 1 < G:
                            turn_max(a, step - 1)
                        if part and 0 <= step - 3 < G:
                            probs_values(a, step - 3, ([], [0], [1], [2, 3])[part])

            def queries3(r):
                if r >= 2:
                    pe.wait_ge(s.q3_act, r - 1)
                    pe.wait_ge(s.q3_dve, r - 1)
                pe.matmul(bank(O_BANKS[r % 2]), W3[:, 0, r * P:(r + 1) * P], lnT[:, :], start=True, stop=True)\
                    .then_inc(s.q3_ready, 1)

            def attention3():
                for i in range(PV3 + 8 * G):
                    if i < N3:
                        _, _, qt, h, b = unit3(i)
                        if i >= 3:
                            pe.wait_ge(s.p3_ready, i - 2)
                        if i < N3 // 2 and i % 4 == 0:
                            pe.wait_ge(s.q3_act, h // 2 + 1)
                            pe.wait_ge(s.q3_dve, h // 2 + 1)
                        q0 = b * SQ + qt * P
                        pe.matmul(bank(S_BANKS[i % 3]), Q3[:, h, q0:q0 + P], K3[:, h // 2, b * SK:(b + 1) * SK],
                                  start=True, stop=True).then_inc(s.s3_ready, 1)
                        if i < 6:
                            queries3(i + 2)
                    j = i - LAG
                    if 0 <= j < N3:
                        pe.wait_ge(s.p3_ready, j + 1)
                        if j >= 2:
                            pe.wait_ge(s.pt3_ready, j - 1)
                        for k in range(4):
                            ins = pe.transpose(bank(T_BANKS[j % 2])[:, k * P:(k + 1) * P],
                                               P3[:, j % 8, k * P:(k + 1) * P], ident)
                        ins.then_inc(s.t3_ready, 1)
                    g, q = divmod(i - PV3, 8)
                    if not 0 <= g < G:
                        continue
                    b, h0 = group_heads(2, g)
                    if q == 0:
                        pe.wait_ge(s.pt3_ready, 8 * (g + 1))
                        pe.wait_ge(s.v3_biased, 4 * (b + 1))
                        if g >= 2:
                            pe.wait_ge(s.o3_ready, g - 1)
                    pr = PRg[:, g % 2, :]
                    r, k = q // 4, q % 4
                    for c in range(2):
                        pv = pe.matmul(bank(O_BANKS[g % 2])[DH3 * c:DH3 * (c + 1), r * SQ:(r + 1) * SQ],
                                       V3[:, 4 * b + k, DH3 * (h0 + 2 * r + c):DH3 * (h0 + 2 * r + c + 1)],
                                       pr[:, (2 * r + c) * 1024 + k * SQ:(2 * r + c) * 1024 + (k + 1) * SQ],
                                       start=(k == 0), stop=(k == 3))
                    if q == 2:
                        pe.wait_ge(s.wide3_ready, g + 1)
                        if g:
                            pe.wait_ge(s.sums3_read, g)
                        for c in range(4):
                            for qt in range(2):
                                to = SQ * (c // 2) + P * qt
                                ins = pe.matmul(bank(2)[DH3 * (c % 2):DH3 * (c % 2 + 1), to:to + P],
                                                rwide3[:, 2 * c + qt, :], ident, start=True, stop=True)
                        ins.then_inc(s.wide3_used, 1)
                    if q == 7:
                        pv.then_inc(s.pv3_ready, 1)

            def project(n, a, w):
                pe.wait_ge(s.o_ready, (a + 1) * G)
                for t in range(NT):
                    i = pe.transpose(bank(0)[:, t * P:(t + 1) * P], Onat[:, t, :], ident)
                i.then_inc(s.onat_turned, 1)
                pe.wait_ge(s.onatT_ready, min(n, 2) + 1)
                for t in range(NT):
                    i = pe.matmul(bank(1)[:, t * P:(t + 1) * P], OT[:, t * P:(t + 1) * P], w, start=True, stop=True)
                i.then_inc(s.proj_ready, 1)

            def project3():
                for t in range(NT):
                    pe.wait_ge(s.o3_ready, G // 2 if t < 2 else G)
                    for r in range(8):
                        i = pe.matmul(bank(1)[:, t * P:(t + 1) * P],
                                      OT3b[t // 2][:, r, (t % 2) * P:(t % 2 + 1) * P],
                                      WD["wo3"][:, r * P:(r + 1) * P], start=(r == 0), stop=(r == 7))
                i.then_inc(s.proj_ready, 1)

            def values3(n0, n1):
                for n in range(n0, n1):
                    if n >= 3:
                        pe.wait_ge(s.v3_act, n - 2 if n < 14 else n - 1)
                    pe.matmul(bank(v3_bank(n)), ctxT[:, (n // 2) * P:(n // 2 + 1) * P],
                              W3[:, 2, (n % 2) * 512:(n % 2 + 1) * 512], start=True, stop=True)\
                        .then_inc(s.v3_ready, 1)

            pe.wait_ge(s.setup_dve, 4)
            stack(PHASE_TILES[0])
            stacked(pe, PHASE_TILES[0][-1])
            pe.wait_ge(s.ld_sel, 32)
            attention(0)
            pe.wait_ge(s.ld_wa, 16)
            project(0, 0, WA["wo0"])

            turn_xn(1)
            pe.wait_ge(s.lnT_ready, 1)
            for t in range(NT):
                i = pe.matmul(bank(2)[:, t * E:(t + 1) * E], lnT[:, t * P:(t + 1) * P], WA["wg0"],
                              start=True, stop=True)
            i.then_inc(s.logit_ready, 1)
            turn_xn(2)
            pe.wait_ge(s.ld_cols, 16)
            pe.wait_ge(s.ld_fc1, 16)
            pe.wait_ge(s.ld_fc2, 16)
            pe.wait_ge(s.lnT_ready, 2)

            def expert_up(e):
                pe.wait_ge(s.hd_ready, e + 1)
                for c in range(4):
                    if e:
                        pe.wait_ge(s.act_ready, 4 * (e - 1) + c + 1)
                    pe.matmul(bank(c), fc1[:, e, c * P:(c + 1) * P], hdT[:, e % 2, :], start=True, stop=True)\
                        .then_inc(s.h_ready, 1)

            def expert_down(e):
                pe.wait_ge(s.act_ready, 4 * e + 4)
                if e >= 2:
                    pe.wait_ge(s.y_added, e - 1)
                for t in range(NT):
                    for c in range(4):
                        i = pe.matmul(bank(4 + e % 2)[:, t * P:(t + 1) * P], actT[:, e % 2, c, t * P:(t + 1) * P],
                                      fc2[:, e, c, :], start=(c == 0), stop=(c == 3))
                i.then_inc(s.y_ready, 1)

            pe.wait_ge(s.ld_wb, 16)
            pe.wait_ge(s.ld_ctxT, 16)

            def keys_values(t):
                if t >= 2:
                    pe.wait_ge(s.stack_dve, lots_till[K1[t - 2]] // 2)
                if t:
                    pe.wait_ge(s.kv1_read, t)
                pe.matmul(bank(6)[:, 0:P], ctxT[:, t * P:(t + 1) * P], WB["wk1"], start=True, stop=True)
                pe.matmul(bank(6)[:, P:2 * P], ctxT[:, t * P:(t + 1) * P], WB["wv1"],
                          start=True, stop=True).then_inc(s.kv1_ready, 1)

            expert_up(0)
            for e in range(E):
                if e == 1:
                    pe.wait_ge(s.comb_ready, 1)
                    for t in range(NT):
                        i = pe.transpose(bank(7)[0:E, t * P:(t + 1) * P], comb[:, t, 0:E], ident)
                    i.then_inc(s.comb_turned, 1)
                if e + 1 < E:
                    expert_up(e + 1)
                keys_values(e)
                expert_down(e)
                if e:
                    pe.wait_ge(s.combT_ready, 1)
                    pe.wait_ge(s.kv1_read, e + 1)
                    stack(K1[e - 1:e])
            for t in range(NT):
                i = pe.matmul(bank(3)[:, t * P:(t + 1) * P], combT[0:E, t * P:(t + 1) * P],
                              CB["fc2_b"][0:E, :], start=True, stop=True)
            i.then_inc(s.y_ready, 1)
            stack(K1[E - 1:E])

            turn_xn(3)
            pe.wait_ge(s.lnT_ready, 3)
            for t in range(NT):
                i = pe.matmul(bank(2)[:, t * P:(t + 1) * P], lnT[:, t * P:(t + 1) * P], WB["wq1"],
                              start=True, stop=True)
            i.then_inc(s.q2_ready, 1)
            stack(PHASE_TILES[1][8:12])
            stacked(pe, PHASE_TILES[1][-1])
            attention(1)
            project(1, 1, WB["wo1"])

            turn_xn(4)
            pe.wait_ge(s.lnT_ready, 4)
            pe.wait_ge(s.ld_wd, 16)
            pe.wait_ge(s.ld_w12, 16)
            pe.wait_ge(s.ld_w3s, 16)
            for t in range(NT):
                i = pe.matmul(bank(7)[:, t * NU:(t + 1) * NU], lnT[:, t * P:(t + 1) * P], WD["wg1"],
                              start=True, stop=True)
            i.then_inc(s.logit_ready, 1)
            for t in range(NT):
                if t >= 2:
                    pe.wait_ge(s.hh_ready, t - 1)
                for c in range(3):
                    w = min(512, NU * P - 512 * c)
                    i = pe.matmul(bank(3 * (t % 2) + c)[:, 0:w], lnT[:, t * P:(t + 1) * P],
                                  w12[:, 512 * c:512 * c + w], start=True, stop=True)
                i.then_inc(s.u_ready, 1)
            pe.wait_ge(s.comb_ready, 2)
            for t in range(NT):
                i = pe.transpose(bank(6)[0:NU, t * P:(t + 1) * P], comb[:, t, :], ident)
            i.then_inc(s.comb_turned, 1)
            for r in range(5):
                i = pe.matmul(bank(7)[0:NU, 0:P], CB["bsel"][:, r * NU:(r + 1) * NU], w3s[:, r, :],
                              start=(r == 0), stop=(r == 4))
            i.then_inc(s.b9_ready, 1)
            pe.wait_ge(s.ld_w3, 16)
            pe.wait_ge(s.hh_ready, 3)
            values3(0, 12)
            pe.wait_ge(s.combT_ready, 2)
            pe.wait_ge(s.b9_read, 1)
            for n in range(2):
                pe.matmul(bank(6 + n), WD["wk2"], ctxT[:, n * 512:(n + 1) * 512], start=True, stop=True)\
                    .then_inc(s.kv2_ready, 1)
            for n in range(2):
                pe.wait_ge(s.kv2_read, n + 1)
                for k in range(4):
                    i = pe.matmul(bank(6 + n)[:, k * P:(k + 1) * P], ctxT[:, (4 * n + k) * P:(4 * n + k + 1) * P],
                                  WD["wv2"], start=True, stop=True)
                i.then_inc(s.kv2_ready, 1)
            pe.wait_ge(s.v3_act, 12)
            pe.wait_ge(s.hh_ready, 4)
            pe.wait_ge(s.z_ready, 1)
            for r in range(5):
                for t in range(NT):
                    i = pe.transpose(bank(r)[:, t * P:(t + 1) * P],
                                     U[:, t, 2 * r:2 * r + 2, :].rearrange("p u n -> p (u n)"), ident)
                i.then_inc(s.z_turned, 1)
            pe.wait_ge(s.zT_dve, 3)
            pe.wait_ge(s.zT_act, 2)
            pe.wait_ge(s.combT_ready, 2)
            pe.wait_ge(s.b9_read, 1)
            for t in range(NT):
                o = bank(5)[:, t * P:(t + 1) * P]
                for r in range(5):
                    pe.matmul(o, ZT[:, r, t * P:(t + 1) * P], w3s[:, r, :], start=(r == 0), stop=False)
                i = pe.matmul(o, combT[:, t * P:(t + 1) * P], b9s[:, :], start=False, stop=True)
            i.then_inc(s.y_ready, 1)

            def keys3(n0, n1):
                for n in range(n0, n1):
                    if n >= 4:
                        pe.wait_ge(s.k3_act, n - 3 if n < 14 else n - 1)
                    r, half = n // 2, n % 2
                    pe.matmul(bank(k3_bank(n)), W3[:, 1, r * P:(r + 1) * P], ctxT[:, half * 512:(half + 1) * 512],
                              start=True, stop=True).then_inc(s.k3_ready, 1)

            keys3(0, 1)
            pe.wait_ge(s.x_ready, 4)
            keys3(1, 4)
            turn_xn(5)
            pe.wait_ge(s.lnT_ready, 5)
            pe.matmul(bank(1), WD["wq2"], lnT[:, :], start=True, stop=True).then_inc(s.q2_ready, 1)
            pe.wait_ge(s.q2_read, 1)
            pe.wait_ge(s.kv2_read, 4)
            for t in range(NT):
                pe.matmul(bank(t), rest[:, t * P:(t + 1) * P], KT2[:, (t // 2) * SK:(t // 2 + 1) * SK],
                          start=True, stop=True).then_inc(s.s2_ready, 1)
            def turn_probs(t):
                pe.wait_ge(s.p2_ready, t + 1)
                for k in range(4):
                    i = pe.transpose(bank(4 + t)[:, k * P:(k + 1) * P], P2[:, t, k * P:(k + 1) * P], ident)
                i.then_inc(s.p2_turned, 1)

            def times_values(t):
                pe.wait_ge(s.pt2_ready, t + 1)
                for k in range(4):
                    i = pe.matmul(bank(0)[:, t * P:(t + 1) * P], PT2[:, t, k, :], V2[:, 4 * (t // 2) + k, :],
                                  start=(k == 0), stop=(k == 3))
                return i

            pe.wait_ge(s.k3_act, 4)
            turn_probs(0)
            for t in range(NT):
                if t + 1 < NT:
                    turn_probs(t + 1)
                i = times_values(t)
            i.then_inc(s.y_ready, 1)

            keys3(4, 8)
            pe.wait_ge(s.wq_ready, 1)
            for m in range(2):
                for c in range(3):
                    i = pe.transpose(bankb(1 + m)[:, c * P:(c + 1) * P], wq2i[:, m, c, :], identb[:, :])
                i.then_inc(s.wq_turned, 1)
            for c in range(3):
                n = P if c < 2 else I2R
                i = pe.transpose(bankb(3)[0:n, c * P:(c + 1) * P], wd2i[:, c * P:c * P + n], identb[:, :])
            i.then_inc(s.wq_turned, 1)
            keys3(8, 12)
            pe.wait_ge(s.xq_ready, 1)
            for t in range(NT):
                i = pe.transpose(bankb(0)[:, t * P:(t + 1) * P], xqi[:, t, :], identb[:, :])
            i.then_inc(s.xq_turned, 1)
            pe.wait_ge(s.xqT_ready, 1)
            pe.wait_ge(s.wq_read, 3)
            pe.wait_ge(s.k3_act, 12)
            for c in range(3):
                n = P if c < 2 else I2R
                for m in range(2):
                    pe.matmul(bank(3 * m + c)[0:n, :], wgT[:, m, c, 0:n], xqT[:, :], start=True, stop=True)\
                        .then_inc(s.g2_ready, 1)
            keys3(12, 16)
            pe.wait_ge(s.k3_act, 16)
            pe.wait_ge(s.hq_ready, 1)
            for c in range(3):
                n = P if c < 2 else I2R
                i = pe.matmul(bank(6), wdT[0:n, c, :], hqT[0:n, c, :], start=(c == 0), stop=(c == 2))
            i.then_inc(s.y2_ready, 1)
            pe.wait_ge(s.y2_read, 1)
            for t in range(NT):
                i = pe.transpose(bank(7)[:, t * P:(t + 1) * P], rest[:, t * P:(t + 1) * P], ident)
            i.then_inc(s.y2_turned, 1)
            values3(12, 13)
            pe.wait_ge(s.x_ready, 6)
            values3(13, 16)

            turn_xn(7)
            pe.wait_ge(s.lnT_ready, 6)
            pe.wait_ge(s.q3_zero, H)
            pe.wait_ge(s.v3_act, 16)
            queries3(0)
            queries3(1)
            attention3()
            project3()

            turn_xn(9)
            pe.wait_ge(s.lnT_ready, 7)
            for pair in range(2):
                for j in range(2):
                    t = 2 * pair + j
                    i = pe.matmul(bank(1 + pair)[:, 192 * j:192 * (j + 1)], lnT[:, t * P:(t + 1) * P],
                                  WD["wqkv"], start=True, stop=True)
                i.then_inc(s.qkv_ready, 1)
            stack(PHASE_TILES[2])
            stacked(pe, PHASE_TILES[2][-1])
            attention(2)
            project(3, 2, WD["wo3f"])
            turn_xn(10)
            pe.wait_ge(s.lnT_ready, 8)
            pe.wait_ge(s.ld_w13, 16)
            pe.wait_ge(s.ld_w2e, 16)

            def up3(e):
                for c in range(4):
                    if e:
                        if c < 2:
                            pe.wait_ge(s.act_ready, 4 * E + 2 * (e - 1) + c + 1)
                        else:
                            pe.wait_ge(s.hd_ready, E + 2 * (e - 1) + c - 1)
                    pe.matmul(bank(c), w13[:, e, c * P:(c + 1) * P], lnT[:, :], start=True, stop=True)\
                        .then_inc(s.h_ready, 1)

            def down3(e):
                pe.wait_ge(s.hd_ready, E + 2 * e + 2)
                if e >= 2:
                    pe.wait_ge(s.y_added, E + e - 1)
                for t in range(NT):
                    for c in range(2):
                        i = pe.matmul(bank(4 + e % 2)[:, t * P:(t + 1) * P], actT[:, e % 2, c, t * P:(t + 1) * P],
                                      w2e[:, e, c, :], start=(c == 0), stop=(c == 1))
                i.then_inc(s.y_ready, 1)

            up3(0)
            for t in range(NT):
                i = pe.matmul(bank(6)[:, t * E:(t + 1) * E], lnT[:, t * P:(t + 1) * P], WD["gate3"],
                              start=True, stop=True)
            i.then_inc(s.logit_ready, 1)
            for e in range(E):
                if e + 1 < E:
                    up3(e + 1)
                down3(e)


def kernel(**inputs):
    import concourse.bacc as bacc
    from concourse.bass_utils import run_bass_kernel_spmd
    from ml_dtypes import bfloat16

    a = {k: np.asarray(v) for k, v in inputs.items()}
    f32 = np.float32

    def pack(widths, parts):
        return np.ascontiguousarray(np.concatenate([np.reshape(parts[k], (P, w)) for k, w in widths.items()], 1))

    def chunks(w):
        return np.moveaxis(w.reshape(*w.shape[:-1], -1, P), -1, 0)

    def row(v):
        return np.broadcast_to(v.reshape(1, -1), (P, v.size))

    def on_top(v):
        return np.concatenate([v, np.zeros((P - v.shape[0], v.shape[1]), v.dtype)], 0)

    i = np.arange(P)
    pos = (np.arange(NT) % 2)[None, :] * P + i[:, None]
    inv_freq = (f32(1.0) / f32(10000.0) ** (np.arange(0, HD, 2, dtype=f32) / f32(HD))).astype(f32)
    angle = pos[:, :, None].astype(f32) * np.concatenate([inv_freq, inv_freq])[None, None, :]
    sign = np.repeat(np.array([-1.0, 1.0], f32), HD // 2)
    const = pack(CONST, dict(
        ident=np.eye(P, dtype=f32), mask_n=np.where(i[None, :] > i[:, None], f32(NEG), f32(0)),
        mask_t=np.where(i[:, None] > i[None, :], f32(NEG), f32(0)), cos=np.cos(angle), sin=np.sin(angle) * sign,
        tokpos=np.stack([i, i + P], 1).astype(f32), eidx=row(np.arange(E, dtype=f32))))
    sel = np.zeros((4 * NPART, H, NK), bfloat16)
    onesel = np.zeros((P, 4, P), bfloat16)
    for c in range(4):
        sel[c::4, c::4] = 1
        onesel[PAD + c:MROW:4, c] = 1

    g, lb = a["L1_ffn_sel_ln_g"], a["L1_ffn_sel_ln_b"]
    gcol = np.stack([np.concatenate([g, g])] * 4 + [np.concatenate([a["L1_ffn_s_ln_g"], np.ones(H1, f32)])], 1)
    bsel = np.zeros((P, 5, NU), f32)
    for u in range(NU):
        bsel[H1 * (u % 2):H1 * (u % 2 + 1), u // 2, u] = lb if u < E else a["L1_ffn_s_ln_b"]
    cols = pack(COLS, dict(
        ln0_w=a["L0_ffn_ln_w"].T, ln0_b=a["L0_ffn_ln_b"].T, fc1_b=chunks(a["L0_ffn_fc1_b"]), gcol=gcol,
        bq3=a["L3_xattn_bq"].reshape(8, P).T, bk3=a["L3_xattn_bk"].reshape(8, P).T,
        rms1=a["L3_ffn_ln1_w"], rms2=a["L3_ffn_ln2_w"], maskk=a["fside_BxS2_0"].reshape(KT, P).T, bsel=bsel,
        fc2_b=on_top(a["L0_ffn_fc2_b"]), b9=on_top(np.concatenate([a["L1_ffn_eb3"], a["L1_ffn_sb3"][None]], 0))))
    rows = pack(ROWS, dict(
        bo0=row(a["L0_xattn_b_out"]), alpha=row(a["L0_ffn_alpha"]), bq1=row(a["L1_xattn_bq"]),
        bk1=row(a["L1_xattn_bk"]), bv1=row(a["L1_xattn_bv"]), bo1=row(a["L1_xattn_bo"]),
        gb=row(np.concatenate([a["L1_ffn_eg_b"], a["L1_ffn_sg_b"]])), ebias=row(a["L1_ffn_exp_bias"]),
        bo3=row(a["L3_xattn_bo"]), clip=row(np.concatenate([a["L2_ffn_clip_x"], a["L2_ffn_clip_down"]])),
        bv3=row(a["L3_xattn_bv"])))
    b1 = np.concatenate([a["L1_ffn_eb1"], a["L1_ffn_sb1"][None]], 0)
    b2 = np.concatenate([a["L1_ffn_eb2"], a["L1_ffn_sb2"][None]], 0)
    w1 = np.concatenate([a["L1_ffn_ew1"], a["L1_ffn_sw1"][None]], 0)
    w2 = np.concatenate([a["L1_ffn_ew2"], a["L1_ffn_sw2"][None]], 0)
    w3 = np.concatenate([a["L1_ffn_ew3"], a["L1_ffn_sw3"][None], np.zeros((1, P, H1), f32)], 0)

    def rows_of_three(w):
        return np.concatenate([w, np.ones((3 * P - I2, P), f32)], 0).reshape(3, P, P).transpose(1, 0, 2)

    arrays = {
        "const": const, "cols": cols, "rows": rows, "sel": sel, "onesel": onesel,
        "x": a["x"].reshape(NT, P, P).transpose(1, 0, 2),
        "ctx": a["ctx_1024"].reshape(KT, P, P).transpose(1, 0, 2),
        "ctxT": a["ctx_1024"].reshape(NK, P).T,
        "w_a": pack(W_A, dict(wo0=a["L0_xattn_w_out"].T, wg0=a["L0_ffn_Wg"])),
        "w_b": pack(W_B, dict(wq1=a["L1_xattn_Wq"], wk1=a["L1_xattn_Wk"], wv1=a["L1_xattn_Wv"],
                              wo1=a["L1_xattn_Wo"])),
        "fc1": a["L0_ffn_fc1_w"].transpose(1, 0, 2),
        "fc2": a["L0_ffn_fc2_w"].reshape(E, 4, P, P).transpose(2, 0, 1, 3),
        "w12": np.concatenate([w1, w2], 1).transpose(2, 0, 1).reshape(P, NU * P),
        "b12": row(np.concatenate([b1, b2], 1)),
        "w3s": w3.transpose(0, 2, 1).reshape(5, P, P).transpose(1, 0, 2),
        "w_d": pack(W_D, dict(
            wg1=np.concatenate([a["L1_ffn_eg_w"], a["L1_ffn_sg_w"]], 0).T, wq2=a["L2_xattn_Wq"].T,
            wk2=a["L2_xattn_Wk"].T, wv2=a["L2_xattn_Wv"].T, wqkv=a["L3_ffn_wqkv"].T, wo3f=a["L3_ffn_wo"].T,
            gate3=a["L3_ffn_gate_w"].T, wo3=a["L3_xattn_Wo"].reshape(8, P, P).transpose(1, 0, 2))),
        "w_2": np.concatenate([rows_of_three(a["L2_ffn_w_gate"]).reshape(P, -1),
                               rows_of_three(a["L2_ffn_w_up"]).reshape(P, -1), a["L2_ffn_w_down"]], 1),
        "w3": np.stack([a["L3_xattn_Wq"].reshape(P, -1), a["L3_xattn_Wk"].reshape(P, -1),
                        a["L3_xattn_Wv"].reshape(P, -1)], 1),
        "w13": a["L3_ffn_w13"].transpose(2, 0, 1),
        "w2e": a["L3_ffn_w2"].reshape(E, P, 2, P).transpose(3, 0, 2, 1),
        "idx": np.broadcast_to(np.stack([a["L1_ffn_index_b"], a["L1_ffn_index_t"]])[None], (P, 2, 256)),
    }
    arrays = {k: np.ascontiguousarray(v) for k, v in arrays.items()}
    nc = bacc.Bacc("TRN2", target_bir_lowering=False, num_devices=1)
    dram = {k: nc.dram_tensor(f"in_{k}", v.shape, mybir.dt.from_np(v.dtype), kind="ExternalInput").ap()
            for k, v in arrays.items()}
    out = nc.dram_tensor("out", (P, NT, P), F32, kind="ExternalOutput").ap()
    mega_kernel(nc, dram, out)
    r = run_bass_kernel_spmd(nc, [{f"in_{k}": v for k, v in arrays.items()}], core_ids=[0])
    got = r.results[0]["out"]
    return np.ascontiguousarray(got.transpose(1, 0, 2)).reshape(B, SQ, P)
```
